# Optimizing a Trainium2 kernel written in Bass

```python
import numpy as np
import jax
import jax.numpy as jnp

def _softmax(x, axis=-1):
    return jax.nn.softmax(x, axis=axis)

def _gelu(x):
    return jax.nn.gelu(x, approximate=True)

def _silu(x):
    return jax.nn.silu(x)

def _sigmoid(x):
    return jax.nn.sigmoid(x)

def _layernorm(x, axis=-1, eps=1e-05):
    m = jnp.mean(x, axis=axis, keepdims=True)
    v = jnp.var(x, axis=axis, keepdims=True)
    return (x - m) / jnp.sqrt(v + eps)

def _scatter_add(tgt, idx, src, axis=0):
    return tgt.at[idx].add(src)

def _segment_sum(src, seg, n):
    return jax.ops.segment_sum(src, seg, n)
kernel_name = 'mk_seq_postln_d1_jaxref_r2_72dee5'

def setup_inputs(seed: int=0):
    np.random.seed(seed)
    _w = jnp.asarray

    def _L0_attn_setup():
        import jax, jax.numpy as jnp
        import numpy as np
        D_MODEL = 512
        NUM_HEADS = 16
        B, S = (1, 2048)
        key = jax.random.key(seed)
        kx, kq, kk, kv, ko = jax.random.split(key, 5)
        std = (1.0 / D_MODEL) ** 0.5

        def trunc(k):
            return std * jax.random.truncated_normal(k, -3.0, 3.0, (D_MODEL, D_MODEL), dtype=jnp.float32)
        return {'x': jax.random.normal(kx, (B, S, D_MODEL), dtype=jnp.float32), 'W_Q': trunc(kq), 'W_K': trunc(kk), 'W_V': trunc(kv), 'W_O': trunc(ko)}
    _L0_attn_in = _L0_attn_setup()

    def _L0_ffn_setup():
        import jax, jax.numpy as jnp
        import numpy as np
        B, S, D, E = (2, 1024, 512, 8)
        key = jax.random.key(seed)
        ks = jax.random.split(key, 5)
        x = jax.random.normal(ks[0], (B, S, D), dtype=jnp.float32)
        router_w = jax.random.normal(ks[1], (E, D), dtype=jnp.float32) * 0.02
        router_b = jnp.zeros((E,), dtype=jnp.float32)
        expert_w = jax.random.normal(ks[2], (E, D, D), dtype=jnp.float32) * 0.02
        expert_b = jnp.zeros((E, D), dtype=jnp.float32)
        return {'x': x, 'router_w': router_w, 'router_b': router_b, 'expert_w': expert_w, 'expert_b': expert_b}
    _L0_ffn_in = _L0_ffn_setup()
    _d = {'L0_attn_x': _L0_attn_in['x'], 'L0_attn_W_Q': _L0_attn_in['W_Q'], 'L0_attn_W_K': _L0_attn_in['W_K'], 'L0_attn_W_V': _L0_attn_in['W_V'], 'L0_attn_W_O': _L0_attn_in['W_O'], 'L0_ffn_router_w': _L0_ffn_in['router_w'], 'L0_ffn_router_b': _L0_ffn_in['router_b'], 'L0_ffn_expert_w': _L0_ffn_in['expert_w'], 'L0_ffn_expert_b': _L0_ffn_in['expert_b']}
    _x0 = _d['L0_attn_x']
    _d['L0_attn_x'] = jax.random.normal(jax.random.fold_in(jax.random.key(seed), 1), (8, 1024, 512), dtype=_x0.dtype)
    del _x0
    return _d

def reference(L0_attn_x, L0_attn_W_Q, L0_attn_W_K, L0_attn_W_V, L0_attn_W_O, L0_ffn_router_w, L0_ffn_router_b, L0_ffn_expert_w, L0_ffn_expert_b):

    def _L0_attn_ref(x, W_Q, W_K, W_V, W_O):
        import jax, jax.numpy as jnp
        import numpy as np
        D_MODEL = 512
        NUM_HEADS = 16
        B, S = (1, 2048)
        Bx, Sx, Dm = x.shape
        H = NUM_HEADS
        d_attn = Dm // H
        Q = x @ W_Q.T
        K = x @ W_K.T
        V = x @ W_V.T
        Q = Q.reshape(Bx, Sx, H, d_attn).transpose(0, 2, 1, 3)
        K = K.reshape(Bx, Sx, H, d_attn).transpose(0, 2, 1, 3)
        V = V.reshape(Bx, Sx, H, d_attn).transpose(0, 2, 1, 3)
        scale = 1.0 / jnp.sqrt(jnp.asarray(d_attn, dtype=x.dtype))
        attn = jnp.einsum('bhqd,bhkd->bhqk', Q, K) * scale
        causal = jnp.tril(jnp.ones((Sx, Sx), dtype=bool))
        attn = jnp.where(causal, attn, jnp.asarray(-jnp.inf, dtype=attn.dtype))
        probs = jax.nn.softmax(attn, axis=-1)
        y = jnp.einsum('bhqk,bhkd->bhqd', probs, V)
        y = y.transpose(0, 2, 1, 3).reshape(Bx, Sx, Dm)
        return y @ W_O.T

    def _L0_ffn_ref(x, router_w, router_b, expert_w, expert_b):
        import jax, jax.numpy as jnp
        import numpy as np
        B, S, D, E = (2, 1024, 512, 8)
        logits = jnp.einsum('bsd,ed->bse', x, router_w) + router_b
        probs = jax.nn.softmax(logits, axis=-1)
        weights = jnp.max(probs, axis=-1)
        top1 = jnp.argmax(probs, axis=-1)
        y_all = jnp.einsum('bsd,eod->bseo', x, expert_w) + expert_b
        y = jnp.take_along_axis(y_all, top1[:, :, None, None], axis=2)[:, :, 0, :]
        out = y * weights[:, :, None]
        return out
    x = L0_attn_x
    x = _layernorm(x + _L0_attn_ref(x, L0_attn_W_Q, L0_attn_W_K, L0_attn_W_V, L0_attn_W_O), axis=-1)
    x = _layernorm(x + _L0_ffn_ref(x, L0_ffn_router_w, L0_ffn_router_b, L0_ffn_expert_w, L0_ffn_expert_b), axis=-1)
    return x

_drawn_inputs = setup_inputs


def setup_inputs(seed=0):
    import zlib

    import numpy as np

    out = dict(_drawn_inputs(seed))
    spreads = {'L0_ffn_router_b': (0.0, 0.1), 'L0_ffn_expert_b': (0.0, 0.347)}
    factors = {}
    for name, (base, spread) in spreads.items():
        noise = np.random.default_rng([zlib.crc32(name.encode()), seed]).standard_normal(out[name].shape)
        drawn = base * np.exp(spread * noise) if base else spread * noise
        out[name] = jnp.asarray(drawn.astype(out[name].dtype))
    for name, factor in factors.items():
        out[name] = (out[name] * factor).astype(out[name].dtype)
    return out
```

```python
from contextlib import ExitStack

import concourse.bass as bass
from concourse import mybir

F32 = mybir.dt.float32
F32R = mybir.dt.float32r
BF16 = mybir.dt.bfloat16
I32 = mybir.dt.int32
U32 = mybir.dt.uint32
ALU = mybir.AluOpType
ACT = mybir.ActivationFunctionType
AX = mybir.AxisListType

P = 128
BATCHES, SEQ, D = 8, 1024, 512
HEADS, DH = 16, 32
EXPERTS = 8
KT = D // P
UNITS = HEADS // 4
BANK = 512
HALVES = SEQ // BANK
ROWT = SEQ // P
TOKENS = BATCHES * SEQ
SCALE = float(DH) ** -0.5
EPS = 1e-5
MASKED = -1e30
HI, LO = 0, 1
SETS = 3
WO_SET, WV_SET = 1, 2
Q, K = 0, 1

ROW = D + 2
W_COL, ID_COL = D, D + 1
REGION = TOKENS + P
SPARE = EXPERTS * REGION
NO_TOKEN = TOKENS + P
TILES = TOKENS // P + EXPERTS
MM3 = ((HI, HI), (HI, LO), (LO, HI))


class Signal:

    def __init__(self, ctx, nc, name, per, first):
        self.sem, self.per, self.first = ctx.enter_context(nc.semaphore(name)), per, first

    def at(self, loop, count):
        assert count >= 0
        return loop * self.per + (count + self.first)


def hold(eng, passed):
    eng.sem_inc(passed, 1)


def split_weights(nc, w_qk_parts, w_vo_parts, wq_t, wk_t, wv_t, wo_t):
    with ExitStack() as ctx:
        raw = [ctx.enter_context(nc.sbuf_tensor(f"w_raw{i}", [P, KT * D], F32)) for i in range(4)]
        both = ctx.enter_context(nc.sbuf_tensor("w_both", [P, 4, 2, KT * D], F32R))
        raw_in = [ctx.enter_context(nc.semaphore(f"w_raw_in{i}")) for i in range(4)]
        high_done = ctx.enter_context(nc.semaphore("w_high_done"))
        low_done = ctx.enter_context(nc.semaphore("w_low_done"))
        parts_out = ctx.enter_context(nc.semaphore("w_parts_out"))
        block = ctx.enter_context(nc.Block())

        @block.sync
        def _(sp):
            for i, w in enumerate((wq_t, wk_t, wv_t, wo_t)):
                sp.dma_start(raw[i][:, :].rearrange("p (k n) -> p k n", k=KT),
                             w.rearrange("(k p) n -> p k n", p=P)).then_inc(raw_in[i], 16)
            sp.wait_ge(high_done, 4)
            sp.wait_ge(low_done, 4)
            for i in range(2):
                for u in range(UNITS):
                    src = both[:, i].rearrange("p c (k n) -> p (c k) n", n=D)[:, :, u * P:(u + 1) * P]
                    sp.dma_start(w_qk_parts[u, i].rearrange("p (c n) -> p c n", n=P), src.bitcast(F32))\
                        .then_inc(parts_out, 16)
                sp.dma_start(w_vo_parts[i], both[:, 2 + i].rearrange("p c n -> p (c n)").bitcast(F32))\
                    .then_inc(parts_out, 16)
            sp.wait_ge(parts_out, 2 * (UNITS + 1) * 16)

        @block.scalar
        def _(act):
            for i in range(4):
                act.wait_ge(raw_in[i], 16)
                nc.scalar.activation(both[:, i, HI], raw[i][:, :], ACT.Copy).then_inc(high_done, 1)

        @block.vector
        def _(dve):
            for i in range(4):
                dve.wait_ge(high_done, i + 1)
                nc.vector.tensor_tensor(both[:, i, LO], raw[i][:, :], both[:, i, HI].bitcast(F32),
                                        ALU.subtract).then_inc(low_done, 1)


def attend(nc, region_end, x_t, x_rows, router_w_t, router_b, w_qk_parts, w_vo, dispatched):
    with ExitStack() as ctx:
        def sb(name, shape, dt=F32):
            return ctx.enter_context(nc.sbuf_tensor(name, shape, dt))

        def sem(name):
            return ctx.enter_context(nc.semaphore(name))

        starting = []

        def signal(name, per, dma=False):
            starting.append(Signal(ctx, nc, name, per, 16 if dma else 1))
            return starting[-1]

        xt = sb("xt", [P, 2, KT, SEQ], F32R)
        xt_raw = sb("xt_raw", [P, 2, SEQ])
        w_qk = sb("w_qk", [P, 2, 2, KT, P], F32R)
        q_st = [sb(f"q_stack{s}", [P, 4, SEQ], F32R) for s in range(SETS)]
        k_st = [sb(f"k_stack{s}", [P, 4, SEQ], F32R) for s in range(SETS)]
        v = sb("v", [P, ROWT, D])
        parts = sb("parts", [P, 2, 2, BANK], F32R)
        probs = sb("probs", [P, 8, BANK])
        rows = sb("rows", [P, ROWT, ROW])
        x_in = xt_raw[:, :, 0:D]
        recip = sb("recip", [P, BANK])
        tile_max = sb("tile_max", [P, 2, 4, ROWT])
        row_max = sb("row_max", [P, 4 * ROWT])
        neg_max = sb("neg_max", [4 * ROWT, P], F32R)
        ident = sb("ident", [P, P])
        ident_b = sb("ident_b", [P, P], BF16)
        mask_qk = sb("mask_qk", [P, P], BF16)
        mask_kq = sb("mask_kq", [P, P], BF16)
        before_b = sb("before_b", [P, P], BF16)
        ones_b = sb("ones_b", [P, P], BF16)
        ones_f = sb("ones_f", [P, DH])
        rw = sb("rw", [P, KT, EXPERTS])
        rb = sb("rb", [P, EXPERTS])
        stats = sb("stats", [P, ROWT, 6])
        mv = sb("mv", [P, ROWT, 2])
        var_eps = sb("var_eps", [P, ROWT])
        half_neg = sb("half_neg", [P, ROWT])
        rstd = sb("rstd", [P, ROWT])
        token = sb("token", [P, ROWT])
        logit = sb("logit", [P, ROWT, EXPERTS])
        expo = sb("expo", [P, ROWT, EXPERTS])
        pick = sb("pick", [P, ROWT, EXPERTS])
        onehot = sb("onehot", [P, ROWT, EXPERTS], BF16)
        order = sb("order", [P, EXPERTS])
        base = sb("base", [P, ROWT, EXPERTS])
        small = sb("small", [P, 4, ROWT])
        dest = sb("dest", [P, ROWT], U32)

        proj = [ctx.enter_context(nc.psum_tensor(f"proj{i}", [P, BANK], F32)) for i in range(2)]
        maxp = [ctx.enter_context(nc.psum_tensor(f"maxp{i}", [P, BANK], F32)) for i in range(2)]
        score = [ctx.enter_context(nc.psum_tensor(f"score{i}", [P, BANK], F32)) for i in range(2)]
        y_ps = ctx.enter_context(nc.psum_tensor("y_ps", [P, BANK], F32))
        den_ps = ctx.enter_context(nc.psum_tensor("den_ps", [P, BANK], F32))
        logit_ps = y_ps[:, 0:ROWT * EXPERTS].rearrange("p (t e) -> p t e", e=EXPERTS)
        rank_ps = den_ps[:, 0:ROWT * EXPERTS].rearrange("p (t e) -> p t e", e=EXPERTS)
        total_ps = den_ps[:, 64:64 + ROWT * EXPERTS].rearrange("p (t e) -> p t e", e=EXPERTS)

        NPROJ = UNITS * 2 * HALVES
        JOBS = NPROJ + ROWT + UNITS + ROWT + ROWT
        MTILES = 4 * sum(1 + (t * P >= BANK) for t in range(ROWT))
        STILES = MTILES
        GROUPS = STILES // 4
        setup_dma = sem("setup_dma")
        w_in = [signal(f"w_in{o}", UNITS * 16, dma=True) for o in range(2)]
        setup_done = sem("setup_done")
        setup_step = sem("setup_step")
        held_sp, held_pool, held_dve = sem("held_sp"), sem("held_pool"), sem("held_dve")
        xt_in = [signal(f"xt_in{i}", 2 * 16, dma=True) for i in range(2)]
        xt_high = signal("xt_high", KT)
        xt_low = signal("xt_low", KT)
        proj_full = [signal(f"proj_full{i}", JOBS // 2) for i in range(2)]
        proj_free = [signal(f"proj_free{i}", JOBS // 2) for i in range(2)]
        part_high = signal("part_high", NPROJ)
        stack_in = [signal(f"stack_in{i}", NPROJ // 2 * 12 * 16, dma=True) for i in range(2)]
        max_full = signal("max_full", UNITS * MTILES)
        max_free = [signal(f"max_free{i}", UNITS * MTILES // 2) for i in range(2)]
        max_step = signal("max_step", UNITS)
        max_ready = signal("max_ready", UNITS)
        neg_in = signal("neg_in", UNITS * 16, dma=True)
        score_full = signal("score_full", UNITS * STILES)
        exp_done = signal("exp_done", UNITS * STILES)
        probs_used = signal("probs_used", UNITS * GROUPS)
        recip_done = signal("recip_done", UNITS * HALVES)
        y_taken = signal("y_taken", UNITS * HALVES)
        wo_in = signal("wo_in", 16, dma=True)
        wv_in = signal("wv_in", 16, dma=True)
        y_high = signal("y_high", ROWT)
        y_low = signal("y_low", ROWT)
        x_in_dma = [signal(f"x_in_dma{i}", ROWT // 2 * 16, dma=True) for i in range(2)]
        norm_step = signal("norm_step", 2 * ROWT + 1)
        var_ready = signal("var_ready", 1)
        rstd_ready = signal("rstd_ready", 1)
        normed = signal("normed", ROWT)
        logits_done = signal("logits_done", ROWT)
        route_step = signal("route_step", 15 + ROWT)
        shifted = signal("shifted", 1)
        exp_route = signal("exp_route", 1)
        onehot_ready = signal("onehot_ready", 1)
        ranks_done = signal("ranks_done", 1)
        dest_ready = signal("dest_ready", 1)
        scattered = Signal(ctx, nc, "scattered", ROWT * 16, 16)
        assert JOBS % 2 == 0

        job_names = [("p", 0, i) for i in range(4)] + [("v", i) for i in range(ROWT)]
        job_names += [("p", 1, i) for i in range(4)] + [("m", 0)]
        for u in range(1, UNITS):
            job_names += [("p", u + 1, i) for i in range(4)] * (u + 1 < UNITS) + [("m", u)]
        job_names += [("o", i) for i in range(ROWT)] + [("x", i) for i in range(ROWT)]
        assert len(job_names) == JOBS
        job = {name: n for n, name in enumerate(job_names)}

        def wait_job(eng, b, sems, name):
            n = job[name]
            eng.wait_ge(sems[n % 2].sem, sems[n % 2].at(b, n // 2 + 1))

        def wait_last_batch(eng, b, sems):
            for s in sems:
                eng.wait_ge(s.sem, s.at(b, 0))

        def weighed(eng, b, n):
            eng.wait_ge(probs_used.sem, probs_used.at(b, n))

        def width(kb, t):
            return max(kb * P - t * BANK, 0)

        def groups():
            return [(t, kb) for t in range(HALVES) for kb in range((t + 1) * BANK // P)]

        def max_tiles():
            for qb in range(ROWT):
                for h in range(4):
                    for j in range(1 + (qb * P >= BANK)):
                        cols = min((qb + 1) * P - j * BANK, BANK)
                        diag = qb * P - j * BANK if qb * P >= j * BANK and qb * P < (j + 1) * BANK else None
                        yield qb, h, j, cols, max(cols, 256), diag

        MAX_TILES = list(max_tiles())
        assert len(MAX_TILES) == MTILES and len(groups()) == GROUPS

        block = ctx.enter_context(nc.Block())

        def next_batch(b):
            return (b + 1) % BATCHES

        @block.sync
        def _(sp):
            for s in starting:
                sp.sem_inc(s.sem, s.first)
            sp.dma_start(rw[:, :, :], router_w_t.rearrange("(k p) e -> p k e", p=P)).then_inc(setup_dma, 16)
            sp.dma_start(rb[:, :], router_b.partition_broadcast(P)).then_inc(setup_dma, 16)
            sp.dma_start(q_st[WV_SET][:, :, :].rearrange("p h n -> p (h n)").bitcast(F32), w_vo[0]).then_inc(setup_dma, 16)

            def load_w(u, o):
                sp.dma_start(w_qk[:, o].rearrange("p c k n -> p (c k n)").bitcast(F32), w_qk_parts[u, o])\
                    .then_inc(w_in[o].sem, 16)

            def load_xt(batch, b, k, first):
                if not first:
                    sp.wait_ge(xt_high.sem, xt_high.at(b, KT + k - 1))
                    sp.wait_ge(xt_low.sem, xt_low.at(b, KT + k - 1))
                hold(sp, held_sp)
                sp.dma_start(xt_raw[:, k % 2, :], x_t[k * P:(k + 1) * P, bass.ds(batch * SEQ, SEQ)])\
                    .then_inc(xt_in[k % 2].sem, 16)

            load_w(0, Q)
            load_w(0, K)
            for k in range(KT):
                if k >= 2:
                    sp.wait_ge(xt_high.sem, xt_high.at(0, k - 1))
                    sp.wait_ge(xt_low.sem, xt_low.at(0, k - 1))
                load_xt(0, 0, k, True)

            with sp.Fori(0, BATCHES) as b:
                def stack_tile(u, i):
                    o, t = divmod(i, HALVES)
                    n = 4 * u + i
                    wait_job(sp, b, proj_free, ("p", u, i))
                    dst = (q_st, k_st)[o][u % SETS]
                    for block_row, part in enumerate((HI, HI, LO) if o == Q else (HI, LO, HI)):
                        for h in range(4):
                            sp.dma_start(dst[DH * block_row:DH * (block_row + 1), h, t * BANK:(t + 1) * BANK].bitcast(F32),
                                         parts[DH * h:DH * (h + 1), n % 2, part, :].bitcast(F32))\
                                .then_inc(stack_in[n % 2].sem, 16)

                def neg_row(u):
                    wait_job(sp, b, proj_free, ("m", u))
                    sp.dma_start(q_st[u % SETS][3 * DH:3 * DH + 1, :, :].rearrange("p h (t c) -> p (h t) c", c=P).bitcast(F32),
                                 neg_max[:, :].bitcast(F32)).then_inc(neg_in.sem, 16)

                def load_x(tb):
                    hold(sp, held_sp)
                    sp.dma_start(x_in[:, tb % 2, :], x_rows[bass.ds(b * SEQ + tb * P, P), :])\
                        .then_inc(x_in_dma[tb % 2].sem, 16)

                def stack_unit(u):
                    hold(sp, held_sp)
                    for i in range(4):
                        stack_tile(u, i)
                        if i % 2:
                            load_w((u + 1) % UNITS, i // 2)

                weighed(sp, b, 0)
                stack_unit(0)
                wait_last_batch(sp, b, proj_full)
                stack_unit(1)
                neg_row(0)
                wait_job(sp, b, proj_full, ("v", ROWT - 2))
                hold(sp, held_sp)
                wait_job(sp, b, proj_full, ("v", ROWT - 1))
                stack_unit(2)
                neg_row(1)
                weighed(sp, b, GROUPS)
                stack_unit(3)
                neg_row(2)
                weighed(sp, b, GROUPS * 2)
                sp.dma_start(q_st[WO_SET][:, :, :].rearrange("p h n -> p (h n)").bitcast(F32), w_vo[1]).then_inc(wo_in.sem, 16)
                neg_row(3)
                weighed(sp, b, GROUPS * 3)
                sp.dma_start(q_st[WV_SET][:, :, :].rearrange("p h n -> p (h n)").bitcast(F32), w_vo[0]).then_inc(wv_in.sem, 16)
                wait_last_batch(sp, b, proj_free)
                for k in range(KT):
                    load_xt(next_batch(b), b, k, False)
                sp.wait_ge(xt_high.sem, xt_high.at(b + 1, KT))
                hold(sp, held_sp)
                sp.wait_ge(xt_low.sem, xt_low.at(b + 1, KT))
                load_x(0)
                load_x(1)
                for tb in range(2, ROWT):
                    wait_job(sp, b, proj_free, ("o", tb - 2))
                    load_x(tb)

        @block.gpsimd
        def _(pool):
            step = 0

            def link(ins):
                nonlocal step
                step += 1
                ins.then_inc(setup_step, 1)
                pool.wait_ge(setup_step, step)

            link(nc.gpsimd.memset(ident[:, :], 0.0))
            link(nc.gpsimd.memset(ones_b[:, :], 1.0))
            link(nc.gpsimd.memset(ones_f[:, :], 1.0))
            link(nc.gpsimd.memset(mask_qk[:, :], MASKED))
            link(nc.gpsimd.memset(mask_kq[:, :], MASKED))
            link(nc.gpsimd.memset(half_neg[:, :], -0.5))
            link(nc.gpsimd.affine_select(out=ident[:, :], in_=ident[:, :], compare_op=ALU.not_equal, fill=1.0,
                                         base=0, pattern=[[-1, P]], channel_multiplier=1))
            link(nc.gpsimd.tensor_copy(ident_b[:, :], ident[:, :]))
            link(nc.gpsimd.affine_select(out=mask_qk[:, :], in_=mask_qk[:, :], compare_op=ALU.is_gt, fill=0.0,
                                         base=0, pattern=[[1, P]], channel_multiplier=-1))
            link(nc.gpsimd.affine_select(out=mask_kq[:, :], in_=mask_kq[:, :], compare_op=ALU.is_gt, fill=0.0,
                                         base=0, pattern=[[-1, P]], channel_multiplier=1))
            link(nc.gpsimd.affine_select(out=before_b[:, :], in_=ones_b[:, :], compare_op=ALU.is_gt, fill=0.0,
                                         base=0, pattern=[[1, P]], channel_multiplier=-1))
            link(nc.gpsimd.iota(order[:, :], [[-1, EXPERTS]], base=EXPERTS, channel_multiplier=0,
                                allow_small_or_imprecise_dtypes=True))
            link(nc.gpsimd.iota(token[:, :], [[P, ROWT]], base=0, channel_multiplier=1,
                                allow_small_or_imprecise_dtypes=True))
            link(nc.gpsimd.iota(region_end[:, :], [[REGION, EXPERTS]], base=0, channel_multiplier=0,
                                allow_small_or_imprecise_dtypes=True))
            for s in range(SETS):
                link(nc.gpsimd.memset(k_st[s][3 * DH:3 * DH + 1, :, :].bitcast(F32), 1.0))
            link(nc.gpsimd.memset(rows[:, 0, 0:ID_COL], 0.0))
            link(nc.gpsimd.memset(rows[:, 0, ID_COL:ROW], float(NO_TOKEN)))
            nc.gpsimd.dma_start(dispatched[SPARE:SPARE + P, :], rows[:, 0, :]).then_inc(scattered.sem, 16)
            nc.gpsimd.memset(small[:, :, :], 0.0).then_inc(setup_done, 1)

            def split_low(k, count):
                pool.wait_ge(xt_high.sem, count)
                nc.gpsimd.tensor_tensor(xt[:, LO, k, :], xt_raw[:, k % 2, :], xt[:, HI, k, :].bitcast(F32),
                                        ALU.subtract).then_inc(xt_low.sem, 1)

            for k in range(KT):
                split_low(k, xt_high.at(0, k + 1))
            with pool.Fori(0, BATCHES) as b:
                for k in range(KT):
                    split_low(k, xt_high.at(b + 1, k + 1))
                for tb in range(ROWT):
                    pool.wait_ge(y_high.sem, y_high.at(b, tb + 1))
                    nc.gpsimd.tensor_tensor(parts[:, tb % 2, LO, :], rows[:, tb, 0:D],
                                            parts[:, tb % 2, HI, :].bitcast(F32), ALU.subtract)\
                        .then_inc(y_low.sem, 1)
                pool.wait_ge(var_ready.sem, var_ready.at(b, 1))
                nc.gpsimd.tensor_tensor(rstd[:, :], var_eps[:, :], half_neg[:, :], ALU.pow).then_inc(rstd_ready.sem, 1)
                pool.wait_ge(dest_ready.sem, dest_ready.at(b, 1))
                hold(pool, held_pool)
                for tb in range(ROWT):
                    nc.gpsimd.indirect_dma_start(
                        out=dispatched, out_offset=bass.IndirectOffsetOnAxis(ap=dest[:, tb:tb + 1], axis=0),
                        in_=rows[:, tb, :], in_offset=None).then_inc(scattered.sem, 16)
            pool.wait_ge(scattered.sem, scattered.at(BATCHES, 0))

        @block.scalar
        def _(act):
            def split_high(k, count):
                act.wait_ge(xt_in[k % 2].sem, count)
                nc.scalar.activation(xt[:, HI, k, :], xt_raw[:, k % 2, :], ACT.Copy).then_inc(xt_high.sem, 1)

            for k in range(KT):
                split_high(k, xt_in[k % 2].at(0, 16 * (k // 2 + 1)))
            with act.Fori(0, BATCHES) as b:
                def take(name):
                    n = job[name]
                    act.wait_ge(proj_full[n % 2].sem, proj_full[n % 2].at(b, n // 2 + 1))
                    return proj[n % 2], proj_free[n % 2].sem

                def high(u, i):
                    n = 4 * u + i
                    bank, _ = take(("p", u, i))
                    act.wait_ge(stack_in[n % 2].sem, stack_in[n % 2].at(b, n // 2 * 12 * 16))
                    nc.scalar.activation(parts[:, n % 2, HI, :], bank[:, :], ACT.Copy).then_inc(part_high.sem, 1)

                def negate(u):
                    bank, free = take(("m", u))
                    act.wait_ge(neg_in.sem, neg_in.at(b, 16 * u))
                    nc.scalar.activation(neg_max[:, :], bank[0:4 * ROWT, 0:P], ACT.Copy, scale=-1.0).then_inc(free, 1)

                wait_last_batch(act, b, proj_full)
                for i in range(4):
                    high(0, i)
                for i in range(ROWT):
                    bank, free = take(("v", i))
                    nc.scalar.activation(v[:, i, :], bank[:, :], ACT.Copy).then_inc(free, 1)
                for i in range(4):
                    high(1, i)
                negate(0)
                act.wait_ge(logits_done.sem, logits_done.at(b, 0))
                for u in range(UNITS):
                    if u == 3:
                        wait_job(act, b, proj_full, ("p", 3, 2))
                        wait_job(act, b, proj_full, ("p", 3, 3))
                        for k in range(KT):
                            split_high(k, xt_in[k % 2].at(b + 1, 16 * (k // 2 + 1)))
                    for j, (t, kb) in enumerate(groups()):
                        n = GROUPS * u + j
                        if n >= 2:
                            act.wait_ge(probs_used.sem, probs_used.at(b, n - 1))
                        for h in range(4):
                            c = width(kb, t)
                            i = STILES * u + 4 * j + h
                            act.wait_ge(score_full.sem, score_full.at(b, i + 1))
                            nc.scalar.activation(probs[:, 4 * (n % 2) + h, c:BANK], score[h % 2][:, c:BANK],
                                                 ACT.Exp, scale=SCALE).then_inc(exp_done.sem, 1)
                        if u + 2 < UNITS and j % 3 == 2:
                            high(u + 2, j // 3)
                    if u + 1 < UNITS:
                        negate(u + 1)
                act.wait_ge(y_taken.sem, y_taken.at(b, UNITS * HALVES))
                act.wait_ge(stack_in[0].sem, stack_in[0].at(b + 1, 0))
                act.wait_ge(stack_in[1].sem, stack_in[1].at(b + 1, 0))
                for tb in range(ROWT):
                    if tb >= 2:
                        wait_job(act, b, proj_full, ("o", tb - 2))
                    nc.scalar.activation(parts[:, tb % 2, HI, :], rows[:, tb, 0:D], ACT.Copy).then_inc(y_high.sem, 1)
                for tb in range(ROWT):
                    bank, free = take(("x", tb))
                    nc.scalar.activation(probs[:, tb, :], bank[:, :], ACT.Copy).then_inc(free, 1)
                act.wait_ge(shifted.sem, shifted.at(b, 1))
                nc.scalar.activation(expo[:, :, :], logit[:, :, :], ACT.Exp).then_inc(exp_route.sem, 1)

        @block.vector
        def _(dve):
            dve.wait_ge(setup_done, 1)
            dve.wait_ge(setup_dma, 48)
            with dve.Fori(0, BATCHES) as b:
                def low(u, i):
                    n, jn = 4 * u + i, job[("p", u, i)]
                    dve.wait_ge(part_high.sem, part_high.at(b, n + 1))
                    nc.vector.tensor_tensor(parts[:, n % 2, LO, :], proj[jn % 2][:, :], parts[:, n % 2, HI, :].bitcast(F32),
                                            ALU.subtract).then_inc(proj_free[jn % 2].sem, 1)

                def reduce_tile(u, i):
                    qb, h, j, cols, _, _ = MAX_TILES[i]
                    n = MTILES * u + i
                    dve.wait_ge(max_full.sem, max_full.at(b, n + 1))
                    nc.vector.tensor_reduce(tile_max[:, j, h, qb:qb + 1], maxp[n % 2][:, 0:cols], AX.X, ALU.max)\
                        .then_inc(max_free[n % 2].sem, 1)

                def unit_max(u):
                    half = BANK // P
                    dve.wait_ge(max_free[0].sem, max_free[0].at(b, MTILES // 2 * (u + 1)))
                    dve.wait_ge(max_free[1].sem, max_free[1].at(b, MTILES // 2 * (u + 1)))
                    if u:
                        wait_job(dve, b, proj_full, ("m", u - 1))
                    rm = row_max[:, :].rearrange("p (h t) -> p h t", h=4)
                    nc.vector.tensor_copy(rm[:, :, 0:half], tile_max[:, 0, :, 0:half]).then_inc(max_step.sem, 1)
                    nc.vector.tensor_tensor(rm[:, :, half:ROWT], tile_max[:, 0, :, half:ROWT],
                                            tile_max[:, 1, :, half:ROWT], ALU.max).then_inc(max_ready.sem, 1)

                def take_y(u, t):
                    n = HALVES * u + t
                    weighed(dve, b, GROUPS * u + (BANK // P if t == 0 else GROUPS))
                    nc.vector.reciprocal(recip[:, :], den_ps[:, :]).then_inc(recip_done.sem, 1)
                    dve.wait_ge(recip_done.sem, recip_done.at(b, n + 1))
                    if n == 0:
                        dve.wait_ge(scattered.sem, scattered.at(b, 0))
                    nc.vector.tensor_tensor(
                        rows[:, 4 * t:4 * t + 4, u * P:(u + 1) * P],
                        y_ps[:, :].rearrange("p (t q) -> p t q", q=P), recip[:, :].rearrange("p (t q) -> p t q", q=P),
                        ALU.mult).then_inc(y_taken.sem, 1)

                for i in range(4):
                    low(0, i)
                for i in range(MTILES):
                    reduce_tile(0, i)
                    if i % 12 == 11:
                        low(1, i // 12)
                unit_max(0)
                for u in range(UNITS):
                    for j in range(GROUPS):
                        if u + 1 < UNITS:
                            for i in range(4 * j, 4 * j + 4):
                                reduce_tile(u + 1, i)
                        if u + 2 < UNITS and j % 3 == 2:
                            low(u + 2, j // 3)
                        if j == BANK // P:
                            take_y(u, 0)
                    if u + 1 < UNITS:
                        unit_max(u + 1)
                    take_y(u, 1)

                step = 0
                for tb in range(ROWT):
                    jn = job[("o", tb)]
                    dve.wait_ge(proj_full[jn % 2].sem, proj_full[jn % 2].at(b, jn // 2 + 1))
                    dve.wait_ge(x_in_dma[tb % 2].sem, x_in_dma[tb % 2].at(b, 16 * (tb // 2 + 1)))
                    nc.vector.tensor_tensor(rows[:, tb, 0:D], proj[jn % 2][:, :], x_in[:, tb % 2, :], ALU.add)\
                        .then_inc(proj_free[jn % 2].sem, 1)
                    wait_job(dve, b, proj_free, ("o", tb))
                    nc.vector.bn_stats(stats[:, tb, :], rows[:, tb, 0:D]).then_inc(norm_step.sem, 1)
                    dve.wait_ge(norm_step.sem, norm_step.at(b, 2 * tb + 1))
                    hold(dve, held_dve)
                    nc.vector.bn_aggr(mv[:, tb, :], stats[:, tb, :]).then_inc(norm_step.sem, 1)
                dve.wait_ge(norm_step.sem, norm_step.at(b, 2 * ROWT))
                nc.vector.tensor_scalar(var_eps[:, :], mv[:, :, 1], EPS, None, ALU.add).then_inc(var_ready.sem, 1)
                nc.vector.tensor_copy(rows[:, :, ID_COL], token[:, :]).then_inc(norm_step.sem, 1)
                dve.wait_ge(rstd_ready.sem, rstd_ready.at(b, 1))
                for tb in range(ROWT):
                    nc.vector.tensor_scalar(rows[:, tb, 0:D], rows[:, tb, 0:D], mv[:, tb, 0:1], rstd[:, tb:tb + 1],
                                            ALU.subtract, ALU.mult).then_inc(normed.sem, 1)

                def link(ins):
                    nonlocal step
                    step += 1
                    ins.then_inc(route_step.sem, 1)
                    dve.wait_ge(route_step.sem, route_step.at(b, step))

                wide = [P, ROWT, EXPERTS]
                per_tile = lambda a: a.unsqueeze(2).to_broadcast(wide)
                per_expert = lambda a: a.unsqueeze(1).to_broadcast(wide)
                dve.wait_ge(norm_step.sem, norm_step.at(b, 2 * ROWT + 1))
                link(nc.vector.tensor_scalar(token[:, :], token[:, :], float(SEQ), None, ALU.add))
                dve.wait_ge(logits_done.sem, logits_done.at(b, ROWT))
                link(nc.vector.tensor_tensor(pick[:, :, :], logit_ps, per_expert(rb[:, :]), ALU.add))
                link(nc.vector.tensor_reduce(small[:, 0, :], pick[:, :, :], AX.X, ALU.max))
                nc.vector.tensor_tensor(logit[:, :, :], pick[:, :, :], per_tile(small[:, 0, :]), ALU.subtract)\
                    .then_inc(shifted.sem, 1)
                dve.wait_ge(shifted.sem, shifted.at(b, 1))
                link(nc.vector.tensor_scalar(pick[:, :, :], logit[:, :, :], 0.0, None, ALU.is_ge))
                link(nc.vector.tensor_tensor(pick[:, :, :], pick[:, :, :], per_expert(order[:, :]), ALU.mult))
                link(nc.vector.tensor_reduce(small[:, 1, :], pick[:, :, :], AX.X, ALU.max))
                nc.vector.tensor_tensor(onehot[:, :, :], pick[:, :, :], per_tile(small[:, 1, :]), ALU.is_equal)\
                    .then_inc(onehot_ready.sem, 1)
                dve.wait_ge(exp_route.sem, exp_route.at(b, 1))
                link(nc.vector.tensor_reduce(small[:, 2, :], expo[:, :, :], AX.X, ALU.add))
                link(nc.vector.reciprocal(rows[:, :, W_COL], small[:, 2, :]))
                dve.wait_ge(ranks_done.sem, ranks_done.at(b, 1))
                link(nc.vector.tensor_copy(base[:, 0, :], region_end[:, :]))
                for tb in range(ROWT):
                    after = base[:, tb + 1, :] if tb + 1 < ROWT else region_end[:, :]
                    link(nc.vector.tensor_tensor(after, total_ps[:, tb, :], base[:, tb, :], ALU.add))
                link(nc.vector.tensor_tensor(base[:, :, :], rank_ps, base[:, :, :], ALU.add))
                link(nc.vector.tensor_tensor(base[:, :, :], base[:, :, :], onehot[:, :, :], ALU.mult))
                link(nc.vector.tensor_reduce(small[:, 3, :], base[:, :, :], AX.X, ALU.add))
                nc.vector.tensor_copy(dest[:, :], small[:, 3, :]).then_inc(dest_ready.sem, 1)
                assert step <= route_step.per, step
                for _ in range(route_step.per - step):
                    dve.sem_inc(route_step.sem, 1)

        @block.tensor
        def _(pe):
            pe.wait_ge(setup_done, 1)
            pe.wait_ge(setup_dma, 48)
            with pe.Fori(0, BATCHES) as b:
                def begin(name):
                    n = job[name]
                    pe.wait_ge(proj_free[n % 2].sem, proj_free[n % 2].at(b, n // 2))
                    return proj[n % 2], proj_full[n % 2].sem

                def project(u, i, piece=None):
                    o, t = divmod(i, HALVES)
                    n = job[("p", u, i)]
                    if piece in (None, 0):
                        begin(("p", u, i))
                        if t == 0:
                            pe.wait_ge(w_in[o].sem, w_in[o].at(b, 16 * (u + 1)))
                    for c in range(3 * KT) if piece is None else range(4 * piece, 4 * piece + 4):
                        k, (ws, xs) = c // 3, MM3[c % 3]
                        mm = nc.tensor.matmul(proj[n % 2][:, :], w_qk[:, o, ws, k, :],
                                              xt[:, xs, k, t * BANK:(t + 1) * BANK], start=c == 0, stop=c == 3 * KT - 1)
                        if c == 3 * KT - 1:
                            mm.then_inc(proj_full[n % 2].sem, 1)

                def values(tb):
                    bank, full = begin(("v", tb))
                    wv = q_st[WV_SET][:, :, :].rearrange("p (c k) (l n) -> p c (k l) n", c=2, n=D)
                    for c in range(3 * KT):
                        k, (xs, ws) = c // 3, MM3[c % 3]
                        mm = nc.tensor.matmul(bank[:, :], xt[:, xs, k, tb * P:(tb + 1) * P], wv[:, ws, k, :],
                                              start=c == 0, stop=c == 3 * KT - 1)
                    mm.then_inc(full, 1)

                def max_tile(u, i):
                    qb, h, j, cols, computed, diag = MAX_TILES[i]
                    n = MTILES * u + i
                    pe.wait_ge(max_free[n % 2].sem, max_free[n % 2].at(b, n // 2))
                    mm = nc.tensor.matmul(maxp[n % 2][:, 0:computed], q_st[u % SETS][0:3 * DH, h, qb * P:(qb + 1) * P],
                                          k_st[u % SETS][0:3 * DH, h, j * BANK:j * BANK + computed],
                                          start=True, stop=True)
                    if diag is not None:
                        mm = nc.tensor.matmul(maxp[n % 2][:, diag:diag + P], ident_b[:, :], mask_qk[:, :],
                                              start=False, stop=True, skip_group_check=True)
                    mm.then_inc(max_full.sem, 1)

                def score_tile(u, j, h):
                    t, kb = groups()[j]
                    i = STILES * u + 4 * j + h
                    c = width(kb, t)
                    c0 = min(c, BANK - 256)
                    if i >= 2:
                        pe.wait_ge(exp_done.sem, exp_done.at(b, i - 1))
                    else:
                        pe.wait_ge(exp_done.sem, exp_done.at(b, 0))
                    mm = nc.tensor.matmul(score[h % 2][:, c0:BANK], k_st[u % SETS][0:3 * DH + 1, h, kb * P:(kb + 1) * P],
                                          q_st[u % SETS][0:3 * DH + 1, h, t * BANK + c0:(t + 1) * BANK],
                                          start=True, stop=True)
                    if kb * P >= t * BANK:
                        mm = nc.tensor.matmul(score[h % 2][:, c:c + P], ident_b[:, :], mask_kq[:, :],
                                              start=False, stop=True, skip_group_check=True)
                    mm.then_inc(score_full.sem, 1)

                def weigh(u, j):
                    t, kb = groups()[j]
                    n = GROUPS * u + j
                    last = kb == (t + 1) * BANK // P - 1
                    c = width(kb, t)
                    pe.wait_ge(exp_done.sem, exp_done.at(b, 4 * (n + 1)))
                    if kb == 0:
                        pe.wait_ge(y_taken.sem, y_taken.at(b, HALVES * u + t))
                    for h in range(4):
                        head = 4 * u + h
                        nc.tensor.matmul(y_ps[DH * h:DH * (h + 1), c:BANK], v[:, kb, head * DH:(head + 1) * DH],
                                         probs[:, 4 * (n % 2) + h, c:BANK], start=kb == 0, stop=last,
                                         tile_position=(0, DH * h), skip_group_check=True)
                    for h in range(4):
                        mm = nc.tensor.matmul(den_ps[DH * h:DH * (h + 1), c:BANK], ones_f[:, :],
                                              probs[:, 4 * (n % 2) + h, c:BANK], start=kb == 0, stop=last,
                                              tile_position=(0, DH * h), skip_group_check=True)
                    mm.then_inc(probs_used.sem, 1)

                def transpose_max(u):
                    pe.wait_ge(max_step.sem, max_step.at(b, u + 1))
                    pe.wait_ge(max_ready.sem, max_ready.at(b, u + 1))
                    bank, full = begin(("m", u))
                    nc.tensor.transpose(bank[0:4 * ROWT, 0:P], row_max[:, :], ident[:, :]).then_inc(full, 1)

                pe.wait_ge(xt_low.sem, xt_low.at(b + 1, 0))
                for i in range(4):
                    project(0, i)
                pe.wait_ge(wv_in.sem, wv_in.at(b, 0))
                for tb in range(ROWT):
                    values(tb)
                for s in range(2):
                    pe.wait_ge(stack_in[s].sem, stack_in[s].at(b, 2 * 12 * 16))
                for i in range(MTILES):
                    if i % 12 in (2, 5, 8):
                        project(1, i // 12, i % 12 // 3)
                    max_tile(0, i)
                transpose_max(0)
                wait_job(pe, b, proj_free, ("v", ROWT - 2))
                wait_job(pe, b, proj_free, ("v", ROWT - 1))
                for u in range(UNITS):
                    if u + 1 < UNITS:
                        for s in range(2):
                            pe.wait_ge(stack_in[s].sem, stack_in[s].at(b, 2 * (u + 2) * 12 * 16))
                    for j in range(GROUPS):
                        for h in range(4):
                            if u + 1 < UNITS:
                                max_tile(u + 1, 4 * j + h)
                            if j == 0 and h == 0:
                                pe.wait_ge(neg_in.sem, neg_in.at(b, 16 * (u + 1)))
                            score_tile(u, j, h)
                        if u + 2 < UNITS:
                            project(u + 2, j // 3, j % 3)
                        if j:
                            weigh(u, j - 1)
                    if u + 1 < UNITS:
                        transpose_max(u + 1)
                    weigh(u, GROUPS - 1)

                wo = q_st[WO_SET][:, :, :].rearrange("p (c k) (l n) -> p c (k l) n", c=2, n=D)
                pe.wait_ge(wo_in.sem, wo_in.at(b, 16))
                for tb in range(ROWT):
                    bank, full = begin(("o", tb))
                    pe.wait_ge(y_low.sem, y_low.at(b, tb + 1))
                    for c in range(3 * UNITS):
                        g, (ys, ws) = c // 3, MM3[c % 3]
                        mm = nc.tensor.matmul(bank[:, :], parts[:, tb % 2, ys, g * P:(g + 1) * P], wo[:, ws, g, :],
                                              start=c == 0, stop=c == 3 * UNITS - 1)
                    mm.then_inc(full, 1)
                for tb in range(ROWT + 1):
                    if tb < ROWT:
                        pe.wait_ge(normed.sem, normed.at(b, tb + 1))
                        bank, full = begin(("x", tb))
                        for k in range(KT):
                            mm = nc.tensor.transpose(bank[:, k * P:(k + 1) * P], rows[:, tb, k * P:(k + 1) * P], ident[:, :])
                        mm.then_inc(full, 1)
                    if tb:
                        wait_job(pe, b, proj_free, ("x", tb - 1))
                        if tb == 1:
                            pe.wait_ge(y_taken.sem, y_taken.at(b, UNITS * HALVES))
                        for k in range(KT):
                            mm = nc.tensor.matmul(logit_ps[:, tb - 1, :], probs[:, tb - 1, k * P:(k + 1) * P], rw[:, k, :],
                                                  start=k == 0, stop=k == KT - 1, skip_group_check=True)
                        mm.then_inc(logits_done.sem, 1)
                pe.wait_ge(onehot_ready.sem, onehot_ready.at(b, 1))
                hot = onehot[:, :, :].rearrange("p t e -> p (t e)")
                nc.tensor.matmul(rank_ps.rearrange("p t e -> p (t e)"), before_b[:, :], hot, start=True, stop=True,
                                 skip_group_check=True)
                nc.tensor.matmul(total_ps.rearrange("p t e -> p (t e)"), ones_b[:, :], hot, start=False, stop=True,
                                 skip_group_check=True).then_inc(ranks_done.sem, 1)
                pe.wait_ge(dest_ready.sem, dest_ready.at(b, 1))


def run_experts(nc, region_end, expert_w_t, expert_b, dispatched, unread, out):
    RING = 4
    STEPS = -(-TILES // RING) * RING
    TABLE = STEPS + 1
    with ExitStack() as ctx:
        def sb(name, shape, dt=F32):
            return ctx.enter_context(nc.sbuf_tensor(name, shape, dt))

        def sem(name):
            return ctx.enter_context(nc.semaphore(name))

        starting = []

        def signal(name, per=RING, dma=False):
            starting.append(Signal(ctx, nc, name, per, 16 if dma else 1))
            return starting[-1]

        weight = sb("weight", [P, 2, EXPERTS * KT * D], F32R)
        w_raw = sb("w_raw", [P, 2, KT * D])
        bias = sb("bias", [P, EXPERTS * D])
        got = sb("got", [P, RING, ROW])
        xt = sb("xt_tile", [P, 2, 2, D], F32R)
        y = sb("y", [P, 2, D])
        ident = sb("ident2", [P, P])
        pad = sb("pad", [P, ROW])
        stats = sb("stats2", [P, 2, 6])
        mv = sb("mv2", [P, 2, 2])
        var_eps = sb("var_eps2", [P, 2])
        half_neg = sb("half_neg2", [P, 1])
        rstd = sb("rstd2", [P, 2])
        home = sb("home", [P, 2], U32)
        lane = sb("lane", [P, EXPERTS])
        first = sb("first", [P, EXPERTS])
        tile_rows = sb("tile_rows", [P, TOKENS // P])
        tile_no = sb("tile_no", [P, TABLE])
        count = sb("count", [P, EXPERTS])
        tiles = sb("tiles", [P, EXPERTS])
        more = sb("more", [P, EXPERTS, TOKENS // P])
        end = sb("end", [P, EXPERTS])
        passed = sb("passed", [P, TABLE, EXPERTS])
        scaled = sb("scaled", [P, TABLE, EXPERTS])
        expert_f = sb("expert_f", [P, TABLE])
        start_f = sb("start_f", [P, TABLE])
        work = sb("work", [P, 2, TABLE])
        expert = sb("expert", [P, TABLE], I32)
        start = sb("start", [P, TABLE], I32)
        tail = sb("tail", [P, EXPERTS])
        tail_row = sb("tail_row", [P, EXPERTS], U32)
        xt_ps = [ctx.enter_context(nc.psum_tensor(f"xt_ps{i}", [P, BANK], F32)) for i in range(2)]
        y_ps = [ctx.enter_context(nc.psum_tensor(f"ye_ps{i}", [P, BANK], F32)) for i in range(2)]

        raw_in = [sem(f"ew_in{i}") for i in range(2)]
        high_done = sem("ew_high")
        low_done = sem("ew_low")
        bias_in = sem("bias_in")
        consts = sem("consts")
        pool_step = sem("pool_step")
        plan_step = sem("plan_step")
        tail_ready = sem("tail_ready")
        table_ready = sem("table_ready")
        padded = sem("padded")
        held_sp, held_pool, held_dve = sem("held_sp2"), sem("held_pool2"), sem("held_dve2")
        got_in = [signal(f"got_in{i}", 16, dma=True) for i in range(RING)]
        turned = signal("turned")
        xt_high = signal("xe_high")
        xt_low = signal("xe_low")
        y_full = signal("ye_full")
        y_free = signal("ye_free")
        row_step = signal("row_step", 3 * RING)
        var_ready = signal("var_ready2")
        rstd_ready = signal("rstd_ready2")
        normed = signal("normed2")
        sent = [Signal(ctx, nc, f"sent{i}", RING // 2 * 16, 16) for i in range(2)]
        block = ctx.enter_context(nc.Block())

        @block.sync
        def _(sp):
            for s in starting:
                sp.sem_inc(s.sem, s.first)
            sp.dma_start(bias[:, :], expert_b.rearrange("e n -> (e n)").partition_broadcast(P)).then_inc(bias_in, 16)
            for e in range(EXPERTS):
                if e >= 2:
                    sp.wait_ge(high_done, e - 1)
                    sp.wait_ge(low_done, e - 1)
                sp.dma_start(w_raw[:, e % 2, :].rearrange("p (k n) -> p k n", k=KT),
                             expert_w_t[e].rearrange("(k p) n -> p k n", p=P)).then_inc(raw_in[e % 2], 16)

            def load(at, slot):
                hold(sp, held_sp)
                row = sp.value_load(start[0:1, at], min_val=0, max_val=SPARE)
                sp.dma_start(got[:, slot, :], dispatched[bass.ds(row, P), :]).then_inc(got_in[slot].sem, 16)

            sp.wait_ge(table_ready, 2)
            sp.wait_ge(padded, EXPERTS * 16)
            load(slice(0, 1), 0)
            with sp.Fori(0, STEPS // RING) as i:
                for s in range(RING):
                    if s < RING - 1:
                        sp.wait_ge(y_free.sem, y_free.at(i, 0))
                        hold(sp, held_sp)
                        sp.wait_ge(row_step.sem, row_step.at(i, 0))
                        load(bass.ds(i * RING + s + 1, 1), s + 1)
                    else:
                        sp.wait_ge(row_step.sem, row_step.at(i, 3))
                        load(bass.ds(i * RING + s + 1, 1), 0)
            sp.wait_ge(got_in[0].sem, got_in[0].at(STEPS // RING, 16))

        @block.gpsimd
        def _(pool):
            step = 0

            def link(ins):
                nonlocal step
                step += 1
                ins.then_inc(pool_step, 1)
                pool.wait_ge(pool_step, step)

            loose = dict(allow_small_or_imprecise_dtypes=True)
            link(nc.gpsimd.memset(ident[:, :], 0.0))
            link(nc.gpsimd.memset(pad[:, 0:ID_COL], 0.0))
            link(nc.gpsimd.memset(pad[:, ID_COL:ROW], float(NO_TOKEN)))
            link(nc.gpsimd.memset(half_neg[:, :], -0.5))
            link(nc.gpsimd.affine_select(out=ident[:, :], in_=ident[:, :], compare_op=ALU.not_equal, fill=1.0,
                                         base=0, pattern=[[-1, P]], channel_multiplier=1))
            link(nc.gpsimd.iota(lane[:, :], [[0, EXPERTS]], base=0, channel_multiplier=1, **loose))
            link(nc.gpsimd.iota(first[:, :], [[REGION, EXPERTS]], base=0, channel_multiplier=0, **loose))
            link(nc.gpsimd.iota(tile_rows[:, :], [[P, TOKENS // P]], base=0, channel_multiplier=0, **loose))
            nc.gpsimd.iota(tile_no[:, :], [[1, TABLE]], base=0, channel_multiplier=0, **loose).then_inc(consts, 1)
            pool.wait_ge(tail_ready, 1)
            pool.wait_ge(consts, 1)
            for s in range(2):
                nc.gpsimd.dma_start(unread[s * P:(s + 1) * P, :], pad[:, :]).then_inc(sent[s].sem, 16)
            for e in range(EXPERTS):
                nc.gpsimd.indirect_dma_start(
                    out=dispatched, out_offset=bass.IndirectOffsetOnAxis(ap=tail_row[:, e:e + 1], axis=0),
                    in_=pad[:, :], in_offset=None).then_inc(padded, 16)
            with pool.Fori(0, STEPS // RING) as i:
                def send(s):
                    pool.wait_ge(normed.sem, normed.at(i, s + 1))
                    hold(pool, held_pool)
                    nc.gpsimd.indirect_dma_start(
                        out=out, out_offset=bass.IndirectOffsetOnAxis(ap=home[:, s % 2:s % 2 + 1], axis=0),
                        in_=y[:, s % 2, :], in_offset=None, bounds_check=TOKENS - 1, oob_is_err=False)\
                        .then_inc(sent[s % 2].sem, 16)

                for s in range(RING):
                    pool.wait_ge(var_ready.sem, var_ready.at(i, s + 1))
                    nc.gpsimd.tensor_tensor(rstd[:, s % 2:s % 2 + 1], var_eps[:, s % 2:s % 2 + 1], half_neg[:, :],
                                            ALU.pow).then_inc(rstd_ready.sem, 1)
                    send(s)
            for s in range(2):
                pool.wait_ge(sent[s].sem, sent[s].at(STEPS // RING, 0))

        @block.scalar
        def _(act):
            for e in range(EXPERTS):
                act.wait_ge(raw_in[e % 2], 16 * (e // 2 + 1))
                nc.scalar.activation(weight[:, HI, e * KT * D:(e + 1) * KT * D], w_raw[:, e % 2, :], ACT.Copy)\
                    .then_inc(high_done, 1)
            with act.Fori(0, STEPS // RING) as i:
                for s in range(RING):
                    act.wait_ge(turned.sem, turned.at(i, s + 1))
                    if s < 2:
                        act.wait_ge(y_full.sem, y_full.at(i, 0))
                    else:
                        act.wait_ge(y_full.sem, y_full.at(i, s - 1))
                    nc.scalar.activation(xt[:, s % 2, HI, :], xt_ps[s % 2][:, :], ACT.Copy).then_inc(xt_high.sem, 1)

        @block.vector
        def _(dve):
            step = 0

            def link(ins):
                nonlocal step
                step += 1
                ins.then_inc(plan_step, 1)
                dve.wait_ge(plan_step, step)

            dve.wait_ge(consts, 1)
            link(nc.vector.tensor_tensor(tail[:, :], region_end[:, :], lane[:, :], ALU.add))
            nc.vector.tensor_copy(tail_row[:, :], tail[:, :]).then_inc(tail_ready, 1)
            link(nc.vector.tensor_tensor(count[:, :], region_end[:, :], first[:, :], ALU.subtract))
            wide = [P, EXPERTS, TOKENS // P]
            link(nc.vector.tensor_tensor(more[:, :, :], count[:, :].unsqueeze(2).to_broadcast(wide),
                                         tile_rows[:, :].unsqueeze(1).to_broadcast(wide), ALU.is_gt))
            link(nc.vector.tensor_reduce(tiles[:, :], more[:, :, :], AX.X, ALU.add))
            link(nc.vector.tensor_copy(end[:, 0:1], tiles[:, 0:1]))
            for e in range(1, EXPERTS):
                link(nc.vector.tensor_tensor(end[:, e:e + 1], end[:, e - 1:e], tiles[:, e:e + 1], ALU.add))
            wide = [P, TABLE, EXPERTS]
            per_expert = lambda a: a.unsqueeze(1).to_broadcast(wide)
            link(nc.vector.tensor_tensor(passed[:, :, :], tile_no[:, :].unsqueeze(2).to_broadcast(wide),
                                         per_expert(end[:, :]), ALU.is_ge))
            link(nc.vector.tensor_reduce(expert_f[:, :], passed[:, :, :], AX.X, ALU.add))
            link(nc.vector.tensor_tensor(scaled[:, :, :], passed[:, :, :], per_expert(tiles[:, :]), ALU.mult))
            link(nc.vector.tensor_reduce(work[:, 0, :], scaled[:, :, :], AX.X, ALU.add))
            link(nc.vector.tensor_tensor(work[:, 1, :], tile_no[:, :], work[:, 0, :], ALU.subtract))
            link(nc.vector.tensor_scalar(work[:, 1, :], work[:, 1, :], float(P), None, ALU.mult))
            link(nc.vector.scalar_tensor_tensor(out=start_f[:, :], in0=expert_f[:, :], scalar=float(REGION),
                                                in1=work[:, 1, :], op0=ALU.mult, op1=ALU.add))
            link(nc.vector.tensor_scalar(start_f[:, :], start_f[:, :], float(SPARE), None, ALU.min))
            link(nc.vector.tensor_scalar(expert_f[:, :], expert_f[:, :], float(EXPERTS - 1), None, ALU.min))
            nc.vector.tensor_copy(start[:, :], start_f[:, :]).then_inc(table_ready, 1)
            nc.vector.tensor_copy(expert[:, :], expert_f[:, :]).then_inc(table_ready, 1)
            for e in range(EXPERTS):
                dve.wait_ge(high_done, e + 1)
                nc.vector.tensor_tensor(weight[:, LO, e * KT * D:(e + 1) * KT * D], w_raw[:, e % 2, :],
                                        weight[:, HI, e * KT * D:(e + 1) * KT * D].bitcast(F32), ALU.subtract)\
                    .then_inc(low_done, 1)
            dve.wait_ge(bias_in, 16)
            dve.wait_ge(table_ready, 2)
            with dve.Fori(0, STEPS // RING) as i:
                def low(s):
                    dve.wait_ge(xt_high.sem, xt_high.at(i, s + 1))
                    nc.vector.tensor_tensor(xt[:, s % 2, LO, :], xt_ps[s % 2][:, :], xt[:, s % 2, HI, :].bitcast(F32),
                                            ALU.subtract).then_inc(xt_low.sem, 1)

                def stage(s):
                    e = dve.value_load(expert[0:1, bass.ds(i * RING + s, 1)], min_val=0, max_val=EXPERTS - 1)
                    slot = s % 2
                    dve.wait_ge(y_full.sem, y_full.at(i, s + 1))
                    for other in (sent[slot],):
                        dve.wait_ge(other.sem, other.at(i, 16 * (s // 2)))
                    nc.vector.tensor_tensor(y[:, slot, :], y_ps[slot][:, :], bias[:, bass.ds(e * D, D)], ALU.add)\
                        .then_inc(y_free.sem, 1)
                    dve.wait_ge(y_free.sem, y_free.at(i, s + 1))
                    nc.vector.scalar_tensor_tensor(out=y[:, slot, :], in0=y[:, slot, :], scalar=got[:, s, W_COL:W_COL + 1],
                                                   in1=got[:, s, 0:D], op0=ALU.mult, op1=ALU.add).then_inc(row_step.sem, 1)
                    dve.wait_ge(row_step.sem, row_step.at(i, 3 * s + 1))
                    nc.vector.bn_stats(stats[:, slot, :], y[:, slot, :]).then_inc(row_step.sem, 1)
                    dve.wait_ge(row_step.sem, row_step.at(i, 3 * s + 2))
                    hold(dve, held_dve)
                    nc.vector.tensor_copy(home[:, slot:slot + 1], got[:, s, ID_COL:ROW])
                    nc.vector.bn_aggr(mv[:, slot, :], stats[:, slot, :]).then_inc(row_step.sem, 1)
                    dve.wait_ge(row_step.sem, row_step.at(i, 3 * s + 3))
                    nc.vector.tensor_scalar(var_eps[:, slot:slot + 1], mv[:, slot, 1:2], EPS, None, ALU.add)\
                        .then_inc(var_ready.sem, 1)

                def norm(s):
                    slot = s % 2
                    dve.wait_ge(rstd_ready.sem, rstd_ready.at(i, s + 1))
                    nc.vector.tensor_scalar(y[:, slot, :], y[:, slot, :], mv[:, slot, 0:1], rstd[:, slot:slot + 1],
                                            ALU.subtract, ALU.mult).then_inc(normed.sem, 1)

                for s in range(RING):
                    low(s)
                    if s:
                        norm(s - 1)
                    stage(s)
                norm(RING - 1)

        @block.tensor
        def _(pe):
            pe.wait_ge(consts, 1)
            pe.wait_ge(high_done, EXPERTS)
            pe.wait_ge(low_done, EXPERTS)
            pe.wait_ge(table_ready, 2)
            with pe.Fori(0, STEPS // RING) as i:
                def turn(s):
                    pe.wait_ge(got_in[s].sem, got_in[s].at(i, 16))
                    if s < 2:
                        pe.wait_ge(xt_low.sem, xt_low.at(i, 0))
                    else:
                        pe.wait_ge(xt_low.sem, xt_low.at(i, s - 1))
                    for k in range(KT):
                        mm = nc.tensor.transpose(xt_ps[s % 2][:, k * P:(k + 1) * P], got[:, s, k * P:(k + 1) * P],
                                                 ident[:, :])
                    mm.then_inc(turned.sem, 1)

                def multiply(s):
                    e = pe.value_load(expert[0:1, bass.ds(i * RING + s, 1)], min_val=0, max_val=EXPERTS - 1)
                    pe.wait_ge(xt_low.sem, xt_low.at(i, s + 1))
                    if s < 2:
                        pe.wait_ge(y_free.sem, y_free.at(i, 0))
                    else:
                        pe.wait_ge(y_free.sem, y_free.at(i, s - 1))
                    for c in range(3 * KT):
                        k, (xs, ws) = c // 3, MM3[c % 3]
                        mm = nc.tensor.matmul(y_ps[s % 2][:, :], xt[:, s % 2, xs, k * P:(k + 1) * P],
                                              weight[:, ws, bass.ds(e * (KT * D) + k * D, D)],
                                              start=c == 0, stop=c == 3 * KT - 1)
                    mm.then_inc(y_full.sem, 1)

                turn(0)
                for s in range(RING):
                    if s + 1 < RING:
                        turn(s + 1)
                    multiply(s)


def run(nc, x_t, x_rows, wq_t, wk_t, wv_t, wo_t, router_w_t, router_b, expert_w_t, expert_b, out=None):
    w_qk_parts = nc.dram_tensor("w_qk_parts", [UNITS, 2, P, 2 * KT * P], F32).ap()
    w_vo_parts = nc.dram_tensor("w_vo_parts", [2, P, 2 * KT * D], F32).ap()
    dispatched = nc.dram_tensor("dispatched", [SPARE + P, ROW], F32).ap()
    unread = nc.dram_tensor("unread", [2 * P, ROW], F32).ap()
    with ExitStack() as ctx:
        region_end = ctx.enter_context(nc.sbuf_tensor("region_end", [P, EXPERTS], F32))
        split_weights(nc, w_qk_parts, w_vo_parts, wq_t, wk_t, wv_t, wo_t)
        attend(nc, region_end, x_t, x_rows, router_w_t, router_b, w_qk_parts, w_vo_parts, dispatched)
        if out is not None:
            run_experts(nc, region_end, expert_w_t, expert_b, dispatched, unread, out)


def kernel(**inputs):
    import numpy as np
    import concourse.bacc as bacc
    from concourse.bass_utils import run_bass_kernel_spmd

    x = np.asarray(inputs["L0_attn_x"])
    rows = x.reshape(TOKENS, D)
    laid_out = {
        "x_t": rows.T,
        "x_rows": rows,
        "wq_t": np.asarray(inputs["L0_attn_W_Q"]).T,
        "wk_t": np.asarray(inputs["L0_attn_W_K"]).T,
        "wv_t": np.asarray(inputs["L0_attn_W_V"]).T,
        "wo_t": np.asarray(inputs["L0_attn_W_O"]).T,
        "router_w_t": np.asarray(inputs["L0_ffn_router_w"]).T,
        "router_b": np.asarray(inputs["L0_ffn_router_b"]),
        "expert_w_t": np.asarray(inputs["L0_ffn_expert_w"]).transpose(0, 2, 1),
        "expert_b": np.asarray(inputs["L0_ffn_expert_b"]),
    }
    laid_out = {name: np.ascontiguousarray(a) for name, a in laid_out.items()}
    nc = bacc.Bacc("TRN2", target_bir_lowering=False, num_devices=1)
    aps = {name: nc.dram_tensor(name, a.shape, mybir.dt.from_np(a.dtype), kind="ExternalInput").ap()
           for name, a in laid_out.items()}
    out = nc.dram_tensor("out", [TOKENS, D], F32, kind="ExternalOutput").ap()
    run(nc, out=out, **aps)
    result = run_bass_kernel_spmd(nc, [laid_out], core_ids=[0])
    return result.results[0]["out"].reshape(BATCHES, SEQ, D)
```

```python
from contextlib import ExitStack

import concourse.bass as bass
from concourse import mybir

F32 = mybir.dt.float32
F32R = mybir.dt.float32r
BF16 = mybir.dt.bfloat16
I32 = mybir.dt.int32
U32 = mybir.dt.uint32
ALU = mybir.AluOpType
ACT = mybir.ActivationFunctionType
AX = mybir.AxisListType

P = 128
BATCHES, SEQ, D = 8, 1024, 512
HEADS, DH = 16, 32
EXPERTS = 8
KT = D // P
UNITS = HEADS // 4
BANK = 512
HALVES = SEQ // BANK
ROWT = SEQ // P
TOKENS = BATCHES * SEQ
SCALE = float(DH) ** -0.5
EPS = 1e-5
MASKED = -1e30
HI, LO = 0, 1
SETS = 3
WO_SET, WV_SET = 1, 2
Q, K = 0, 1

ROW = D + 2
W_COL, ID_COL = D, D + 1
REGION = TOKENS + P
SPARE = EXPERTS * REGION
NO_TOKEN = TOKENS + P
TILES = TOKENS // P + EXPERTS
MM3 = ((HI, HI), (HI, LO), (LO, HI))


class Signal:

    def __init__(self, ctx, nc, name, per, first, before=0):
        self.sem, self.per = ctx.enter_context(nc.semaphore(name)), per
        self.first, self.before = first, before

    def at(self, loop, count):
        assert count + self.before + self.first > 0
        return loop * self.per + (count + self.before + self.first)

    def early(self, count):
        assert 0 < count <= self.before
        return count + self.first


def hold(eng, passed):
    eng.sem_inc(passed, 1)


def split_weights(nc, w_qk_parts, w_vo_parts, wq_t, wk_t, wv_t, wo_t):
    with ExitStack() as ctx:
        raw = [ctx.enter_context(nc.sbuf_tensor(f"w_raw{i}", [P, KT * D], F32)) for i in range(4)]
        both = ctx.enter_context(nc.sbuf_tensor("w_both", [P, 4, 2, KT * D], F32R))
        raw_in = [ctx.enter_context(nc.semaphore(f"w_raw_in{i}")) for i in range(4)]
        high_done = ctx.enter_context(nc.semaphore("w_high_done"))
        low_done = ctx.enter_context(nc.semaphore("w_low_done"))
        parts_out = ctx.enter_context(nc.semaphore("w_parts_out"))
        block = ctx.enter_context(nc.Block())

        @block.sync
        def _(sp):
            for i, w in enumerate((wq_t, wk_t, wv_t, wo_t)):
                sp.dma_start(raw[i][:, :].rearrange("p (k n) -> p k n", k=KT),
                             w.rearrange("(k p) n -> p k n", p=P)).then_inc(raw_in[i], 16)
            sp.wait_ge(high_done, 4)
            sp.wait_ge(low_done, 4)
            for i in range(2):
                for u in range(UNITS):
                    src = both[:, i].rearrange("p c (k n) -> p (c k) n", n=D)[:, :, u * P:(u + 1) * P]
                    sp.dma_start(w_qk_parts[u, i].rearrange("p (c n) -> p c n", n=P), src.bitcast(F32))\
                        .then_inc(parts_out, 16)
                sp.dma_start(w_vo_parts[i], both[:, 2 + i].rearrange("p c n -> p (c n)").bitcast(F32))\
                    .then_inc(parts_out, 16)
            sp.wait_ge(parts_out, 2 * (UNITS + 1) * 16)

        @block.scalar
        def _(act):
            for i in range(4):
                act.wait_ge(raw_in[i], 16)
                nc.scalar.activation(both[:, i, HI], raw[i][:, :], ACT.Copy).then_inc(high_done, 1)

        @block.vector
        def _(dve):
            for i in range(4):
                dve.wait_ge(high_done, i + 1)
                nc.vector.tensor_tensor(both[:, i, LO], raw[i][:, :], both[:, i, HI].bitcast(F32),
                                        ALU.subtract).then_inc(low_done, 1)


def attend(nc, region_end, x_t, x_rows, router_w_t, router_b, w_qk_parts, w_vo, dispatched):
    with ExitStack() as ctx:
        def sb(name, shape, dt=F32):
            return ctx.enter_context(nc.sbuf_tensor(name, shape, dt))

        def sem(name):
            return ctx.enter_context(nc.semaphore(name))

        starting = []

        def signal(name, per, before=0, dma=False):
            starting.append(Signal(ctx, nc, name, per, 16 if dma else 1, before))
            return starting[-1]

        xt = sb("xt", [P, 2, KT, SEQ], F32R)
        xt_raw = sb("xt_raw", [P, 2, SEQ])
        w_qk = sb("w_qk", [P, 2, 2, KT, P], F32R)
        q_st = [sb(f"q_stack{s}", [P, 4, SEQ], F32R) for s in range(SETS)]
        k_st = [sb(f"k_stack{s}", [P, 4, SEQ], F32R) for s in range(SETS)]
        v = sb("v", [P, ROWT, D])
        parts = sb("parts", [P, 2, 2, BANK], F32R)
        probs = sb("probs", [P, 8, BANK])
        rows = sb("rows", [P, ROWT, ROW])
        x_in = xt_raw[:, :, 0:D]
        sums = sb("sums", [P, BANK])
        tile_max = sb("tile_max", [P, 2, 4, ROWT])
        row_max = sb("row_max", [P, 4 * ROWT])
        neg_max = sb("neg_max", [4 * ROWT, P], F32R)
        ident = sb("ident", [P, P])
        ident_b = sb("ident_b", [P, P], BF16)
        mask_qk = sb("mask_qk", [P, P], BF16)
        mask_kq = sb("mask_kq", [P, P], BF16)
        before_b = sb("before_b", [P, P], BF16)
        ones_b = sb("ones_b", [P, P], BF16)
        ones_f = sb("ones_f", [P, DH])
        rw = sb("rw", [P, KT, EXPERTS])
        rb = sb("rb", [P, EXPERTS])
        stats = sb("stats", [P, ROWT, 6])
        mv = sb("mv", [P, ROWT, 2])
        var_eps = sb("var_eps", [P, ROWT])
        half_neg = sb("half_neg", [P, ROWT])
        rstd = sb("rstd", [P, ROWT])
        token = sb("token", [P, ROWT])
        logit = sb("logit", [P, ROWT, EXPERTS])
        expo = sb("expo", [P, ROWT, EXPERTS])
        pick = sb("pick", [P, ROWT, EXPERTS])
        onehot = sb("onehot", [P, ROWT, EXPERTS], BF16)
        order = sb("order", [P, EXPERTS])
        base = sb("base", [P, ROWT, EXPERTS])
        small = sb("small", [P, 4, ROWT])
        dest = sb("dest", [P, ROWT], U32)

        proj = [ctx.enter_context(nc.psum_tensor(f"proj{i}", [P, BANK], F32)) for i in range(2)]
        maxp = [ctx.enter_context(nc.psum_tensor(f"maxp{i}", [P, BANK], F32)) for i in range(2)]
        score = [ctx.enter_context(nc.psum_tensor(f"score{i}", [P, BANK], F32)) for i in range(2)]
        y_ps = ctx.enter_context(nc.psum_tensor("y_ps", [P, BANK], F32))
        den_ps = ctx.enter_context(nc.psum_tensor("den_ps", [P, BANK], F32))
        logit_ps = y_ps[:, 0:ROWT * EXPERTS].rearrange("p (t e) -> p t e", e=EXPERTS)
        rank_ps = den_ps[:, 0:ROWT * EXPERTS].rearrange("p (t e) -> p t e", e=EXPERTS)
        total_ps = den_ps[:, 64:64 + ROWT * EXPERTS].rearrange("p (t e) -> p t e", e=EXPERTS)

        NPROJ = UNITS * 2 * HALVES
        SP_BLOCKS = 2
        V_AHEAD = ROWT // 2
        JOBS = NPROJ + ROWT + UNITS + ROWT + ROWT
        AHEAD = 4 + V_AHEAD
        MTILES = 4 * sum(1 + (t * P >= BANK) for t in range(ROWT))
        STILES = MTILES
        GROUPS = STILES // 4
        HALF0 = BANK // P
        setup_dma = sem("setup_dma")
        w_in = [signal(f"w_in{o}", UNITS * 16, 32, dma=True) for o in range(2)]
        setup_done = sem("setup_done")
        setup_step = sem("setup_step")
        held_sp, held_pool, held_dve = sem("held_sp"), sem("held_pool"), sem("held_dve")
        xt_in = [signal(f"xt_in{i}", 2 * 16, 32, dma=True) for i in range(2)]
        xt_high = signal("xt_high", KT, KT)
        xt_low = signal("xt_low", KT, KT)
        proj_full = [signal(f"proj_full{i}", JOBS // 2, AHEAD // 2) for i in range(2)]
        proj_free = [signal(f"proj_free{i}", JOBS // 2, AHEAD // 2) for i in range(2)]
        part_high = signal("part_high", NPROJ, 4)
        SP_GAIN, POOL_GAIN = 4 * SP_BLOCKS * 16, 4 * (3 - SP_BLOCKS) * 16
        sp_in = [signal(f"sp_in{i}", UNITS * 2 * SP_GAIN, 2 * SP_GAIN, dma=True) for i in range(2)]
        pool_in = [Signal(ctx, nc, f"pool_in{i}", UNITS * 2 * POOL_GAIN, 0, 2 * POOL_GAIN) for i in range(2)]
        max_full = signal("max_full", UNITS * MTILES)
        max_free = [signal(f"max_free{i}", UNITS * MTILES // 2) for i in range(2)]
        max_step = signal("max_step", UNITS)
        max_ready = signal("max_ready", UNITS)
        neg_in = signal("neg_in", UNITS * 16, dma=True)
        score_full = signal("score_full", UNITS * STILES)
        exp_done = signal("exp_done", UNITS * STILES)
        probs_used = signal("probs_used", UNITS * GROUPS)
        y_copied = signal("y_copied", UNITS * HALVES)
        sums_copied = signal("sums_copied", UNITS * HALVES)
        recip_done = signal("recip_done", UNITS * HALVES)
        y_ready = signal("y_ready", UNITS * HALVES)
        wo_in = signal("wo_in", 16, dma=True)
        wv_in = signal("wv_in", 16, dma=True)
        y_high = signal("y_high", ROWT)
        y_low = signal("y_low", ROWT)
        x_in_dma = [signal(f"x_in_dma{i}", ROWT // 2 * 16, dma=True) for i in range(2)]
        norm_step = signal("norm_step", 2 * ROWT + 1)
        var_ready = signal("var_ready", 1)
        rstd_ready = signal("rstd_ready", 1)
        normed = signal("normed", ROWT)
        logits_done = signal("logits_done", ROWT)
        ROUTE_STEPS = 11 + ROWT
        route_step = signal("route_step", ROUTE_STEPS)
        shifted = signal("shifted", 1)
        exp_route = signal("exp_route", 1)
        onehot_ready = signal("onehot_ready", 1)
        ranks_done = signal("ranks_done", 1)
        dest_ready = signal("dest_ready", 1)
        scattered = Signal(ctx, nc, "scattered", ROWT * 16, 16)

        OPENING = [("p", 1, 0), ("v", 4), ("p", 1, 1), ("v", 5), ("p", 1, 2), ("v", 6), ("p", 1, 3), ("v", 7)]
        AHEAD_JOBS = [("p", 0, i) for i in range(4)] + [("v", i) for i in range(V_AHEAD)]
        job_names = OPENING + [("m", 0)]
        for u in range(1, UNITS):
            job_names += [("p", u + 1, i) for i in range(4)] * (u + 1 < UNITS) + [("m", u)]
        job_names += [("v", 0), ("v", 1)] + [("o", i) for i in range(ROWT)] + [("p", 0, i) for i in range(4)]
        job_names += [("x", i) for i in range(ROWT)] + [("v", 2), ("v", 3)]
        assert len(job_names) == JOBS and JOBS % 2 == 0 and AHEAD % 2 == 0 and len(AHEAD_JOBS) == AHEAD

        def place_of(b, name):
            n = AHEAD_JOBS.index(name) if b is None else job_names.index(name)
            return n % 2, n // 2

        def wait_job(eng, b, sems, name):
            bank, n = place_of(b, name)
            s = sems[bank]
            eng.wait_ge(s.sem, s.early(n + 1) if b is None else s.at(b, n + 1))
            return proj[bank]

        def wait_last_batch(eng, b, sems):
            for s in sems:
                eng.wait_ge(s.sem, s.at(b, 0))

        def weighed(eng, b, n):
            eng.wait_ge(probs_used.sem, probs_used.at(b, n))

        def tile_turn(b, u):
            return 0 if b is None else (u - 1) % UNITS

        def stacked(eng, b, slot, tiles):
            for s, gain in ((sp_in[slot], SP_GAIN), (pool_in[slot], POOL_GAIN)):
                eng.wait_ge(s.sem, s.early(tiles * gain) if b is None else s.at(b, tiles * gain))

        def column(kb, t):
            return max(kb * P - t * BANK, 0)

        def pieces(j):
            return range(2 * j, 2 * j + 2) if j < 6 else ()

        def tiles_made(j):
            return [p // 3 for p in pieces(j) if p % 3 == 2]

        def maxima(j):
            return range(6 * (j - 2), 6 * (j - 1)) if 2 <= j < 10 else ()

        SCORE_GROUPS = [(t, kb) for t in range(HALVES) for kb in range((t + 1) * BANK // P)]
        MAX_TILES = []
        for qb in range(ROWT):
            for h in range(4):
                for j in range(1 + (qb * P >= BANK)):
                    cols = min((qb + 1) * P - j * BANK, BANK)
                    diag = qb * P - j * BANK if j * BANK <= qb * P < (j + 1) * BANK else None
                    MAX_TILES.append((qb, h, j, cols, max(cols, 256), diag))
        assert len(MAX_TILES) == MTILES and len(SCORE_GROUPS) == GROUPS

        block = ctx.enter_context(nc.Block())

        def send_tile(eng, b, u, o, t, blocks, done, held):
            wait_job(eng, b, proj_free, ("p", u, 2 * o + t))
            if b is not None:
                hold(eng, held)
            dst = (q_st, k_st)[o][u % SETS]
            for block_row in blocks:
                part = ((HI, HI, LO), (HI, LO, HI))[o][block_row]
                for h in range(4):
                    eng.dma_start(dst[DH * block_row:DH * (block_row + 1), h, t * BANK:(t + 1) * BANK].bitcast(F32),
                                  parts[DH * h:DH * (h + 1), t, part, :].bitcast(F32)).then_inc(done[t].sem, 16)

        @block.sync
        def _(sp):
            for s in starting:
                sp.sem_inc(s.sem, s.first)

            def load_w(u, o):
                sp.dma_start(w_qk[:, o].rearrange("p c k n -> p (c k n)").bitcast(F32), w_qk_parts[u, o])\
                    .then_inc(w_in[o].sem, 16)

            def load_xt(batch, k):
                sp.dma_start(xt_raw[:, k % 2, :], x_t[k * P:(k + 1) * P, bass.ds(batch * SEQ, SEQ)])\
                    .then_inc(xt_in[k % 2].sem, 16)

            def load_wv(done):
                sp.dma_start(q_st[WV_SET][:, :, :].rearrange("p h n -> p (h n)").bitcast(F32), w_vo[0]).then_inc(done, 16)

            def send(b, u):
                for o in (Q, K):
                    for t in range(HALVES):
                        send_tile(sp, b, u, o, t, range(SP_BLOCKS), sp_in, held_sp)
                    load_w((u + 1) % UNITS, o)

            for k in range(2):
                load_xt(0, k)
            load_w(0, Q)
            load_w(0, K)
            load_wv(setup_dma)
            sp.dma_start(rw[:, :, :], router_w_t.rearrange("(k p) e -> p k e", p=P)).then_inc(setup_dma, 16)
            sp.dma_start(rb[:, :], router_b.partition_broadcast(P)).then_inc(setup_dma, 16)
            for k in range(2, KT):
                sp.wait_ge(xt_high.sem, xt_high.early(k - 1))
                sp.wait_ge(xt_low.sem, xt_low.early(k - 1))
                load_xt(0, k)
            send(None, 0)

            with sp.Fori(0, BATCHES) as b:
                def load_x(tb):
                    hold(sp, held_sp)
                    sp.dma_start(x_in[:, tb % 2, :], x_rows[bass.ds(b * SEQ + tb * P, P), :])\
                        .then_inc(x_in_dma[tb % 2].sem, 16)

                wait_last_batch(sp, b, proj_full)
                hold(sp, held_sp)
                send(b, 1)
                hold(sp, held_sp)
                wait_last_batch(sp, b, proj_free)
                hold(sp, held_sp)
                for k in range(2):
                    load_xt((b + 1) % BATCHES, k)
                wait_job(sp, b, proj_full, ("v", 6))
                hold(sp, held_sp)
                wait_job(sp, b, proj_full, ("v", 7))
                hold(sp, held_sp)
                send(b, 2)
                hold(sp, held_sp)
                weighed(sp, b, GROUPS)
                hold(sp, held_sp)
                send(b, 3)
                hold(sp, held_sp)
                weighed(sp, b, GROUPS * 2)
                sp.dma_start(q_st[WO_SET][:, :, :].rearrange("p h n -> p (h n)").bitcast(F32), w_vo[1]).then_inc(wo_in.sem, 16)
                for k in range(2, KT):
                    hold(sp, held_sp)
                    sp.wait_ge(xt_high.sem, xt_high.at(b, k - 1))
                    hold(sp, held_sp)
                    sp.wait_ge(xt_low.sem, xt_low.at(b, k - 1))
                    hold(sp, held_sp)
                    load_xt((b + 1) % BATCHES, k)
                weighed(sp, b, GROUPS * 3)
                load_wv(wv_in.sem)
                hold(sp, held_sp)
                sp.wait_ge(xt_high.sem, xt_high.at(b, KT))
                hold(sp, held_sp)
                sp.wait_ge(xt_low.sem, xt_low.at(b, KT))
                load_x(0)
                load_x(1)
                for tb in range(2, ROWT):
                    wait_job(sp, b, proj_free, ("o", tb - 2))
                    load_x(tb)
                send(b, 0)
            wait_last_batch(sp, BATCHES, w_in)

        @block.gpsimd
        def _(pool):
            step = 0

            def link(ins):
                nonlocal step
                step += 1
                ins.then_inc(setup_step, 1)
                pool.wait_ge(setup_step, step)

            def split_low(k, count):
                pool.wait_ge(xt_high.sem, count)
                nc.gpsimd.tensor_tensor(xt[:, LO, k, :], xt_raw[:, k % 2, :], xt[:, HI, k, :].bitcast(F32),
                                        ALU.subtract).then_inc(xt_low.sem, 1)

            link(nc.gpsimd.memset(ident[:, :], 0.0))
            for k in range(2):
                split_low(k, xt_high.early(k + 1))
            link(nc.gpsimd.memset(ones_b[:, :], 1.0))
            link(nc.gpsimd.memset(ones_f[:, :], 1.0))
            link(nc.gpsimd.memset(mask_qk[:, :], MASKED))
            link(nc.gpsimd.memset(mask_kq[:, :], MASKED))
            link(nc.gpsimd.memset(half_neg[:, :], -0.5))
            for k in range(2, KT):
                split_low(k, xt_high.early(k + 1))
            link(nc.gpsimd.affine_select(out=ident[:, :], in_=ident[:, :], compare_op=ALU.not_equal, fill=1.0,
                                         base=0, pattern=[[-1, P]], channel_multiplier=1))
            link(nc.gpsimd.tensor_copy(ident_b[:, :], ident[:, :]))
            link(nc.gpsimd.affine_select(out=mask_qk[:, :], in_=mask_qk[:, :], compare_op=ALU.is_gt, fill=0.0,
                                         base=0, pattern=[[1, P]], channel_multiplier=-1))
            link(nc.gpsimd.affine_select(out=mask_kq[:, :], in_=mask_kq[:, :], compare_op=ALU.is_gt, fill=0.0,
                                         base=0, pattern=[[-1, P]], channel_multiplier=1))
            link(nc.gpsimd.affine_select(out=before_b[:, :], in_=ones_b[:, :], compare_op=ALU.is_gt, fill=0.0,
                                         base=0, pattern=[[1, P]], channel_multiplier=-1))
            loose = dict(allow_small_or_imprecise_dtypes=True)
            link(nc.gpsimd.iota(order[:, :], [[-1, EXPERTS]], base=EXPERTS, channel_multiplier=0, **loose))
            link(nc.gpsimd.iota(token[:, :], [[P, ROWT]], base=0, channel_multiplier=1, **loose))
            link(nc.gpsimd.iota(region_end[:, :], [[REGION, EXPERTS]], base=0, channel_multiplier=0, **loose))
            for s in range(SETS):
                link(nc.gpsimd.memset(k_st[s][3 * DH:3 * DH + 1, :, :].bitcast(F32), 1.0))
            link(nc.gpsimd.memset(rows[:, 0, 0:ID_COL], 0.0))
            link(nc.gpsimd.memset(rows[:, 0, ID_COL:ROW], float(NO_TOKEN)))
            nc.gpsimd.dma_start(dispatched[SPARE:SPARE + P, :], rows[:, 0, :]).then_inc(scattered.sem, 16)
            nc.gpsimd.memset(small[:, :, :], 0.0).then_inc(setup_done, 1)

            def send(b, u):
                for o in (Q, K):
                    for t in range(HALVES):
                        send_tile(pool, b, u, o, t, range(SP_BLOCKS, 3), pool_in, held_pool)

            send(None, 0)
            with pool.Fori(0, BATCHES) as b:
                wait_last_batch(pool, b, proj_full)
                hold(pool, held_pool)
                send(b, 1)
                wait_job(pool, b, proj_full, ("v", 6))
                hold(pool, held_pool)
                wait_job(pool, b, proj_full, ("v", 7))
                hold(pool, held_pool)
                send(b, 2)
                hold(pool, held_pool)
                weighed(pool, b, GROUPS)
                hold(pool, held_pool)
                send(b, 3)
                for k in range(KT):
                    split_low(k, xt_high.at(b, k + 1))
                for tb in range(ROWT):
                    pool.wait_ge(y_high.sem, y_high.at(b, tb + 1))
                    nc.gpsimd.tensor_tensor(parts[:, tb % 2, LO, :], rows[:, tb, 0:D],
                                            parts[:, tb % 2, HI, :].bitcast(F32), ALU.subtract)\
                        .then_inc(y_low.sem, 1)
                pool.wait_ge(var_ready.sem, var_ready.at(b, 1))
                nc.gpsimd.tensor_tensor(rstd[:, :], var_eps[:, :], half_neg[:, :], ALU.pow).then_inc(rstd_ready.sem, 1)
                send(b, 0)
                pool.wait_ge(dest_ready.sem, dest_ready.at(b, 1))
                hold(pool, held_pool)
                for tb in range(ROWT):
                    nc.gpsimd.indirect_dma_start(
                        out=dispatched, out_offset=bass.IndirectOffsetOnAxis(ap=dest[:, tb:tb + 1], axis=0),
                        in_=rows[:, tb, :], in_offset=None).then_inc(scattered.sem, 16)
            pool.wait_ge(scattered.sem, scattered.at(BATCHES, 0))

        @block.scalar
        def _(act):
            def split_high(k, count):
                act.wait_ge(xt_in[k % 2].sem, count)
                nc.scalar.activation(xt[:, HI, k, :], xt_raw[:, k % 2, :], ACT.Copy).then_inc(xt_high.sem, 1)

            def free_of(b, name):
                return proj_free[place_of(b, name)[0]].sem

            def high(b, u, i):
                o, t = divmod(i, HALVES)
                bank = wait_job(act, b, proj_full, ("p", u, i))
                if b is not None or o == K:
                    stacked(act, b, t, 2 * tile_turn(b, u) + o)
                nc.scalar.activation(parts[:, t, HI, :], bank[:, :], ACT.Copy).then_inc(part_high.sem, 1)

            def take_v(b, tb):
                bank = wait_job(act, b, proj_full, ("v", tb))
                nc.scalar.activation(v[:, tb, :], bank[:, :], ACT.Copy).then_inc(free_of(b, ("v", tb)), 1)

            for k in range(KT):
                split_high(k, xt_in[k % 2].early(16 * (k // 2 + 1)))
            for i in range(4):
                high(None, 0, i)
            for tb in range(V_AHEAD):
                take_v(None, tb)

            with act.Fori(0, BATCHES) as b:
                def negate(u):
                    bank = wait_job(act, b, proj_full, ("m", u))
                    act.wait_ge(neg_in.sem, neg_in.at(b, 16 * u))
                    nc.scalar.activation(neg_max[:, :], bank[0:4 * ROWT, 0:P], ACT.Copy, scale=-1.0)\
                        .then_inc(free_of(b, ("m", u)), 1)
                    wait_job(act, b, proj_free, ("m", u))
                    act.dma_start(q_st[u % SETS][3 * DH:3 * DH + 1, :, :].rearrange("p h (t c) -> p (h t) c", c=P).bitcast(F32),
                                  neg_max[:, :].bitcast(F32)).then_inc(neg_in.sem, 16)

                def copy_sums(n):
                    weighed(act, b, GROUPS * (n // HALVES) + (HALF0 if n % HALVES == 0 else GROUPS))
                    act.wait_ge(y_ready.sem, y_ready.at(b, n))
                    nc.scalar.activation(sums[:, :], den_ps[:, :], ACT.Copy).then_inc(sums_copied.sem, 1)

                for name in OPENING:
                    if name[0] == "p":
                        high(b, 1, name[2])
                    else:
                        take_v(b, name[1])
                negate(0)
                act.wait_ge(logits_done.sem, logits_done.at(b, 0))
                for u in range(UNITS):
                    for j, (t, kb) in enumerate(SCORE_GROUPS):
                        if u and j == 0:
                            copy_sums(2 * u - 1)
                        if u == 2 and j in (1, 3, 5, 7):
                            if j == 1:
                                wait_job(act, b, proj_full, ("p", 3, 2))
                                wait_job(act, b, proj_full, ("p", 3, 3))
                            k = j // 2
                            split_high(k, xt_in[k % 2].at(b, 16 * (k // 2 + 1)))
                        n = GROUPS * u + j
                        if n >= 2:
                            weighed(act, b, n - 1)
                        for h in range(4):
                            c = column(kb, t)
                            act.wait_ge(score_full.sem, score_full.at(b, 4 * n + h + 1))
                            nc.scalar.activation(probs[:, 4 * (n % 2) + h, c:BANK], score[h % 2][:, c:BANK],
                                                 ACT.Exp, scale=SCALE).then_inc(exp_done.sem, 1)
                        if u + 2 < UNITS:
                            for i in tiles_made(j):
                                high(b, u + 2, i)
                        if j == HALF0:
                            copy_sums(2 * u)
                        if u + 1 < UNITS and j == 10:
                            negate(u + 1)
                copy_sums(2 * UNITS - 1)
                take_v(b, 0)
                take_v(b, 1)
                act.wait_ge(y_ready.sem, y_ready.at(b, UNITS * HALVES))
                for s in range(2):
                    stacked(act, b, s, 6)
                for tb in range(ROWT):
                    if tb >= 2:
                        wait_job(act, b, proj_full, ("o", tb - 2))
                    nc.scalar.activation(parts[:, tb % 2, HI, :], rows[:, tb, 0:D], ACT.Copy).then_inc(y_high.sem, 1)
                wait_job(act, b, proj_full, ("o", ROWT - 2))
                wait_job(act, b, proj_full, ("o", ROWT - 1))
                for i in range(4):
                    high(b, 0, i)
                for tb in range(ROWT):
                    bank = wait_job(act, b, proj_full, ("x", tb))
                    nc.scalar.activation(probs[:, tb, :], bank[:, :], ACT.Copy).then_inc(free_of(b, ("x", tb)), 1)
                take_v(b, 2)
                take_v(b, 3)
                act.wait_ge(shifted.sem, shifted.at(b, 1))
                nc.scalar.activation(expo[:, :, :], logit[:, :, :], ACT.Exp).then_inc(exp_route.sem, 1)

        @block.vector
        def _(dve):
            def low(b, u, i):
                bank, _ = place_of(b, ("p", u, i))
                n = 4 * tile_turn(b, u) + i
                dve.wait_ge(part_high.sem, part_high.early(n + 1) if b is None else part_high.at(b, n + 1))
                nc.vector.tensor_tensor(parts[:, i % 2, LO, :], proj[bank][:, :], parts[:, i % 2, HI, :].bitcast(F32),
                                        ALU.subtract).then_inc(proj_free[bank].sem, 1)

            for i in range(4):
                low(None, 0, i)
            dve.wait_ge(setup_done, 1)
            dve.wait_ge(setup_dma, 48)
            with dve.Fori(0, BATCHES) as b:
                def reduce_tile(u, i):
                    qb, h, j, cols, _, _ = MAX_TILES[i]
                    n = MTILES * u + i
                    dve.wait_ge(max_full.sem, max_full.at(b, n + 1))
                    nc.vector.tensor_reduce(tile_max[:, j, h, qb:qb + 1], maxp[n % 2][:, 0:cols], AX.X, ALU.max)\
                        .then_inc(max_free[n % 2].sem, 1)

                def unit_max(u):
                    half = BANK // P
                    for s in range(2):
                        dve.wait_ge(max_free[s].sem, max_free[s].at(b, MTILES // 2 * (u + 1)))
                    if u:
                        wait_job(dve, b, proj_full, ("m", u - 1))
                    rm = row_max[:, :].rearrange("p (h t) -> p h t", h=4)
                    nc.vector.tensor_copy(rm[:, :, 0:half], tile_max[:, 0, :, 0:half]).then_inc(max_step.sem, 1)
                    nc.vector.tensor_tensor(rm[:, :, half:ROWT], tile_max[:, 0, :, half:ROWT],
                                            tile_max[:, 1, :, half:ROWT], ALU.max).then_inc(max_ready.sem, 1)

                def y_of(n):
                    u, t = divmod(n, HALVES)
                    return rows[:, 4 * t:4 * t + 4, u * P:(u + 1) * P]

                def copy_y(n):
                    weighed(dve, b, GROUPS * (n // HALVES) + (HALF0 if n % HALVES == 0 else GROUPS))
                    if n == 0:
                        dve.wait_ge(scattered.sem, scattered.at(b, 0))
                    nc.vector.tensor_copy(y_of(n), y_ps[:, :].rearrange("p (t q) -> p t q", q=P))\
                        .then_inc(y_copied.sem, 1)

                def divide(n):
                    dve.wait_ge(sums_copied.sem, sums_copied.at(b, n + 1))
                    nc.vector.reciprocal(sums[:, :], sums[:, :]).then_inc(recip_done.sem, 1)
                    dve.wait_ge(recip_done.sem, recip_done.at(b, n + 1))
                    dve.wait_ge(y_copied.sem, y_copied.at(b, n + 1))
                    nc.vector.tensor_tensor(y_of(n), y_of(n), sums[:, :].rearrange("p (t q) -> p t q", q=P), ALU.mult)\
                        .then_inc(y_ready.sem, 1)

                for j, name in enumerate(OPENING):
                    for i in range(6 * j, 6 * j + 6):
                        reduce_tile(0, i)
                    if name[0] == "p":
                        low(b, 1, name[2])
                unit_max(0)
                for u in range(UNITS):
                    for j in range(GROUPS):
                        if u and j == 0:
                            copy_y(2 * u - 1)
                        if u and j == 1:
                            divide(2 * u - 1)
                        if j == HALF0 + 1:
                            copy_y(2 * u)
                        due = list(maxima(j)) if u + 1 < UNITS else []
                        for i in due[0:3]:
                            reduce_tile(u + 1, i)
                        if u + 2 < UNITS and j:
                            for i in tiles_made(j - 1):
                                low(b, u + 2, i)
                        for i in due[3:]:
                            reduce_tile(u + 1, i)
                        if u + 1 < UNITS:
                            if j == 9:
                                unit_max(u + 1)
                        if j == 10:
                            divide(2 * u)
                copy_y(2 * UNITS - 1)
                divide(2 * UNITS - 1)

                for tb in range(ROWT):
                    bank = wait_job(dve, b, proj_full, ("o", tb))
                    dve.wait_ge(x_in_dma[tb % 2].sem, x_in_dma[tb % 2].at(b, 16 * (tb // 2 + 1)))
                    nc.vector.tensor_tensor(rows[:, tb, 0:D], bank[:, :], x_in[:, tb % 2, :], ALU.add)\
                        .then_inc(proj_free[place_of(b, ("o", tb))[0]].sem, 1)
                    wait_job(dve, b, proj_free, ("o", tb))
                    nc.vector.bn_stats(stats[:, tb, :], rows[:, tb, 0:D]).then_inc(norm_step.sem, 1)
                    dve.wait_ge(norm_step.sem, norm_step.at(b, 2 * tb + 1))
                    hold(dve, held_dve)
                    nc.vector.bn_aggr(mv[:, tb, :], stats[:, tb, :]).then_inc(norm_step.sem, 1)
                dve.wait_ge(norm_step.sem, norm_step.at(b, 2 * ROWT))
                nc.vector.tensor_scalar(var_eps[:, :], mv[:, :, 1], EPS, None, ALU.add).then_inc(var_ready.sem, 1)
                nc.vector.tensor_copy(rows[:, :, ID_COL], token[:, :]).then_inc(norm_step.sem, 1)
                for i in range(2):
                    low(b, 0, i)
                dve.wait_ge(rstd_ready.sem, rstd_ready.at(b, 1))
                for tb in range(ROWT):
                    nc.vector.tensor_scalar(rows[:, tb, 0:D], rows[:, tb, 0:D], mv[:, tb, 0:1], rstd[:, tb:tb + 1],
                                            ALU.subtract, ALU.mult).then_inc(normed.sem, 1)
                for i in range(2, 4):
                    low(b, 0, i)

                step = 0

                def link(ins):
                    nonlocal step
                    step += 1
                    ins.then_inc(route_step.sem, 1)
                    dve.wait_ge(route_step.sem, route_step.at(b, step))

                wide = [P, ROWT, EXPERTS]
                per_tile = lambda a: a.unsqueeze(2).to_broadcast(wide)
                per_expert = lambda a: a.unsqueeze(1).to_broadcast(wide)
                dve.wait_ge(norm_step.sem, norm_step.at(b, 2 * ROWT + 1))
                link(nc.vector.tensor_scalar(token[:, :], token[:, :], float(SEQ), None, ALU.add))
                dve.wait_ge(logits_done.sem, logits_done.at(b, ROWT))
                link(nc.vector.tensor_tensor(pick[:, :, :], logit_ps, per_expert(rb[:, :]), ALU.add))
                link(nc.vector.tensor_reduce(small[:, 0, :], pick[:, :, :], AX.X, ALU.max))
                nc.vector.tensor_tensor(logit[:, :, :], pick[:, :, :], per_tile(small[:, 0, :]), ALU.subtract)\
                    .then_inc(shifted.sem, 1)
                dve.wait_ge(shifted.sem, shifted.at(b, 1))
                link(nc.vector.scalar_tensor_tensor(out=pick[:, :, :], in0=logit[:, :, :], scalar=0.0,
                                                    in1=per_expert(order[:, :]), op0=ALU.is_ge, op1=ALU.mult))
                link(nc.vector.tensor_reduce(small[:, 1, :], pick[:, :, :], AX.X, ALU.max))
                nc.vector.tensor_tensor(onehot[:, :, :], pick[:, :, :], per_tile(small[:, 1, :]), ALU.is_equal)\
                    .then_inc(onehot_ready.sem, 1)
                dve.wait_ge(exp_route.sem, exp_route.at(b, 1))
                link(nc.vector.tensor_reduce(small[:, 2, :], expo[:, :, :], AX.X, ALU.add))
                link(nc.vector.reciprocal(rows[:, :, W_COL], small[:, 2, :]))
                dve.wait_ge(ranks_done.sem, ranks_done.at(b, 1))
                nc.vector.tensor_copy(base[:, 0, :], region_end[:, :]).then_inc(route_step.sem, 1)
                step += 1
                for tb in range(ROWT):
                    dve.wait_ge(route_step.sem, route_step.at(b, step))
                    after = base[:, tb + 1, :] if tb + 1 < ROWT else region_end[:, :]
                    nc.vector.tensor_tensor(after, total_ps[:, tb, :], base[:, tb, :], ALU.add)\
                        .then_inc(route_step.sem, 1)
                    step += 1
                dve.wait_ge(route_step.sem, route_step.at(b, step))
                link(nc.vector.tensor_tensor(base[:, :, :], rank_ps, base[:, :, :], ALU.add))
                link(nc.vector.tensor_tensor(base[:, :, :], base[:, :, :], onehot[:, :, :], ALU.mult))
                link(nc.vector.tensor_reduce(small[:, 3, :], base[:, :, :], AX.X, ALU.add))
                nc.vector.tensor_copy(dest[:, :], small[:, 3, :]).then_inc(dest_ready.sem, 1)
                assert step == ROUTE_STEPS, step

        @block.tensor
        def _(pe):
            def begin(b, name):
                bank, n = place_of(b, name)
                if b is not None:
                    pe.wait_ge(proj_free[bank].sem, proj_free[bank].at(b, n))
                elif n:
                    pe.wait_ge(proj_free[bank].sem, proj_free[bank].early(n))
                return proj[bank], proj_full[bank].sem

            def project(b, u, i, piece):
                o, t = divmod(i, HALVES)
                bank, _ = place_of(b, ("p", u, i))
                if piece == 0:
                    begin(b, ("p", u, i))
                    if t == 0:
                        turn = tile_turn(b, u)
                        pe.wait_ge(w_in[o].sem, w_in[o].early(16) if b is None else w_in[o].at(b, 16 * turn))
                for c in range(4 * piece, 4 * piece + 4):
                    k, (ws, xs) = c // 3, MM3[c % 3]
                    mm = nc.tensor.matmul(proj[bank][:, :], w_qk[:, o, ws, k, :], xt[:, xs, k, t * BANK:(t + 1) * BANK],
                                          start=c == 0, stop=c == 3 * KT - 1)
                if piece == 2:
                    mm.then_inc(proj_full[bank].sem, 1)

            def values(b, tb, piece=None):
                bank, _ = place_of(b, ("v", tb))
                if piece in (None, 0):
                    begin(b, ("v", tb))
                wv = q_st[WV_SET][:, :, :].rearrange("p (c k) (l n) -> p c (k l) n", c=2, n=D)
                for c in range(3 * KT) if piece is None else range(4 * piece, 4 * piece + 4):
                    k, (xs, ws) = c // 3, MM3[c % 3]
                    mm = nc.tensor.matmul(proj[bank][:, :], xt[:, xs, k, tb * P:(tb + 1) * P], wv[:, ws, k, :],
                                          start=c == 0, stop=c == 3 * KT - 1)
                if piece in (None, 2):
                    mm.then_inc(proj_full[bank].sem, 1)

            pe.wait_ge(xt_low.sem, xt_low.early(KT))
            for i in range(4):
                for piece in range(3):
                    project(None, 0, i, piece)
            pe.wait_ge(setup_done, 1)
            pe.wait_ge(setup_dma, 48)
            for tb in range(V_AHEAD):
                values(None, tb)

            with pe.Fori(0, BATCHES) as b:
                def stacks_ready(turns):
                    for s in range(2):
                        stacked(pe, b, s, 2 * turns)

                def max_tile(u, i):
                    qb, h, j, cols, computed, diag = MAX_TILES[i]
                    n = MTILES * u + i
                    pe.wait_ge(max_free[n % 2].sem, max_free[n % 2].at(b, n // 2))
                    mm = nc.tensor.matmul(maxp[n % 2][:, 0:computed], q_st[u % SETS][0:3 * DH, h, qb * P:(qb + 1) * P],
                                          k_st[u % SETS][0:3 * DH, h, j * BANK:j * BANK + computed],
                                          start=True, stop=True)
                    if diag is not None:
                        mm = nc.tensor.matmul(maxp[n % 2][:, diag:diag + P], ident_b[:, :], mask_qk[:, :],
                                              start=False, stop=True, skip_group_check=True)
                    mm.then_inc(max_full.sem, 1)

                def score_tile(u, j, h):
                    t, kb = SCORE_GROUPS[j]
                    i = STILES * u + 4 * j + h
                    c = column(kb, t)
                    c0 = min(c, BANK - 256)
                    pe.wait_ge(exp_done.sem, exp_done.at(b, max(i - 1, 0)))
                    mm = nc.tensor.matmul(score[h % 2][:, c0:BANK], k_st[u % SETS][0:3 * DH + 1, h, kb * P:(kb + 1) * P],
                                          q_st[u % SETS][0:3 * DH + 1, h, t * BANK + c0:(t + 1) * BANK],
                                          start=True, stop=True)
                    if kb * P >= t * BANK:
                        mm = nc.tensor.matmul(score[h % 2][:, c:c + P], ident_b[:, :], mask_kq[:, :],
                                              start=False, stop=True, skip_group_check=True)
                    mm.then_inc(score_full.sem, 1)

                def weigh(u, j, sums_too):
                    t, kb = SCORE_GROUPS[j]
                    n = GROUPS * u + j
                    last = kb == (t + 1) * BANK // P - 1
                    c = column(kb, t)
                    half = HALVES * u + t
                    if not sums_too:
                        pe.wait_ge(exp_done.sem, exp_done.at(b, 4 * (n + 1)))
                    if kb == 0:
                        free = sums_copied if sums_too else y_copied
                        pe.wait_ge(free.sem, free.at(b, half))
                    for h in range(4):
                        head = 4 * u + h
                        mm = nc.tensor.matmul((den_ps if sums_too else y_ps)[DH * h:DH * (h + 1), c:BANK],
                                              ones_f[:, :] if sums_too else v[:, kb, head * DH:(head + 1) * DH],
                                              probs[:, 4 * (n % 2) + h, c:BANK], start=kb == 0, stop=last,
                                              tile_position=(0, DH * h), skip_group_check=True)
                    if sums_too:
                        mm.then_inc(probs_used.sem, 1)

                def transpose_max(u):
                    pe.wait_ge(max_step.sem, max_step.at(b, u + 1))
                    pe.wait_ge(max_ready.sem, max_ready.at(b, u + 1))
                    bank, full = begin(b, ("m", u))
                    nc.tensor.transpose(bank[0:4 * ROWT, 0:P], row_max[:, :], ident[:, :]).then_inc(full, 1)

                stacks_ready(0)
                for j, name in enumerate(OPENING):
                    for piece in range(3):
                        if name[0] == "p":
                            project(b, 1, name[2], piece)
                        else:
                            values(b, name[1], piece)
                        for i in range(6 * j + 2 * piece, 6 * j + 2 * piece + 2):
                            max_tile(0, i)
                transpose_max(0)
                wait_job(pe, b, proj_free, ("v", ROWT - 2))
                wait_job(pe, b, proj_free, ("v", ROWT - 1))
                pe.wait_ge(dest_ready.sem, dest_ready.at(b, 0))
                for u in range(UNITS):
                    for j in range(GROUPS):
                        made = list(pieces(j)) if u + 2 < UNITS else []
                        maxed = list(maxima(j)) if u + 1 < UNITS else []
                        if j == 2 and maxed:
                            stacks_ready(u + 1)
                        for p in made[0:1]:
                            project(b, u + 2, p // 3, p % 3)
                        if j == 0:
                            pe.wait_ge(neg_in.sem, neg_in.at(b, 16 * (u + 1)))
                        for h in range(4):
                            score_tile(u, j, h)
                            for i in maxed[len(maxed) * h // 4:len(maxed) * (h + 1) // 4]:
                                max_tile(u + 1, i)
                            if h == 1:
                                for p in made[1:2]:
                                    project(b, u + 2, p // 3, p % 3)
                            if j and h == 2:
                                weigh(u, j - 1, False)
                        if j:
                            weigh(u, j - 1, True)
                        if u + 1 < UNITS and j == 10:
                            transpose_max(u + 1)
                    weigh(u, GROUPS - 1, False)
                    weigh(u, GROUPS - 1, True)

                pe.wait_ge(wv_in.sem, wv_in.at(b, 16))
                pe.wait_ge(xt_low.sem, xt_low.at(b, KT))
                values(b, 0)
                values(b, 1)
                wo = q_st[WO_SET][:, :, :].rearrange("p (c k) (l n) -> p c (k l) n", c=2, n=D)
                pe.wait_ge(wo_in.sem, wo_in.at(b, 16))
                for tb in range(ROWT):
                    bank, full = begin(b, ("o", tb))
                    pe.wait_ge(y_low.sem, y_low.at(b, tb + 1))
                    for c in range(3 * UNITS):
                        g, (ys, ws) = c // 3, MM3[c % 3]
                        mm = nc.tensor.matmul(bank[:, :], parts[:, tb % 2, ys, g * P:(g + 1) * P], wo[:, ws, g, :],
                                              start=c == 0, stop=c == 3 * UNITS - 1)
                    mm.then_inc(full, 1)
                for i in range(4):
                    for piece in range(3):
                        project(b, 0, i, piece)
                for tb in range(ROWT + 1):
                    if tb < ROWT:
                        pe.wait_ge(normed.sem, normed.at(b, tb + 1))
                        bank, full = begin(b, ("x", tb))
                        for k in range(KT):
                            mm = nc.tensor.transpose(bank[:, k * P:(k + 1) * P], rows[:, tb, k * P:(k + 1) * P], ident[:, :])
                        mm.then_inc(full, 1)
                    if tb:
                        wait_job(pe, b, proj_free, ("x", tb - 1))
                        if tb == 1:
                            pe.wait_ge(y_copied.sem, y_copied.at(b, UNITS * HALVES))
                            pe.wait_ge(sums_copied.sem, sums_copied.at(b, UNITS * HALVES))
                        for k in range(KT):
                            mm = nc.tensor.matmul(logit_ps[:, tb - 1, :], probs[:, tb - 1, k * P:(k + 1) * P], rw[:, k, :],
                                                  start=k == 0, stop=k == KT - 1, skip_group_check=True)
                        mm.then_inc(logits_done.sem, 1)
                values(b, 2)
                values(b, 3)
                pe.wait_ge(onehot_ready.sem, onehot_ready.at(b, 1))
                hot = onehot[:, :, :].rearrange("p t e -> p (t e)")
                nc.tensor.matmul(rank_ps.rearrange("p t e -> p (t e)"), before_b[:, :], hot, start=True, stop=True,
                                 skip_group_check=True)
                nc.tensor.matmul(total_ps.rearrange("p t e -> p (t e)"), ones_b[:, :], hot, start=False, stop=True,
                                 skip_group_check=True).then_inc(ranks_done.sem, 1)


def run_experts(nc, region_end, expert_w_t, expert_b, dispatched, unread, out):
    RING = 4
    AHEAD = RING - 1
    STEPS = -(-TILES // RING) * RING
    TABLE = STEPS + AHEAD
    with ExitStack() as ctx:
        def sb(name, shape, dt=F32):
            return ctx.enter_context(nc.sbuf_tensor(name, shape, dt))

        def sem(name):
            return ctx.enter_context(nc.semaphore(name))

        starting = []

        def signal(name, per=RING, before=0, first=RING, dma=False):
            starting.append(Signal(ctx, nc, name, per, 16 if dma else first, before))
            return starting[-1]

        weight = sb("weight", [P, 2, EXPERTS * KT * D], F32R)
        w_raw = sb("w_raw", [P, 2, KT * D])
        bias = sb("bias", [P, EXPERTS * D], F32R)
        pick_bias = sb("pick_bias", [P, P], F32R)
        got = sb("got", [P, RING, ROW])
        xt = sb("xt_tile", [P, 2, 2, D], F32R)
        y = sb("y", [P, RING, D])
        bias_raw = y[0:2, :, :].rearrange("p s n -> p (s n)")
        minus_row = sb("minus_row", [2, 1])
        ident = sb("ident2", [P, P])
        pad = sb("pad", [P, ROW])
        stats = sb("stats2", [P, RING, 6])
        mv = sb("mv2", [P, RING, 2])
        var_eps = sb("var_eps2", [P, RING])
        half_neg = sb("half_neg2", [P, 1])
        rstd = sb("rstd2", [P, RING])
        shift = sb("shift2", [P, RING])
        home = sb("home", [P, RING], U32)
        lane = sb("lane", [P, EXPERTS])
        first = sb("first", [P, EXPERTS])
        tile_rows = sb("tile_rows", [P, TOKENS // P])
        tile_no = sb("tile_no", [P, TABLE])
        count = sb("count", [P, EXPERTS])
        tiles = sb("tiles", [P, EXPERTS])
        more = sb("more", [P, EXPERTS, TOKENS // P])
        end = sb("end", [P, EXPERTS])
        passed = sb("passed", [P, TABLE, EXPERTS])
        scaled = sb("scaled", [P, TABLE, EXPERTS])
        expert_f = sb("expert_f", [P, TABLE])
        start_f = sb("start_f", [P, TABLE])
        work = sb("work", [P, 2, TABLE])
        expert = sb("expert", [P, TABLE], I32)
        start = sb("start", [P, TABLE], I32)
        tail = sb("tail", [P, EXPERTS])
        tail_row = sb("tail_row", [P, EXPERTS], U32)
        xt_ps = [ctx.enter_context(nc.psum_tensor(f"xt_ps{i}", [P, BANK], F32)) for i in range(2)]
        y_ps = [ctx.enter_context(nc.psum_tensor(f"ye_ps{i}", [P, BANK], F32)) for i in range(RING)]

        raw_in = [sem(f"ew_in{i}") for i in range(2)]
        high_done = sem("ew_high")
        low_done = sem("ew_low")
        bias_in = sem("bias_in")
        bias_high = sem("bias_high")
        bias_low = sem("bias_low")
        consts = sem("consts")
        pool_step = sem("pool_step")
        plan_step = sem("plan_step")
        tail_ready = sem("tail_ready")
        table_ready = sem("table_ready")
        padded = sem("padded")
        held_sp, held_pool, held_dve = sem("held_sp2"), sem("held_pool2"), sem("held_dve2")
        got_in = [signal(f"got_in{i}", 16, 16 * (i < AHEAD), dma=True) for i in range(RING)]
        turned = signal("turned", before=1)
        xt_high = signal("xe_high", before=1)
        xt_low = signal("xe_low", before=1)
        y_full = signal("ye_full")
        summed = signal("summed")
        row_step = signal("row_step", 2 * RING)
        stats_ready = signal("stats_ready2")
        norm_step = signal("norm_step2", 3 * RING)
        normed = signal("normed2")
        sent = [Signal(ctx, nc, f"sent{i}", 16, 16) for i in range(RING)]
        block = ctx.enter_context(nc.Block())

        @block.sync
        def _(sp):
            for s in starting:
                sp.sem_inc(s.sem, s.first)
            for e in range(EXPERTS):
                if e >= 2:
                    sp.wait_ge(high_done, e - 1)
                    sp.wait_ge(low_done, e - 1)
                sp.dma_start(w_raw[:, e % 2, :].rearrange("p (k n) -> p k n", k=KT),
                             expert_w_t[e].rearrange("(k p) n -> p k n", p=P)).then_inc(raw_in[e % 2], 16)
                if e in (1, 2):
                    if e == 2:
                        sp.wait_ge(bias_low, 1)
                    half = slice((e - 1) * RING * D, e * RING * D)
                    sp.dma_start(bias_raw, expert_b.rearrange("e n -> (e n)")[half].partition_broadcast(2))\
                        .then_inc(bias_in, 16)

            def load(at, slot):
                hold(sp, held_sp)
                row = sp.value_load(start[0:1, at], min_val=0, max_val=SPARE)
                sp.dma_start(got[:, slot, :], dispatched[bass.ds(row, P), :]).then_inc(got_in[slot].sem, 16)

            sp.wait_ge(table_ready, 2)
            sp.wait_ge(padded, EXPERTS * 16)
            for t in range(AHEAD):
                load(slice(t, t + 1), t)
            with sp.Fori(0, STEPS // RING) as i:
                for s in range(RING):
                    sp.wait_ge(summed.sem, summed.at(i, s))
                    load(bass.ds(i * RING + s + AHEAD, 1), (s + AHEAD) % RING)
            for s in range(RING):
                sp.wait_ge(got_in[s].sem, got_in[s].at(STEPS // RING, 0))

        @block.gpsimd
        def _(pool):
            step = 0

            def link(ins):
                nonlocal step
                step += 1
                ins.then_inc(pool_step, 1)
                pool.wait_ge(pool_step, step)

            loose = dict(allow_small_or_imprecise_dtypes=True)
            link(nc.gpsimd.memset(ident[:, :], 0.0))
            link(nc.gpsimd.memset(pad[:, 0:ID_COL], 0.0))
            link(nc.gpsimd.memset(pad[:, ID_COL:ROW], float(NO_TOKEN)))
            link(nc.gpsimd.memset(half_neg[:, :], -0.5))
            link(nc.gpsimd.affine_select(out=ident[:, :], in_=ident[:, :], compare_op=ALU.not_equal, fill=1.0,
                                         base=0, pattern=[[-1, P]], channel_multiplier=1))
            link(nc.gpsimd.iota(lane[:, :], [[0, EXPERTS]], base=0, channel_multiplier=1, **loose))
            link(nc.gpsimd.iota(first[:, :], [[REGION, EXPERTS]], base=0, channel_multiplier=0, **loose))
            link(nc.gpsimd.iota(tile_rows[:, :], [[P, TOKENS // P]], base=0, channel_multiplier=0, **loose))
            link(nc.gpsimd.iota(tile_no[:, :], [[1, TABLE]], base=0, channel_multiplier=0, **loose))
            link(nc.gpsimd.memset(pick_bias[:, :].bitcast(F32), 0.0))
            link(nc.gpsimd.memset(pick_bias[0:2, :].bitcast(F32), 1.0))
            link(nc.gpsimd.iota(minus_row[:, :], [[0, 1]], base=0, channel_multiplier=-1, **loose))
            nc.gpsimd.memset(bias[:, :].bitcast(F32), 0.0).then_inc(consts, 1)
            pool.wait_ge(tail_ready, 1)
            pool.wait_ge(consts, 1)
            for s in range(RING):
                nc.gpsimd.dma_start(unread[s * P:(s + 1) * P, :], pad[:, :]).then_inc(sent[s].sem, 16)
            for e in range(EXPERTS):
                nc.gpsimd.indirect_dma_start(
                    out=dispatched, out_offset=bass.IndirectOffsetOnAxis(ap=tail_row[:, e:e + 1], axis=0),
                    in_=pad[:, :], in_offset=None).then_inc(padded, 16)
            with pool.Fori(0, STEPS // RING) as i:
                def send(s):
                    pool.wait_ge(normed.sem, normed.at(i, s + 1))
                    hold(pool, held_pool)
                    nc.gpsimd.indirect_dma_start(
                        out=out, out_offset=bass.IndirectOffsetOnAxis(ap=home[:, s:s + 1], axis=0),
                        in_=y[:, s, :], in_offset=None, bounds_check=TOKENS - 1, oob_is_err=False)\
                        .then_inc(sent[s].sem, 16)

                for s in range(RING):
                    one = slice(s, s + 1)
                    pool.wait_ge(stats_ready.sem, stats_ready.at(i, s + 1))
                    hold(pool, held_pool)
                    nc.gpsimd.tensor_scalar(var_eps[:, one], mv[:, s, 1:2], EPS, None, ALU.add)\
                        .then_inc(norm_step.sem, 1)
                    pool.wait_ge(norm_step.sem, norm_step.at(i, 3 * s + 1))
                    nc.gpsimd.tensor_tensor(rstd[:, one], var_eps[:, one], half_neg[:, :], ALU.pow)\
                        .then_inc(norm_step.sem, 1)
                    pool.wait_ge(norm_step.sem, norm_step.at(i, 3 * s + 2))
                    hold(pool, held_pool)
                    nc.gpsimd.tensor_scalar(shift[:, one], mv[:, s, 0:1], rstd[:, one], -1.0, ALU.mult, ALU.mult)\
                        .then_inc(norm_step.sem, 1)
                    if s:
                        send(s - 1)
                send(RING - 1)
            for s in range(RING):
                pool.wait_ge(sent[s].sem, sent[s].at(STEPS // RING, 0))

        @block.scalar
        def _(act):
            for e in range(EXPERTS):
                act.wait_ge(raw_in[e % 2], 16 * (e // 2 + 1))
                nc.scalar.activation(weight[:, HI, e * KT * D:(e + 1) * KT * D], w_raw[:, e % 2, :], ACT.Copy)\
                    .then_inc(high_done, 1)
                if e in (1, 2):
                    act.wait_ge(bias_in, 16 * e)
                    act.wait_ge(consts, 1)
                    nc.scalar.activation(bias[0:2, (e - 1) * RING * D:e * RING * D], bias_raw, ACT.Copy)\
                        .then_inc(bias_high, 1)

            def high(slot):
                nc.scalar.activation(xt[:, slot, HI, :], xt_ps[slot][:, :], ACT.Copy).then_inc(xt_high.sem, 1)

            act.wait_ge(turned.sem, turned.early(1))
            high(0)
            with act.Fori(0, STEPS // RING) as i:
                def norm(s):
                    act.wait_ge(norm_step.sem, norm_step.at(i, 3 * s + 3))
                    nc.scalar.activation(y[:, s, :], y[:, s, :], ACT.Identity, bias=shift[:, s:s + 1],
                                         scale=rstd[:, s:s + 1]).then_inc(normed.sem, 1)

                for s in range(RING):
                    act.wait_ge(turned.sem, turned.at(i, s + 1))
                    act.wait_ge(y_full.sem, y_full.at(i, s))
                    high((s + 1) % 2)
                    if s:
                        norm(s - 1)
                norm(RING - 1)

        @block.vector
        def _(dve):
            step = 0

            def link(ins):
                nonlocal step
                step += 1
                ins.then_inc(plan_step, 1)
                dve.wait_ge(plan_step, step)

            dve.wait_ge(consts, 1)
            link(nc.vector.tensor_tensor(tail[:, :], region_end[:, :], lane[:, :], ALU.add))
            nc.vector.tensor_copy(tail_row[:, :], tail[:, :]).then_inc(tail_ready, 1)
            link(nc.vector.tensor_tensor(count[:, :], region_end[:, :], first[:, :], ALU.subtract))
            wide = [P, EXPERTS, TOKENS // P]
            link(nc.vector.tensor_tensor(more[:, :, :], count[:, :].unsqueeze(2).to_broadcast(wide),
                                         tile_rows[:, :].unsqueeze(1).to_broadcast(wide), ALU.is_gt))
            link(nc.vector.tensor_reduce(tiles[:, :], more[:, :, :], AX.X, ALU.add))
            link(nc.vector.tensor_copy(end[:, 0:1], tiles[:, 0:1]))
            for e in range(1, EXPERTS):
                link(nc.vector.tensor_tensor(end[:, e:e + 1], end[:, e - 1:e], tiles[:, e:e + 1], ALU.add))
            wide = [P, TABLE, EXPERTS]
            per_expert = lambda a: a.unsqueeze(1).to_broadcast(wide)
            link(nc.vector.tensor_tensor(passed[:, :, :], tile_no[:, :].unsqueeze(2).to_broadcast(wide),
                                         per_expert(end[:, :]), ALU.is_ge))
            link(nc.vector.tensor_reduce(expert_f[:, :], passed[:, :, :], AX.X, ALU.add))
            link(nc.vector.tensor_tensor(scaled[:, :, :], passed[:, :, :], per_expert(tiles[:, :]), ALU.mult))
            link(nc.vector.tensor_reduce(work[:, 0, :], scaled[:, :, :], AX.X, ALU.add))
            link(nc.vector.tensor_tensor(work[:, 1, :], tile_no[:, :], work[:, 0, :], ALU.subtract))
            link(nc.vector.tensor_scalar(work[:, 1, :], work[:, 1, :], float(P), None, ALU.mult))
            link(nc.vector.scalar_tensor_tensor(out=start_f[:, :], in0=expert_f[:, :], scalar=float(REGION),
                                                in1=work[:, 1, :], op0=ALU.mult, op1=ALU.add))
            link(nc.vector.tensor_scalar(start_f[:, :], start_f[:, :], float(SPARE), None, ALU.min))
            link(nc.vector.tensor_scalar(expert_f[:, :], expert_f[:, :], float(EXPERTS - 1), None, ALU.min))
            nc.vector.tensor_copy(start[:, :], start_f[:, :]).then_inc(table_ready, 1)
            nc.vector.tensor_copy(expert[:, :], expert_f[:, :]).then_inc(table_ready, 1)
            for e in range(EXPERTS):
                dve.wait_ge(high_done, e + 1)
                nc.vector.tensor_tensor(weight[:, LO, e * KT * D:(e + 1) * KT * D], w_raw[:, e % 2, :],
                                        weight[:, HI, e * KT * D:(e + 1) * KT * D].bitcast(F32), ALU.subtract)\
                    .then_inc(low_done, 1)
                if e in (1, 2):
                    half = bias[0:2, (e - 1) * RING * D:e * RING * D]
                    dve.wait_ge(bias_high, e)
                    nc.vector.scalar_tensor_tensor(out=half, in0=half.bitcast(F32), scalar=minus_row[:, :],
                                                   in1=bias_raw, op0=ALU.mult, op1=ALU.add).then_inc(bias_low, 1)

            def low(slot):
                nc.vector.tensor_tensor(xt[:, slot, LO, :], xt_ps[slot][:, :], xt[:, slot, HI, :].bitcast(F32),
                                        ALU.subtract).then_inc(xt_low.sem, 1)

            dve.wait_ge(xt_high.sem, xt_high.early(1))
            low(0)
            with dve.Fori(0, STEPS // RING) as i:
                for s in range(RING):
                    dve.wait_ge(xt_high.sem, xt_high.at(i, s + 1))
                    low((s + 1) % 2)
                    dve.wait_ge(sent[s].sem, sent[s].at(i, 0))
                    dve.wait_ge(got_in[s].sem, got_in[s].at(i, 16 * (s == AHEAD)))
                    nc.vector.tensor_copy(home[:, s:s + 1], got[:, s, ID_COL:ROW]).then_inc(row_step.sem, 1)
                    dve.wait_ge(y_full.sem, y_full.at(i, s + 1))
                    nc.vector.scalar_tensor_tensor(out=y[:, s, :], in0=y_ps[s][:, :], scalar=got[:, s, W_COL:W_COL + 1],
                                                   in1=got[:, s, 0:D], op0=ALU.mult, op1=ALU.add).then_inc(summed.sem, 1)
                    dve.wait_ge(summed.sem, summed.at(i, s + 1))
                    nc.vector.bn_stats(stats[:, s, :], y[:, s, :]).then_inc(row_step.sem, 1)
                    dve.wait_ge(row_step.sem, row_step.at(i, 2 * s + 2))
                    hold(dve, held_dve)
                    nc.vector.bn_aggr(mv[:, s, :], stats[:, s, :]).then_inc(stats_ready.sem, 1)

        @block.tensor
        def _(pe):
            def turn(slot, bank):
                for k in range(KT):
                    mm = nc.tensor.transpose(xt_ps[bank][:, k * P:(k + 1) * P], got[:, slot, k * P:(k + 1) * P],
                                             ident[:, :])
                mm.then_inc(turned.sem, 1)

            pe.wait_ge(consts, 1)
            pe.wait_ge(table_ready, 2)
            pe.wait_ge(got_in[0].sem, got_in[0].early(16))
            turn(0, 0)
            pe.wait_ge(bias_low, 2)
            with pe.Fori(0, STEPS // RING) as i:
                for s in range(RING):
                    nxt = (s + 1) % RING
                    pe.wait_ge(got_in[nxt].sem, got_in[nxt].at(i, 16 * (nxt in (0, AHEAD))))
                    pe.wait_ge(xt_low.sem, xt_low.at(i, s - 1))
                    turn(nxt, (s + 1) % 2)
                    e = pe.value_load(expert[0:1, bass.ds(i * RING + s, 1)], min_val=0, max_val=EXPERTS - 1)
                    pe.wait_ge(low_done, e + 1)
                    pe.wait_ge(xt_low.sem, xt_low.at(i, s))
                    pe.wait_ge(summed.sem, summed.at(i, s - AHEAD))
                    nc.tensor.matmul(y_ps[s][:, :], pick_bias[:, :], bias[:, bass.ds(e * D, D)], start=True, stop=False)
                    for c in range(3 * KT):
                        k, (xs, ws) = c // 3, MM3[c % 3]
                        mm = nc.tensor.matmul(y_ps[s][:, :], xt[:, s % 2, xs, k * P:(k + 1) * P],
                                              weight[:, ws, bass.ds(e * (KT * D) + k * D, D)],
                                              start=False, stop=c == 3 * KT - 1)
                    mm.then_inc(y_full.sem, 1)


def run(nc, x_t, x_rows, wq_t, wk_t, wv_t, wo_t, router_w_t, router_b, expert_w_t, expert_b, out=None):
    w_qk_parts = nc.dram_tensor("w_qk_parts", [UNITS, 2, P, 2 * KT * P], F32).ap()
    w_vo_parts = nc.dram_tensor("w_vo_parts", [2, P, 2 * KT * D], F32).ap()
    dispatched = nc.dram_tensor("dispatched", [SPARE + P, ROW], F32).ap()
    unread = nc.dram_tensor("unread", [4 * P, ROW], F32).ap()
    with ExitStack() as ctx:
        region_end = ctx.enter_context(nc.sbuf_tensor("region_end", [P, EXPERTS], F32))
        split_weights(nc, w_qk_parts, w_vo_parts, wq_t, wk_t, wv_t, wo_t)
        attend(nc, region_end, x_t, x_rows, router_w_t, router_b, w_qk_parts, w_vo_parts, dispatched)
        if out is not None:
            run_experts(nc, region_end, expert_w_t, expert_b, dispatched, unread, out)


def kernel(**inputs):
    import numpy as np
    import concourse.bacc as bacc
    from concourse.bass_utils import run_bass_kernel_spmd

    x = np.asarray(inputs["L0_attn_x"])
    rows = x.reshape(TOKENS, D)
    laid_out = {
        "x_t": rows.T,
        "x_rows": rows,
        "wq_t": np.asarray(inputs["L0_attn_W_Q"]).T,
        "wk_t": np.asarray(inputs["L0_attn_W_K"]).T,
        "wv_t": np.asarray(inputs["L0_attn_W_V"]).T,
        "wo_t": np.asarray(inputs["L0_attn_W_O"]).T,
        "router_w_t": np.asarray(inputs["L0_ffn_router_w"]).T,
        "router_b": np.asarray(inputs["L0_ffn_router_b"]),
        "expert_w_t": np.asarray(inputs["L0_ffn_expert_w"]).transpose(0, 2, 1),
        "expert_b": np.asarray(inputs["L0_ffn_expert_b"]),
    }
    laid_out = {name: np.ascontiguousarray(a) for name, a in laid_out.items()}
    nc = bacc.Bacc("TRN2", target_bir_lowering=False, num_devices=1)
    aps = {name: nc.dram_tensor(name, a.shape, mybir.dt.from_np(a.dtype), kind="ExternalInput").ap()
           for name, a in laid_out.items()}
    out = nc.dram_tensor("out", [TOKENS, D], F32, kind="ExternalOutput").ap()
    run(nc, out=out, **aps)
    result = run_bass_kernel_spmd(nc, [laid_out], core_ids=[0])
    return result.results[0]["out"].reshape(BATCHES, SEQ, D)
```

```python
from contextlib import ExitStack

import concourse.bass as bass
from concourse import mybir

F32 = mybir.dt.float32
F32R = mybir.dt.float32r
BF16 = mybir.dt.bfloat16
I32 = mybir.dt.int32
U32 = mybir.dt.uint32
ALU = mybir.AluOpType
ACT = mybir.ActivationFunctionType
AX = mybir.AxisListType

P = 128
BATCHES, SEQ, D = 8, 1024, 512
HEADS, DH = 16, 32
EXPERTS = 8
KT = D // P
UNITS = HEADS // 4
BANK = 512
HALVES = SEQ // BANK
ROWT = SEQ // P
TOKENS = BATCHES * SEQ
SCALE = float(DH) ** -0.5
EPS = 1e-5
MASKED = -1e30
HI, LO = 0, 1
SETS = 3
WO_SET, WV_SET = 1, 2
Q, K = 0, 1

ROW = D + 2
W_COL, ID_COL = D, D + 1
REGION = TOKENS + P
SPARE = EXPERTS * REGION
NO_TOKEN = TOKENS + P
TILES = TOKENS // P + EXPERTS
MM3 = ((HI, HI), (HI, LO), (LO, HI))


class Signal:

    def __init__(self, ctx, nc, name, per, first, before=0):
        self.sem, self.per = ctx.enter_context(nc.semaphore(name)), per
        self.first, self.before = first, before

    def at(self, loop, count):
        assert count + self.before + self.first > 0
        return loop * self.per + (count + self.before + self.first)

    def early(self, count):
        assert 0 < count <= self.before
        return count + self.first


def hold(eng, passed):
    eng.sem_inc(passed, 1)


def split_weights(nc, xt, xt_raw, x_t, w_qk_parts, w_vo_parts, wq_t, wk_t, wv_t, wo_t):
    with ExitStack() as ctx:
        raw = [ctx.enter_context(nc.sbuf_tensor(f"w_raw{i}", [P, KT * D], F32)) for i in range(4)]
        both = ctx.enter_context(nc.sbuf_tensor("w_both", [P, 4, 2, KT * D], F32R))
        raw_in = [ctx.enter_context(nc.semaphore(f"w_raw_in{i}")) for i in range(4)]
        x_in = [ctx.enter_context(nc.semaphore(f"first_x_in{i}")) for i in range(2)]
        high_done = ctx.enter_context(nc.semaphore("w_high_done"))
        low_done = ctx.enter_context(nc.semaphore("w_low_done"))
        x_high = ctx.enter_context(nc.semaphore("first_x_high"))
        x_low = ctx.enter_context(nc.semaphore("first_x_low"))
        parts_out = ctx.enter_context(nc.semaphore("w_parts_out"))
        block = ctx.enter_context(nc.Block())

        @block.sync
        def _(sp):
            def load_x(k):
                sp.dma_start(xt_raw[:, k % 2, :], x_t[k * P:(k + 1) * P, 0:SEQ]).then_inc(x_in[k % 2], 16)

            for i, w in enumerate((wq_t, wk_t, wv_t, wo_t)):
                sp.dma_start(raw[i][:, :].rearrange("p (k n) -> p k n", k=KT),
                             w.rearrange("(k p) n -> p k n", p=P)).then_inc(raw_in[i], 16)
            for k in range(2):
                load_x(k)
            for i in range(2):
                sp.wait_ge(high_done, i + 1)
                sp.wait_ge(low_done, i + 1)
                for u in range(UNITS):
                    src = both[:, i].rearrange("p c (k n) -> p (c k) n", n=D)[:, :, u * P:(u + 1) * P]
                    sp.dma_start(w_qk_parts[u, i].rearrange("p (c n) -> p c n", n=P), src.bitcast(F32))\
                        .then_inc(parts_out, 16)
            for k in range(2, KT):
                sp.wait_ge(x_high, k - 1)
                sp.wait_ge(x_low, k - 1)
                load_x(k)
            for i in range(2):
                sp.wait_ge(high_done, i + 3)
                sp.wait_ge(low_done, i + 3)
                sp.dma_start(w_vo_parts[i], both[:, 2 + i].rearrange("p c n -> p (c n)").bitcast(F32))\
                    .then_inc(parts_out, 16)
            sp.wait_ge(parts_out, 2 * (UNITS + 1) * 16)

        @block.scalar
        def _(act):
            for i in range(4):
                act.wait_ge(raw_in[i], 16)
                nc.scalar.activation(both[:, i, HI], raw[i][:, :], ACT.Copy).then_inc(high_done, 1)
            for k in range(KT):
                act.wait_ge(x_in[k % 2], 16 * (k // 2 + 1))
                nc.scalar.activation(xt[:, HI, k, :], xt_raw[:, k % 2, :], ACT.Copy).then_inc(x_high, 1)

        @block.vector
        def _(dve):
            for i in range(4):
                dve.wait_ge(high_done, i + 1)
                nc.vector.tensor_tensor(both[:, i, LO], raw[i][:, :], both[:, i, HI].bitcast(F32),
                                        ALU.subtract).then_inc(low_done, 1)
            for k in range(KT):
                dve.wait_ge(x_high, k + 1)
                nc.vector.tensor_tensor(xt[:, LO, k, :], xt_raw[:, k % 2, :], xt[:, HI, k, :].bitcast(F32),
                                        ALU.subtract).then_inc(x_low, 1)


def attend(nc, region_end, xt, xt_raw, x_t, x_rows, router_w_t, router_b, w_qk_parts, w_vo, dispatched):
    with ExitStack() as ctx:
        def sb(name, shape, dt=F32):
            return ctx.enter_context(nc.sbuf_tensor(name, shape, dt))

        def sem(name):
            return ctx.enter_context(nc.semaphore(name))

        starting = []

        def signal(name, per, before=0, dma=False):
            starting.append(Signal(ctx, nc, name, per, 16 if dma else 1, before))
            return starting[-1]

        w_qk = sb("w_qk", [P, 2, 2, KT, P], F32R)
        q_st = [sb(f"q_stack{s}", [P, 4, SEQ], F32R) for s in range(SETS)]
        k_st = [sb(f"k_stack{s}", [P, 4, SEQ], F32R) for s in range(SETS)]
        v = sb("v", [P, ROWT, D])
        parts = sb("parts", [P, 2, 2, BANK], F32R)
        probs = sb("probs", [P, 8, BANK])
        rows = sb("rows", [P, ROWT, ROW])
        x_in = xt_raw[:, :, 0:D]
        sums = sb("sums", [P, BANK])
        tile_max = sb("tile_max", [P, 2, 4, ROWT])
        row_max = sb("row_max", [P, 4 * ROWT])
        neg_max = sb("neg_max", [4 * ROWT, P], F32R)
        ident = sb("ident", [P, P])
        ident_b = sb("ident_b", [P, P], BF16)
        mask_qk = sb("mask_qk", [P, P], BF16)
        mask_kq = sb("mask_kq", [P, P], BF16)
        before_b = sb("before_b", [P, P], BF16)
        ones_b = sb("ones_b", [P, P], BF16)
        ones_f = sb("ones_f", [P, DH])
        rw = sb("rw", [P, KT, EXPERTS])
        rb = sb("rb", [P, EXPERTS])
        stats = sb("stats", [P, ROWT, 6])
        mv = sb("mv", [P, ROWT, 2])
        var_eps = sb("var_eps", [P, ROWT])
        half_neg = sb("half_neg", [P, ROWT])
        rstd = sb("rstd", [P, ROWT])
        token = sb("token", [P, ROWT])
        logit = sb("logit", [P, ROWT, EXPERTS])
        expo = sb("expo", [P, ROWT, EXPERTS])
        pick = sb("pick", [P, ROWT, EXPERTS])
        onehot = sb("onehot", [P, ROWT, EXPERTS], BF16)
        order = sb("order", [P, EXPERTS])
        base = sb("base", [P, ROWT, EXPERTS])
        small = sb("small", [P, 4, ROWT])
        dest = sb("dest", [P, ROWT], U32)

        proj = [ctx.enter_context(nc.psum_tensor(f"proj{i}", [P, BANK], F32)) for i in range(2)]
        maxp = [ctx.enter_context(nc.psum_tensor(f"maxp{i}", [P, BANK], F32)) for i in range(2)]
        score = [ctx.enter_context(nc.psum_tensor(f"score{i}", [P, BANK], F32)) for i in range(2)]
        y_ps = ctx.enter_context(nc.psum_tensor("y_ps", [P, BANK], F32))
        den_ps = ctx.enter_context(nc.psum_tensor("den_ps", [P, BANK], F32))
        logit_ps = y_ps[:, 0:ROWT * EXPERTS].rearrange("p (t e) -> p t e", e=EXPERTS)
        rank_ps = den_ps[:, 0:ROWT * EXPERTS].rearrange("p (t e) -> p t e", e=EXPERTS)
        total_ps = den_ps[:, 64:64 + ROWT * EXPERTS].rearrange("p (t e) -> p t e", e=EXPERTS)

        NPROJ = UNITS * 2 * HALVES
        SP_BLOCKS = 2
        V_AHEAD = 6
        QUARTER = ROWT // HALVES
        JOBS = NPROJ + ROWT + UNITS + ROWT + ROWT
        AHEAD = 4 + V_AHEAD
        STILES = 4 * sum(1 + (t * P >= BANK) for t in range(ROWT))
        GROUPS = STILES // 4
        MAX_TILES = []
        for qb in range(ROWT):
            for j in range(1 + (qb * P >= BANK)):
                cols = min((qb + 1) * P - j * BANK, BANK)
                diag = cols - P if (qb + 1) * P <= (j + 1) * BANK else None
                for h in range(0, 4, min(BANK // cols, 4)):
                    MAX_TILES.append((qb, range(h, h + min(BANK // cols, 4)), j, cols, diag))
        MTILES = len(MAX_TILES)
        HALF0 = BANK // P
        setup_dma = sem("setup_dma")
        w_in = [signal(f"w_in{o}", UNITS * 16, 32, dma=True) for o in range(2)]
        setup_done = sem("setup_done")
        setup_step = sem("setup_step")
        held_sp, held_pool, held_dve = sem("held_sp"), sem("held_pool"), sem("held_dve")
        xt_in = [signal(f"xt_in{i}", 2 * 16, dma=True) for i in range(2)]
        xt_high = signal("xt_high", KT)
        xt_low = signal("xt_low", KT)
        proj_full = [signal(f"proj_full{i}", JOBS // 2, AHEAD // 2) for i in range(2)]
        proj_free = [signal(f"proj_free{i}", JOBS // 2, AHEAD // 2) for i in range(2)]
        part_high = signal("part_high", NPROJ, 4)
        SP_GAIN, POOL_GAIN = 4 * SP_BLOCKS * 16, 4 * (3 - SP_BLOCKS) * 16
        sp_in = [signal(f"sp_in{i}", UNITS * 2 * SP_GAIN, 2 * SP_GAIN, dma=True) for i in range(2)]
        pool_in = [Signal(ctx, nc, f"pool_in{i}", UNITS * 2 * POOL_GAIN, 0, 2 * POOL_GAIN) for i in range(2)]
        max_full = signal("max_full", UNITS * MTILES)
        max_free = [signal(f"max_free{i}", UNITS * MTILES // 2) for i in range(2)]
        max_step = signal("max_step", UNITS)
        max_ready = signal("max_ready", UNITS)
        neg_in = signal("neg_in", UNITS * 16, dma=True)
        score_full = signal("score_full", UNITS * STILES)
        exp_done = signal("exp_done", UNITS * STILES)
        probs_used = signal("probs_used", UNITS * GROUPS)
        y_copied = signal("y_copied", UNITS * HALVES)
        sums_copied = signal("sums_copied", UNITS * HALVES)
        recip_done = signal("recip_done", UNITS * HALVES * QUARTER)
        y_ready = signal("y_ready", UNITS * HALVES * QUARTER)
        wo_in = signal("wo_in", 16, dma=True)
        wv_in = signal("wv_in", 16, dma=True)
        y_high = signal("y_high", ROWT)
        y_low = signal("y_low", ROWT)
        x_in_dma = [signal(f"x_in_dma{i}", ROWT // 2 * 16, dma=True) for i in range(2)]
        norm_step = signal("norm_step", 2 * ROWT + 1)
        var_ready = signal("var_ready", HALVES)
        rstd_ready = signal("rstd_ready", HALVES)
        normed = signal("normed", ROWT)
        logits_done = signal("logits_done", ROWT)
        ROUTE_STEPS = 11 + ROWT
        route_step = signal("route_step", ROUTE_STEPS)
        shifted = signal("shifted", 1)
        exp_route = signal("exp_route", 1)
        onehot_ready = signal("onehot_ready", 1)
        ranks_done = signal("ranks_done", 1)
        dest_ready = signal("dest_ready", 1)
        scattered = Signal(ctx, nc, "scattered", ROWT * 16, 16)

        OPENING = [("p", 1, 0), ("p", 1, 1), ("v", 6), ("p", 1, 2), ("p", 1, 3)]
        O_GROUP = {8: 0, 9: 1, 10: 2}
        HIGH_GROUP = {7: (0, 1), 8: (2,), 9: (3,)}
        CLOSING = [("o", 3), ("v", 0), ("v", 1), ("o", 4), ("x", 0), ("o", 5), ("x", 1), ("o", 6), ("x", 2), ("o", 7),
                   ("x", 3), ("p", 0, 0), ("p", 0, 1), ("v", 2), ("x", 4), ("x", 5), ("x", 6), ("x", 7),
                   ("p", 0, 2), ("p", 0, 3), ("v", 3), ("v", 4), ("v", 5)]
        AHEAD_JOBS = [("p", 0, 0), ("p", 0, 1), ("v", 0), ("v", 1), ("p", 0, 2), ("v", 2), ("p", 0, 3), ("v", 3),
                      ("v", 4), ("v", 5)]
        job_names = OPENING + [("m", 0), ("v", 7)]
        for u in range(1, UNITS):
            job_names += [("p", u + 1, i) for i in range(4)] * (u + 1 < UNITS) + [("m", u)]
        job_names += [("o", i) for i in O_GROUP.values()] + CLOSING
        LAST_CLOSING = [name for name in CLOSING if name[0] in "ox"]
        last_names = job_names[:-len(CLOSING)] + LAST_CLOSING
        assert len(job_names) == JOBS and JOBS % 2 == 0 and AHEAD % 2 == 0 and len(AHEAD_JOBS) == AHEAD

        def place_of(b, name):
            names = AHEAD_JOBS if b is None else last_names if isinstance(b, int) else job_names
            n = names.index(name)
            return n % 2, n // 2

        def wait_job(eng, b, sems, name):
            bank, n = place_of(b, name)
            s = sems[bank]
            eng.wait_ge(s.sem, s.early(n + 1) if b is None else s.at(b, n + 1))
            return proj[bank]

        def wait_last_batch(eng, b, sems):
            for s in sems:
                eng.wait_ge(s.sem, s.at(b, 0))

        def weighed(eng, b, n):
            eng.wait_ge(probs_used.sem, probs_used.at(b, n))

        def tile_turn(b, u):
            return 0 if b is None else (u - 1) % UNITS

        def stacked(eng, b, slot, tiles):
            for s, gain in ((sp_in[slot], SP_GAIN), (pool_in[slot], POOL_GAIN)):
                eng.wait_ge(s.sem, s.early(tiles * gain) if b is None else s.at(b, tiles * gain))

        def max_bank(u, i):
            return (maxp + score)[i % 4] if u == 0 else maxp[i % 2]

        def column(kb, t):
            return max(kb * P - t * BANK, 0)

        MAX_GROUPS = (2, 10), (0, 9)

        def pieces(j):
            return range((3 * j + 1) // 2, (3 * (j + 1) + 1) // 2) if j < 8 else ()

        def opening_maxima(j):
            return range(MTILES * (j - 1) // (len(OPENING) - 1), MTILES * j // (len(OPENING) - 1)) if j else range(0)

        def tiles_made(j):
            return [p // 3 for p in pieces(j) if p % 3 == 2]

        def maxima(u, j):
            begin, end = MAX_GROUPS[u > 0]
            if not begin <= j < end or u + 1 == UNITS:
                return []
            return list(range(MTILES * (j - begin) // (end - begin), MTILES * (j + 1 - begin) // (end - begin)))

        SCORE_GROUPS = [(t, kb) for t in range(HALVES) for kb in range((t + 1) * BANK // P)]
        assert len(SCORE_GROUPS) == GROUPS

        block = ctx.enter_context(nc.Block())

        def send_tile(eng, b, u, o, t, blocks, done, held):
            wait_job(eng, b, proj_free, ("p", u, 2 * o + t))
            if b is not None:
                hold(eng, held)
            dst = (q_st, k_st)[o][u % SETS]
            for block_row in blocks:
                part = ((HI, HI, LO), (HI, LO, HI))[o][block_row]
                for h in range(4):
                    eng.dma_start(dst[DH * block_row:DH * (block_row + 1), h, t * BANK:(t + 1) * BANK].bitcast(F32),
                                  parts[DH * h:DH * (h + 1), t, part, :].bitcast(F32)).then_inc(done[t].sem, 16)

        @block.sync
        def _(sp):
            for s in starting:
                sp.sem_inc(s.sem, s.first)

            def load_w(u, o):
                sp.dma_start(w_qk[:, o].rearrange("p c k n -> p (c k n)").bitcast(F32), w_qk_parts[u, o])\
                    .then_inc(w_in[o].sem, 16)

            def load_xt(batch, k):
                sp.dma_start(xt_raw[:, k % 2, :], x_t[k * P:(k + 1) * P, bass.ds(batch * SEQ, SEQ)])\
                    .then_inc(xt_in[k % 2].sem, 16)

            def load_wv(done):
                sp.dma_start(q_st[WV_SET][:, :, :].rearrange("p h n -> p (h n)").bitcast(F32), w_vo[0]).then_inc(done, 16)

            def send(b, u):
                for o in (Q, K):
                    for t in range(HALVES):
                        send_tile(sp, b, u, o, t, range(SP_BLOCKS), sp_in, held_sp)
                    if not (u == UNITS - 1 and isinstance(b, int)):
                        load_w((u + 1) % UNITS, o)

            load_w(0, Q)
            load_w(0, K)
            load_wv(setup_dma)
            sp.dma_start(rw[:, :, :], router_w_t.rearrange("(k p) e -> p k e", p=P)).then_inc(setup_dma, 16)
            sp.dma_start(rb[:, :], router_b.partition_broadcast(P)).then_inc(setup_dma, 16)
            send(None, 0)

            def one_pass(b, last):
                def load_x(tb):
                    hold(sp, held_sp)
                    sp.dma_start(x_in[:, tb % 2, :], x_rows[bass.ds(b * SEQ + tb * P, P), :])\
                        .then_inc(x_in_dma[tb % 2].sem, 16)

                wait_last_batch(sp, b, proj_full)
                hold(sp, held_sp)
                send(b, 1)
                hold(sp, held_sp)
                wait_last_batch(sp, b, proj_free)
                hold(sp, held_sp)
                for k in range(0 if last else 2):
                    load_xt(b + 1, k)
                wait_job(sp, b, proj_full, ("v", 6))
                hold(sp, held_sp)
                wait_job(sp, b, proj_full, ("v", 7))
                hold(sp, held_sp)
                send(b, 2)
                hold(sp, held_sp)
                weighed(sp, b, GROUPS)
                hold(sp, held_sp)
                send(b, 3)
                hold(sp, held_sp)
                weighed(sp, b, GROUPS * 2)
                sp.dma_start(q_st[WO_SET][:, :, :].rearrange("p h n -> p (h n)").bitcast(F32), w_vo[1]).then_inc(wo_in.sem, 16)
                if not last:
                    for k in range(2, KT):
                        hold(sp, held_sp)
                        sp.wait_ge(xt_high.sem, xt_high.at(b, k - 1))
                        hold(sp, held_sp)
                        sp.wait_ge(xt_low.sem, xt_low.at(b, k - 1))
                        hold(sp, held_sp)
                        load_xt(b + 1, k)
                    weighed(sp, b, GROUPS * 3)
                    load_wv(wv_in.sem)
                    hold(sp, held_sp)
                    sp.wait_ge(xt_high.sem, xt_high.at(b, KT))
                    hold(sp, held_sp)
                    sp.wait_ge(xt_low.sem, xt_low.at(b, KT))
                load_x(0)
                load_x(1)
                for tb in range(2, ROWT):
                    wait_job(sp, b, proj_free, ("o", tb - 2))
                    load_x(tb)
                if not last:
                    send(b, 0)

            with sp.Fori(0, BATCHES - 1) as b:
                one_pass(b, False)
            one_pass(BATCHES - 1, True)

        @block.gpsimd
        def _(pool):
            step = 0

            def link(ins):
                nonlocal step
                step += 1
                ins.then_inc(setup_step, 1)
                pool.wait_ge(setup_step, step)

            def split_low(k, count):
                pool.wait_ge(xt_high.sem, count)
                nc.gpsimd.tensor_tensor(xt[:, LO, k, :], xt_raw[:, k % 2, :], xt[:, HI, k, :].bitcast(F32),
                                        ALU.subtract).then_inc(xt_low.sem, 1)

            link(nc.gpsimd.memset(ident[:, :], 0.0))
            link(nc.gpsimd.memset(ones_b[:, :], 1.0))
            link(nc.gpsimd.memset(ones_f[:, :], 1.0))
            link(nc.gpsimd.memset(mask_qk[:, :], MASKED))
            link(nc.gpsimd.memset(mask_kq[:, :], MASKED))
            link(nc.gpsimd.memset(half_neg[:, :], -0.5))
            link(nc.gpsimd.affine_select(out=ident[:, :], in_=ident[:, :], compare_op=ALU.not_equal, fill=1.0,
                                         base=0, pattern=[[-1, P]], channel_multiplier=1))
            link(nc.gpsimd.tensor_copy(ident_b[:, :], ident[:, :]))
            link(nc.gpsimd.affine_select(out=mask_qk[:, :], in_=mask_qk[:, :], compare_op=ALU.is_gt, fill=0.0,
                                         base=0, pattern=[[1, P]], channel_multiplier=-1))
            link(nc.gpsimd.affine_select(out=mask_kq[:, :], in_=mask_kq[:, :], compare_op=ALU.is_gt, fill=0.0,
                                         base=0, pattern=[[-1, P]], channel_multiplier=1))
            link(nc.gpsimd.affine_select(out=before_b[:, :], in_=ones_b[:, :], compare_op=ALU.is_gt, fill=0.0,
                                         base=0, pattern=[[1, P]], channel_multiplier=-1))
            loose = dict(allow_small_or_imprecise_dtypes=True)
            link(nc.gpsimd.iota(order[:, :], [[-1, EXPERTS]], base=EXPERTS, channel_multiplier=0, **loose))
            link(nc.gpsimd.iota(token[:, :], [[P, ROWT]], base=0, channel_multiplier=1, **loose))
            link(nc.gpsimd.iota(region_end[:, :], [[REGION, EXPERTS]], base=0, channel_multiplier=0, **loose))
            for s in range(SETS):
                link(nc.gpsimd.memset(k_st[s][3 * DH:3 * DH + 1, :, :].bitcast(F32), 1.0))
            link(nc.gpsimd.memset(rows[:, 0, 0:ID_COL], 0.0))
            link(nc.gpsimd.memset(rows[:, 0, ID_COL:ROW], float(NO_TOKEN)))
            nc.gpsimd.dma_start(dispatched[SPARE:SPARE + P, :], rows[:, 0, :]).then_inc(scattered.sem, 16)
            nc.gpsimd.memset(small[:, :, :], 0.0).then_inc(setup_done, 1)

            def send(b, u):
                for o in (Q, K):
                    for t in range(HALVES):
                        send_tile(pool, b, u, o, t, range(SP_BLOCKS, 3), pool_in, held_pool)

            send(None, 0)
            def one_pass(b, last):
                wait_last_batch(pool, b, proj_full)
                hold(pool, held_pool)
                send(b, 1)
                wait_job(pool, b, proj_full, ("v", 6))
                hold(pool, held_pool)
                wait_job(pool, b, proj_full, ("v", 7))
                hold(pool, held_pool)
                send(b, 2)
                hold(pool, held_pool)
                weighed(pool, b, GROUPS)
                hold(pool, held_pool)
                send(b, 3)
                for k in range(0 if last else KT):
                    split_low(k, xt_high.at(b, k + 1))
                for tb in range(ROWT):
                    pool.wait_ge(y_high.sem, y_high.at(b, tb + 1))
                    nc.gpsimd.tensor_tensor(parts[:, tb % 2, LO, :], rows[:, tb, 0:D],
                                            parts[:, tb % 2, HI, :].bitcast(F32), ALU.subtract)\
                        .then_inc(y_low.sem, 1)
                    if tb in (QUARTER + 1, ROWT - 1):
                        half = 0 if tb < ROWT - 1 else 1
                        of = slice(QUARTER * half, QUARTER * (half + 1))
                        pool.wait_ge(var_ready.sem, var_ready.at(b, half + 1))
                        nc.gpsimd.tensor_tensor(rstd[:, of], var_eps[:, of], half_neg[:, of], ALU.pow)\
                            .then_inc(rstd_ready.sem, 1)
                if not last:
                    send(b, 0)
                pool.wait_ge(dest_ready.sem, dest_ready.at(b, 1))
                hold(pool, held_pool)
                for tb in range(ROWT):
                    nc.gpsimd.indirect_dma_start(
                        out=dispatched, out_offset=bass.IndirectOffsetOnAxis(ap=dest[:, tb:tb + 1], axis=0),
                        in_=rows[:, tb, :], in_offset=None).then_inc(scattered.sem, 16)

            with pool.Fori(0, BATCHES - 1) as b:
                one_pass(b, False)
            one_pass(BATCHES - 1, True)
            pool.wait_ge(scattered.sem, scattered.at(BATCHES, 0))

        @block.scalar
        def _(act):
            def split_high(k, count):
                act.wait_ge(xt_in[k % 2].sem, count)
                nc.scalar.activation(xt[:, HI, k, :], xt_raw[:, k % 2, :], ACT.Copy).then_inc(xt_high.sem, 1)

            def free_of(b, name):
                return proj_free[place_of(b, name)[0]].sem

            def high(b, u, i):
                o, t = divmod(i, HALVES)
                bank = wait_job(act, b, proj_full, ("p", u, i))
                if b is not None or o == K:
                    stacked(act, b, t, 2 * tile_turn(b, u) + o)
                nc.scalar.activation(parts[:, t, HI, :], bank[:, :], ACT.Copy).then_inc(part_high.sem, 1)

            def take_v(b, tb):
                bank = wait_job(act, b, proj_full, ("v", tb))
                nc.scalar.activation(v[:, tb, :], bank[:, :], ACT.Copy).then_inc(free_of(b, ("v", tb)), 1)

            for name in AHEAD_JOBS:
                if name[0] == "p":
                    high(None, 0, name[2])
                else:
                    take_v(None, name[1])

            def one_pass(b, last):
                def negate(u):
                    bank = wait_job(act, b, proj_full, ("m", u))
                    act.wait_ge(neg_in.sem, neg_in.at(b, 16 * u))
                    nc.scalar.activation(neg_max[:, :], bank[0:4 * ROWT, 0:P], ACT.Copy, scale=-1.0)\
                        .then_inc(free_of(b, ("m", u)), 1)
                    wait_job(act, b, proj_free, ("m", u))
                    act.dma_start(q_st[u % SETS][3 * DH:3 * DH + 1, :, :].rearrange("p h (t c) -> p (h t) c", c=P).bitcast(F32),
                                  neg_max[:, :].bitcast(F32)).then_inc(neg_in.sem, 16)

                def copy_sums(n):
                    weighed(act, b, GROUPS * (n // HALVES) + (HALF0 if n % HALVES == 0 else GROUPS))
                    act.wait_ge(y_ready.sem, y_ready.at(b, QUARTER * n))
                    nc.scalar.activation(sums[:, :], den_ps[:, :], ACT.Copy).then_inc(sums_copied.sem, 1)

                def high_y(tb):
                    if tb == 0:
                        act.wait_ge(y_ready.sem, y_ready.at(b, QUARTER * (UNITS * HALVES - 1)))
                    if tb >= QUARTER:
                        act.wait_ge(y_ready.sem, y_ready.at(b, QUARTER * (UNITS * HALVES - 1) + tb - QUARTER + 1))
                    if tb == 0:
                        for s in range(2):
                            stacked(act, b, s, 6)
                    if tb >= 2:
                        wait_job(act, b, proj_full, ("o", tb - 2))
                    nc.scalar.activation(parts[:, tb % 2, HI, :], rows[:, tb, 0:D], ACT.Copy).then_inc(y_high.sem, 1)

                for name in OPENING:
                    if name[0] == "p":
                        high(b, 1, name[2])
                    else:
                        take_v(b, name[1])
                negate(0)
                take_v(b, ROWT - 1)
                act.wait_ge(logits_done.sem, logits_done.at(b, 0))
                for u in range(UNITS):
                    for j, (t, kb) in enumerate(SCORE_GROUPS):
                        if u and j == 0:
                            copy_sums(2 * u - 1)
                        if u == 2 and j in (1, 3, 5, 7) and not last:
                            if j == 1:
                                wait_job(act, b, proj_full, ("p", 3, 2))
                                wait_job(act, b, proj_full, ("p", 3, 3))
                            k = j // 2
                            split_high(k, xt_in[k % 2].at(b, 16 * (k // 2 + 1)))
                        n = GROUPS * u + j
                        if n >= 2:
                            weighed(act, b, n - 1)
                        for h in range(4):
                            c = column(kb, t)
                            act.wait_ge(score_full.sem, score_full.at(b, 4 * n + h + 1))
                            nc.scalar.activation(probs[:, 4 * (n % 2) + h, c:BANK], score[h % 2][:, c:BANK],
                                                 ACT.Exp, scale=SCALE).then_inc(exp_done.sem, 1)
                        if u + 2 < UNITS:
                            for i in tiles_made(j):
                                high(b, u + 2, i)
                        if j == HALF0:
                            copy_sums(2 * u)
                        if u + 1 < UNITS and j == MAX_GROUPS[u > 0][1]:
                            negate(u + 1)
                        if u == UNITS - 1:
                            for tb in HIGH_GROUP.get(j, ()):
                                high_y(tb)
                copy_sums(2 * UNITS - 1)
                for name in CLOSING:
                    if name[0] == "v":
                        if name[1] < 2:
                            high_y(QUARTER + name[1])
                        if not last:
                            take_v(b, name[1])
                    if name[0] == "x":
                        tb = name[1]
                        bank = wait_job(act, b, proj_full, name)
                        nc.scalar.activation(probs[:, tb, :], bank[:, :], ACT.Copy).then_inc(free_of(b, name), 1)
                        if tb < 2:
                            high_y(QUARTER + 2 + tb)
                    if name[0] == "p" and not last:
                        if name[2] == 0:
                            wait_job(act, b, proj_full, ("o", ROWT - 2))
                            wait_job(act, b, proj_full, ("o", ROWT - 1))
                        high(b, 0, name[2])
                act.wait_ge(shifted.sem, shifted.at(b, 1))
                nc.scalar.activation(expo[:, :, :], logit[:, :, :], ACT.Exp).then_inc(exp_route.sem, 1)

            with act.Fori(0, BATCHES - 1) as b:
                one_pass(b, False)
            one_pass(BATCHES - 1, True)

        @block.vector
        def _(dve):
            def low(b, u, i):
                bank, _ = place_of(b, ("p", u, i))
                n = 4 * tile_turn(b, u) + i
                dve.wait_ge(part_high.sem, part_high.early(n + 1) if b is None else part_high.at(b, n + 1))
                nc.vector.tensor_tensor(parts[:, i % 2, LO, :], proj[bank][:, :], parts[:, i % 2, HI, :].bitcast(F32),
                                        ALU.subtract).then_inc(proj_free[bank].sem, 1)

            for i in range(4):
                low(None, 0, i)
            dve.wait_ge(setup_done, 1)
            dve.wait_ge(setup_dma, 48)
            def one_pass(b, last):
                def reduce_tile(u, i):
                    qb, heads, j, cols, _ = MAX_TILES[i]
                    tiles = max_bank(u, i)[:, 0:len(heads) * cols].rearrange("p (h c) -> p h c", c=cols)
                    n = MTILES * u + i
                    dve.wait_ge(max_full.sem, max_full.at(b, n + 1))
                    nc.vector.tensor_reduce(tile_max[:, j, heads[0]:heads[-1] + 1, qb], tiles, AX.X, ALU.max)\
                        .then_inc(max_free[n % 2].sem, 1)

                def unit_max(u):
                    half = BANK // P
                    for s in max_free:
                        dve.wait_ge(s.sem, s.at(b, MTILES // 2 * (u + 1)))
                    if u:
                        wait_job(dve, b, proj_full, ("m", u - 1))
                    rm = row_max[:, :].rearrange("p (h t) -> p h t", h=4)
                    nc.vector.tensor_copy(rm[:, :, 0:half], tile_max[:, 0, :, 0:half]).then_inc(max_step.sem, 1)
                    nc.vector.tensor_tensor(rm[:, :, half:ROWT], tile_max[:, 0, :, half:ROWT],
                                            tile_max[:, 1, :, half:ROWT], ALU.max).then_inc(max_ready.sem, 1)

                def y_of(n):
                    u, t = divmod(n, HALVES)
                    return rows[:, 4 * t:4 * t + 4, u * P:(u + 1) * P]

                def copy_y(n):
                    weighed(dve, b, GROUPS * (n // HALVES) + (HALF0 if n % HALVES == 0 else GROUPS))
                    if n == 0:
                        dve.wait_ge(scattered.sem, scattered.at(b, 0))
                    nc.vector.tensor_copy(y_of(n), y_ps[:, :].rearrange("p (t q) -> p t q", q=P))\
                        .then_inc(y_copied.sem, 1)

                def divide(n, tiles=range(QUARTER)):
                    for t in tiles:
                        cols, count = slice(t * P, (t + 1) * P), QUARTER * n + t + 1
                        if t == 0:
                            dve.wait_ge(sums_copied.sem, sums_copied.at(b, n + 1))
                            dve.wait_ge(y_copied.sem, y_copied.at(b, n + 1))
                        nc.vector.reciprocal(sums[:, cols], sums[:, cols]).then_inc(recip_done.sem, 1)
                        dve.wait_ge(recip_done.sem, recip_done.at(b, count))
                        nc.vector.tensor_tensor(y_of(n)[:, t, :], y_of(n)[:, t, :], sums[:, cols], ALU.mult)\
                            .then_inc(y_ready.sem, 1)

                def residual(tb):
                    bank = wait_job(dve, b, proj_full, ("o", tb))
                    dve.wait_ge(x_in_dma[tb % 2].sem, x_in_dma[tb % 2].at(b, 16 * (tb // 2 + 1)))
                    nc.vector.tensor_tensor(rows[:, tb, 0:D], bank[:, :], x_in[:, tb % 2, :], ALU.add)\
                        .then_inc(proj_free[place_of(b, ("o", tb))[0]].sem, 1)
                    wait_job(dve, b, proj_free, ("o", tb))
                    nc.vector.bn_stats(stats[:, tb, :], rows[:, tb, 0:D]).then_inc(norm_step.sem, 1)
                    dve.wait_ge(norm_step.sem, norm_step.at(b, 2 * tb + 1))
                    hold(dve, held_dve)
                    nc.vector.bn_aggr(mv[:, tb, :], stats[:, tb, :]).then_inc(norm_step.sem, 1)

                def variance(half):
                    of = slice(QUARTER * half, QUARTER * (half + 1))
                    dve.wait_ge(norm_step.sem, norm_step.at(b, 2 * QUARTER * (half + 1)))
                    nc.vector.tensor_scalar(var_eps[:, of], mv[:, of, 1], EPS, None, ALU.add).then_inc(var_ready.sem, 1)

                def normalize(half):
                    dve.wait_ge(rstd_ready.sem, rstd_ready.at(b, half + 1))
                    for tb in range(QUARTER * half, QUARTER * (half + 1)):
                        nc.vector.tensor_scalar(rows[:, tb, 0:D], rows[:, tb, 0:D], mv[:, tb, 0:1], rstd[:, tb:tb + 1],
                                                ALU.subtract, ALU.mult).then_inc(normed.sem, 1)

                for j, name in enumerate(OPENING):
                    for i in opening_maxima(j):
                        reduce_tile(0, i)
                    if name[0] == "p":
                        low(b, 1, name[2])
                unit_max(0)
                for u in range(UNITS):
                    for j in range(GROUPS):
                        if u and j == 0:
                            copy_y(2 * u - 1)
                        if j == HALF0 + 1:
                            copy_y(2 * u)
                            if u == UNITS - 1:
                                divide(2 * u)
                        due = maxima(u, j)
                        for n, i in enumerate(due[0:3]):
                            reduce_tile(u + 1, i)
                            if u and j < 4 and n == 1:
                                divide(2 * u - 1, [j])
                        if u == UNITS - 1 and j == 1:
                            divide(2 * u - 1)
                        if u + 2 < UNITS and j:
                            for i in tiles_made(j - 1):
                                low(b, u + 2, i)
                        for i in due[3:]:
                            reduce_tile(u + 1, i)
                        if u + 1 < UNITS:
                            if j == MAX_GROUPS[u > 0][1] - 1:
                                unit_max(u + 1)
                        if u < UNITS - 1 and j == 10:
                            divide(2 * u)
                        if u == UNITS - 1 and j in O_GROUP:
                            residual(O_GROUP[j])
                copy_y(2 * UNITS - 1)
                divide(2 * UNITS - 1)
                residual(QUARTER - 1)
                variance(0)
                normalize(0)
                for tb in range(QUARTER, ROWT):
                    residual(tb)
                variance(1)
                nc.vector.tensor_copy(rows[:, :, ID_COL], token[:, :]).then_inc(norm_step.sem, 1)
                normalize(1)
                for i in range(0 if last else 2):
                    low(b, 0, i)

                step = 0

                def link(ins):
                    nonlocal step
                    step += 1
                    ins.then_inc(route_step.sem, 1)
                    dve.wait_ge(route_step.sem, route_step.at(b, step))

                wide = [P, ROWT, EXPERTS]
                per_tile = lambda a: a.unsqueeze(2).to_broadcast(wide)
                per_expert = lambda a: a.unsqueeze(1).to_broadcast(wide)
                dve.wait_ge(norm_step.sem, norm_step.at(b, 2 * ROWT + 1))
                link(nc.vector.tensor_scalar(token[:, :], token[:, :], float(SEQ), None, ALU.add))
                dve.wait_ge(logits_done.sem, logits_done.at(b, ROWT))
                link(nc.vector.tensor_tensor(pick[:, :, :], logit_ps, per_expert(rb[:, :]), ALU.add))
                link(nc.vector.tensor_reduce(small[:, 0, :], pick[:, :, :], AX.X, ALU.max))
                nc.vector.tensor_tensor(logit[:, :, :], pick[:, :, :], per_tile(small[:, 0, :]), ALU.subtract)\
                    .then_inc(shifted.sem, 1)
                dve.wait_ge(shifted.sem, shifted.at(b, 1))
                link(nc.vector.scalar_tensor_tensor(out=pick[:, :, :], in0=logit[:, :, :], scalar=0.0,
                                                    in1=per_expert(order[:, :]), op0=ALU.is_ge, op1=ALU.mult))
                link(nc.vector.tensor_reduce(small[:, 1, :], pick[:, :, :], AX.X, ALU.max))
                nc.vector.tensor_tensor(onehot[:, :, :], pick[:, :, :], per_tile(small[:, 1, :]), ALU.is_equal)\
                    .then_inc(onehot_ready.sem, 1)
                for i in range(2, 2 if last else 4):
                    low(b, 0, i)
                dve.wait_ge(exp_route.sem, exp_route.at(b, 1))
                link(nc.vector.tensor_reduce(small[:, 2, :], expo[:, :, :], AX.X, ALU.add))
                link(nc.vector.reciprocal(rows[:, :, W_COL], small[:, 2, :]))
                dve.wait_ge(ranks_done.sem, ranks_done.at(b, 1))
                nc.vector.tensor_copy(base[:, 0, :], region_end[:, :]).then_inc(route_step.sem, 1)
                step += 1
                for tb in range(ROWT):
                    dve.wait_ge(route_step.sem, route_step.at(b, step))
                    after = base[:, tb + 1, :] if tb + 1 < ROWT else region_end[:, :]
                    nc.vector.tensor_tensor(after, total_ps[:, tb, :], base[:, tb, :], ALU.add)\
                        .then_inc(route_step.sem, 1)
                    step += 1
                dve.wait_ge(route_step.sem, route_step.at(b, step))
                link(nc.vector.tensor_tensor(base[:, :, :], rank_ps, base[:, :, :], ALU.add))
                link(nc.vector.tensor_tensor(base[:, :, :], base[:, :, :], onehot[:, :, :], ALU.mult))
                link(nc.vector.tensor_reduce(small[:, 3, :], base[:, :, :], AX.X, ALU.add))
                nc.vector.tensor_copy(dest[:, :], small[:, 3, :]).then_inc(dest_ready.sem, 1)
                assert step == ROUTE_STEPS, step

            with dve.Fori(0, BATCHES - 1) as b:
                one_pass(b, False)
            one_pass(BATCHES - 1, True)

        @block.tensor
        def _(pe):
            def begin(b, name):
                bank, n = place_of(b, name)
                if b is not None:
                    pe.wait_ge(proj_free[bank].sem, proj_free[bank].at(b, n))
                elif n:
                    pe.wait_ge(proj_free[bank].sem, proj_free[bank].early(n))
                return proj[bank], proj_full[bank].sem

            ALL = range(3 * KT)
            third = lambda piece: range(KT * piece, KT * (piece + 1))

            def project(b, u, i, cs):
                o, t = divmod(i, HALVES)
                bank, _ = place_of(b, ("p", u, i))
                if 0 in cs:
                    begin(b, ("p", u, i))
                    if t == 0:
                        turn = tile_turn(b, u)
                        pe.wait_ge(w_in[o].sem, w_in[o].early(16) if b is None else w_in[o].at(b, 16 * turn))
                for c in cs:
                    k, (ws, xs) = c // 3, MM3[c % 3]
                    mm = nc.tensor.matmul(proj[bank][:, :], w_qk[:, o, ws, k, :], xt[:, xs, k, t * BANK:(t + 1) * BANK],
                                          start=c == 0, stop=c == 3 * KT - 1)
                if ALL[-1] in cs:
                    mm.then_inc(proj_full[bank].sem, 1)

            def values(b, tb, cs=ALL):
                bank, _ = place_of(b, ("v", tb))
                if 0 in cs:
                    begin(b, ("v", tb))
                wv = q_st[WV_SET][:, :, :].rearrange("p (c k) (l n) -> p c (k l) n", c=2, n=D)
                for c in cs:
                    k, (xs, ws) = c // 3, MM3[c % 3]
                    mm = nc.tensor.matmul(proj[bank][:, :], xt[:, xs, k, tb * P:(tb + 1) * P], wv[:, ws, k, :],
                                          start=c == 0, stop=c == 3 * KT - 1)
                if ALL[-1] in cs:
                    mm.then_inc(proj_full[bank].sem, 1)

            for name in AHEAD_JOBS:
                if name == ("v", 0):
                    pe.wait_ge(setup_dma, 48)
                if name[0] == "p":
                    project(None, 0, name[2], ALL)
                else:
                    values(None, name[1])
            pe.wait_ge(setup_done, 1)

            def one_pass(b, last):
                def stacks_ready(turns):
                    for s in range(2):
                        stacked(pe, b, s, 2 * turns)

                def max_tile(u, i):
                    qb, heads, j, cols, diag = MAX_TILES[i]
                    n = MTILES * u + i
                    bank = max_bank(u, i)
                    free = max_free[n % 2]
                    pe.wait_ge(free.sem, free.at(b, n // 2 if u else max(n // 2 - 1, 0)))
                    if n == 2:
                        pe.wait_ge(exp_done.sem, exp_done.at(b, 0))
                    for place, h in enumerate(heads):
                        to = min(place * cols + max(cols, 256), BANK)
                        mm = nc.tensor.matmul(bank[:, place * cols:to], q_st[u % SETS][0:3 * DH, h, qb * P:(qb + 1) * P],
                                              k_st[u % SETS][0:3 * DH, h, j * BANK:j * BANK + to - place * cols],
                                              start=True, stop=True, skip_group_check=True)
                    if diag is not None:
                        for place in range(len(heads)):
                            mm = nc.tensor.matmul(bank[:, place * cols + diag:place * cols + diag + P], ident_b[:, :], mask_qk[:, :],
                                                  start=False, stop=True, skip_group_check=True)
                    mm.then_inc(max_full.sem, 1)

                def score_tile(u, j, h):
                    t, kb = SCORE_GROUPS[j]
                    i = STILES * u + 4 * j + h
                    c = column(kb, t)
                    c0 = min(c, BANK - 256)
                    pe.wait_ge(exp_done.sem, exp_done.at(b, max(i - 1, 0)))
                    mm = nc.tensor.matmul(score[h % 2][:, c0:BANK], k_st[u % SETS][0:3 * DH + 1, h, kb * P:(kb + 1) * P],
                                          q_st[u % SETS][0:3 * DH + 1, h, t * BANK + c0:(t + 1) * BANK],
                                          start=True, stop=True)
                    if kb * P >= t * BANK:
                        mm = nc.tensor.matmul(score[h % 2][:, c:c + P], ident_b[:, :], mask_kq[:, :],
                                              start=False, stop=True, skip_group_check=True)
                    mm.then_inc(score_full.sem, 1)

                def weigh(u, j, sums_too):
                    t, kb = SCORE_GROUPS[j]
                    n = GROUPS * u + j
                    last = kb == (t + 1) * BANK // P - 1
                    c = column(kb, t)
                    half = HALVES * u + t
                    if not sums_too:
                        pe.wait_ge(exp_done.sem, exp_done.at(b, 4 * (n + 1)))
                    if kb == 0:
                        free = sums_copied if sums_too else y_copied
                        pe.wait_ge(free.sem, free.at(b, half))
                    for h in range(4):
                        head = 4 * u + h
                        mm = nc.tensor.matmul((den_ps if sums_too else y_ps)[DH * h:DH * (h + 1), c:BANK],
                                              ones_f[:, :] if sums_too else v[:, kb, head * DH:(head + 1) * DH],
                                              probs[:, 4 * (n % 2) + h, c:BANK], start=kb == 0, stop=last,
                                              tile_position=(0, DH * h), skip_group_check=True)
                    if sums_too:
                        mm.then_inc(probs_used.sem, 1)

                def transpose_max(u):
                    pe.wait_ge(max_step.sem, max_step.at(b, u + 1))
                    pe.wait_ge(max_ready.sem, max_ready.at(b, u + 1))
                    bank, full = begin(b, ("m", u))
                    nc.tensor.transpose(bank[0:4 * ROWT, 0:P], row_max[:, :], ident[:, :]).then_inc(full, 1)

                wo = q_st[WO_SET][:, :, :].rearrange("p (c k) (l n) -> p c (k l) n", c=2, n=D)

                def output(tb):
                    bank, full = begin(b, ("o", tb))
                    pe.wait_ge(y_low.sem, y_low.at(b, tb + 1))
                    for c in range(3 * UNITS):
                        g, (ys, ws) = c // 3, MM3[c % 3]
                        mm = nc.tensor.matmul(bank[:, :], parts[:, tb % 2, ys, g * P:(g + 1) * P], wo[:, ws, g, :],
                                              start=c == 0, stop=c == 3 * UNITS - 1)
                    mm.then_inc(full, 1)

                def turn(tb):
                    pe.wait_ge(normed.sem, normed.at(b, tb + 1))
                    bank, full = begin(b, ("x", tb))
                    for k in range(KT):
                        mm = nc.tensor.transpose(bank[:, k * P:(k + 1) * P], rows[:, tb, k * P:(k + 1) * P], ident[:, :])
                    mm.then_inc(full, 1)

                def logits(tb):
                    wait_job(pe, b, proj_free, ("x", tb))
                    if tb == 0:
                        pe.wait_ge(y_copied.sem, y_copied.at(b, UNITS * HALVES))
                        pe.wait_ge(sums_copied.sem, sums_copied.at(b, UNITS * HALVES))
                    for k in range(KT):
                        mm = nc.tensor.matmul(logit_ps[:, tb, :], probs[:, tb, k * P:(k + 1) * P], rw[:, k, :],
                                              start=k == 0, stop=k == KT - 1, skip_group_check=True)
                    mm.then_inc(logits_done.sem, 1)

                for j, name in enumerate(OPENING):
                    beside = opening_maxima(j)
                    if j == 1:
                        stacks_ready(0)
                    for c in ALL:
                        if name[0] == "p":
                            project(b, 1, name[2], range(c, c + 1))
                        else:
                            values(b, name[1], range(c, c + 1))
                        for i in beside[len(beside) * c // len(ALL):len(beside) * (c + 1) // len(ALL)]:
                            max_tile(0, i)
                transpose_max(0)
                values(b, ROWT - 1)
                for u in range(UNITS):
                    for j in range(GROUPS):
                        made = list(pieces(j)) if u + 2 < UNITS else []
                        maxed = maxima(u, j)
                        if maxed and maxed[0] == 0:
                            stacks_ready(u + 1)
                        if j == 0:
                            pe.wait_ge(neg_in.sem, neg_in.at(b, 16 * (u + 1)))
                        work = [(lambda p=p: project(b, u + 2, p // 3, third(p % 3)), 4) for p in made]
                        tile = [(lambda h=h: score_tile(u, j, h), 1) for h in range(4)]
                        if j:
                            sums, products = [[(lambda sums_too=s: weigh(u, j - 1, sums_too), 4)] for s in (True, False)]
                        else:
                            sums, products = [], []
                        work = work[0:1] + tile[0:2] + products + tile[2:3] + work[1:2] + tile[3:4] + sums
                        total, passed, laid = sum(w for _, w in work), 0, 0
                        for do, share in work:
                            do()
                            passed += share
                            upto = len(maxed) * passed // total
                            for i in maxed[laid:upto]:
                                max_tile(u + 1, i)
                            laid = upto
                        if u == 0 and j == 0:
                            wait_job(pe, b, proj_free, ("v", ROWT - 2))
                            wait_job(pe, b, proj_free, ("v", ROWT - 1))
                            pe.wait_ge(dest_ready.sem, dest_ready.at(b, 0))
                        if u == UNITS - 1 and j in O_GROUP:
                            if j == min(O_GROUP):
                                pe.wait_ge(wo_in.sem, wo_in.at(b, 16))
                            output(O_GROUP[j])
                        if u + 1 < UNITS and j == MAX_GROUPS[u > 0][1]:
                            transpose_max(u + 1)
                    weigh(u, GROUPS - 1, False)
                    weigh(u, GROUPS - 1, True)

                if not last:
                    pe.wait_ge(wv_in.sem, wv_in.at(b, 16))
                    pe.wait_ge(xt_low.sem, xt_low.at(b, KT))
                closing = LAST_CLOSING if last else CLOSING
                for before, name in zip([("m", 0)] + closing, closing):
                    if name[0] == "o":
                        output(name[1])
                    elif name[0] == "v":
                        values(b, name[1])
                    elif name[0] == "p":
                        project(b, 0, name[2], ALL)
                    else:
                        turn(name[1])
                    if before[0] == "x":
                        logits(before[1])
                if last:
                    logits(ROWT - 1)
                pe.wait_ge(onehot_ready.sem, onehot_ready.at(b, 1))
                hot = onehot[:, :, :].rearrange("p t e -> p (t e)")
                nc.tensor.matmul(rank_ps.rearrange("p t e -> p (t e)"), before_b[:, :], hot, start=True, stop=True,
                                 skip_group_check=True)
                nc.tensor.matmul(total_ps.rearrange("p t e -> p (t e)"), ones_b[:, :], hot, start=False, stop=True,
                                 skip_group_check=True).then_inc(ranks_done.sem, 1)

            with pe.Fori(0, BATCHES - 1) as b:
                one_pass(b, False)
            one_pass(BATCHES - 1, True)

def run_experts(nc, region_end, expert_w_t, expert_b, dispatched, unread, out):
    RING = 4
    RAWS = 3
    AHEAD = RING - 1
    STEPS = -(-TILES // RING) * RING
    TABLE = STEPS + AHEAD
    with ExitStack() as ctx:
        def sb(name, shape, dt=F32):
            return ctx.enter_context(nc.sbuf_tensor(name, shape, dt))

        def sem(name):
            return ctx.enter_context(nc.semaphore(name))

        starting = []

        def signal(name, per=RING, before=0, first=RING, dma=False):
            starting.append(Signal(ctx, nc, name, per, 16 if dma else first, before))
            return starting[-1]

        weight = sb("weight", [P, 2, EXPERTS * KT * D], F32R)
        w_raw = sb("w_raw", [P, RAWS, KT * D])
        bias = sb("bias", [P, EXPERTS * D], F32R)
        pick_bias = sb("pick_bias", [P, P], F32R)
        got = sb("got", [P, RING, ROW])
        xt = sb("xt_tile", [P, 2, 2, D], F32R)
        y = sb("y", [P, RING, D])
        bias_raw = y[0:2, :, :].rearrange("p s n -> p (s n)")
        minus_row = sb("minus_row", [2, 1])
        ident = sb("ident2", [P, P])
        pad = sb("pad", [P, ROW])
        stats = sb("stats2", [P, RING, 6])
        mv = sb("mv2", [P, RING, 2])
        var_eps = sb("var_eps2", [P, RING])
        half_neg = sb("half_neg2", [P, 1])
        rstd = sb("rstd2", [P, RING])
        shift = sb("shift2", [P, RING])
        home = sb("home", [P, RING], U32)
        lane = sb("lane", [P, EXPERTS])
        first = sb("first", [P, EXPERTS])
        tile_rows = sb("tile_rows", [P, TOKENS // P])
        tile_no = sb("tile_no", [P, TABLE])
        count = sb("count", [P, EXPERTS])
        tiles = sb("tiles", [P, EXPERTS])
        more = sb("more", [P, EXPERTS, TOKENS // P])
        end = sb("end", [P, EXPERTS])
        passed = sb("passed", [P, TABLE, EXPERTS])
        scaled = sb("scaled", [P, TABLE, EXPERTS])
        expert_f = sb("expert_f", [P, TABLE])
        start_f = sb("start_f", [P, TABLE])
        work = sb("work", [P, 2, TABLE])
        expert = sb("expert", [P, TABLE], I32)
        start = sb("start", [P, TABLE], I32)
        tail = sb("tail", [P, EXPERTS])
        tail_row = sb("tail_row", [P, EXPERTS], U32)
        xt_ps = [ctx.enter_context(nc.psum_tensor(f"xt_ps{i}", [P, BANK], F32)) for i in range(2)]
        y_ps = [ctx.enter_context(nc.psum_tensor(f"ye_ps{i}", [P, BANK], F32)) for i in range(RING)]

        raw_in = [sem(f"ew_in{i}") for i in range(RAWS)]
        high_done = sem("ew_high")
        low_done = sem("ew_low")
        bias_in = sem("bias_in")
        bias_high = sem("bias_high")
        bias_low = sem("bias_low")
        plan_consts = sem("plan_consts")
        consts = sem("consts")
        pool_step = sem("pool_step")
        plan_step = sem("plan_step")
        tail_ready = sem("tail_ready")
        table_ready = sem("table_ready")
        padded = sem("padded")
        held_sp, held_pool, held_dve = sem("held_sp2"), sem("held_pool2"), sem("held_dve2")
        got_in = [signal(f"got_in{i}", 16, 16 * (i < AHEAD), dma=True) for i in range(RING)]
        turned = signal("turned", before=1)
        xt_high = signal("xe_high", before=1)
        xt_low = signal("xe_low", before=1)
        y_full = signal("ye_full")
        summed = signal("summed")
        row_step = signal("row_step", 2 * RING)
        stats_ready = signal("stats_ready2")
        norm_step = signal("norm_step2", 3 * RING)
        normed = signal("normed2")
        sent = [Signal(ctx, nc, f"sent{i}", 16, 16) for i in range(RING)]
        block = ctx.enter_context(nc.Block())

        @block.sync
        def _(sp):
            for s in starting:
                sp.sem_inc(s.sem, s.first)
            def load(at, slot):
                hold(sp, held_sp)
                row = sp.value_load(start[0:1, at], min_val=0, max_val=SPARE)
                sp.dma_start(got[:, slot, :], dispatched[bass.ds(row, P), :]).then_inc(got_in[slot].sem, 16)

            for e in range(EXPERTS):
                if e == RAWS:
                    sp.wait_ge(table_ready, 2)
                    sp.wait_ge(padded, EXPERTS * 16)
                    for t in range(AHEAD):
                        load(slice(t, t + 1), t)
                if e >= RAWS:
                    sp.wait_ge(high_done, e - RAWS + 1)
                    sp.wait_ge(low_done, e - RAWS + 1)
                sp.dma_start(w_raw[:, e % RAWS, :].rearrange("p (k n) -> p k n", k=KT),
                             expert_w_t[e].rearrange("(k p) n -> p k n", p=P)).then_inc(raw_in[e % RAWS], 16)
                if e in (1, 2):
                    if e == 2:
                        sp.wait_ge(bias_low, 1)
                    half = slice((e - 1) * RING * D, e * RING * D)
                    sp.dma_start(bias_raw, expert_b.rearrange("e n -> (e n)")[half].partition_broadcast(2))\
                        .then_inc(bias_in, 16)

            with sp.Fori(0, STEPS // RING) as i:
                for s in range(RING):
                    sp.wait_ge(summed.sem, summed.at(i, s))
                    load(bass.ds(i * RING + s + AHEAD, 1), (s + AHEAD) % RING)
            for s in range(RING):
                sp.wait_ge(got_in[s].sem, got_in[s].at(STEPS // RING, 0))

        @block.gpsimd
        def _(pool):
            step = 0

            def link(ins):
                nonlocal step
                step += 1
                ins.then_inc(pool_step, 1)
                pool.wait_ge(pool_step, step)

            loose = dict(allow_small_or_imprecise_dtypes=True)
            link(nc.gpsimd.iota(lane[:, :], [[0, EXPERTS]], base=0, channel_multiplier=1, **loose))
            link(nc.gpsimd.iota(first[:, :], [[REGION, EXPERTS]], base=0, channel_multiplier=0, **loose))
            link(nc.gpsimd.iota(tile_rows[:, :], [[P, TOKENS // P]], base=0, channel_multiplier=0, **loose))
            nc.gpsimd.iota(tile_no[:, :], [[1, TABLE]], base=0, channel_multiplier=0, **loose).then_inc(plan_consts, 1)
            link(nc.gpsimd.memset(pad[:, 0:ID_COL], 0.0))
            link(nc.gpsimd.memset(pad[:, ID_COL:ROW], float(NO_TOKEN)))
            pool.wait_ge(tail_ready, 1)
            for e in range(EXPERTS):
                nc.gpsimd.indirect_dma_start(
                    out=dispatched, out_offset=bass.IndirectOffsetOnAxis(ap=tail_row[:, e:e + 1], axis=0),
                    in_=pad[:, :], in_offset=None).then_inc(padded, 16)
            link(nc.gpsimd.memset(ident[:, :], 0.0))
            link(nc.gpsimd.affine_select(out=ident[:, :], in_=ident[:, :], compare_op=ALU.not_equal, fill=1.0,
                                         base=0, pattern=[[-1, P]], channel_multiplier=1))
            link(nc.gpsimd.memset(half_neg[:, :], -0.5))
            link(nc.gpsimd.memset(pick_bias[:, :].bitcast(F32), 0.0))
            link(nc.gpsimd.memset(pick_bias[0:2, :].bitcast(F32), 1.0))
            link(nc.gpsimd.iota(minus_row[:, :], [[0, 1]], base=0, channel_multiplier=-1, **loose))
            nc.gpsimd.memset(bias[:, :].bitcast(F32), 0.0).then_inc(consts, 1)
            for s in range(RING):
                nc.gpsimd.dma_start(unread[s * P:(s + 1) * P, :], pad[:, :]).then_inc(sent[s].sem, 16)
            with pool.Fori(0, STEPS // RING) as i:
                def send(s):
                    pool.wait_ge(normed.sem, normed.at(i, s + 1))
                    hold(pool, held_pool)
                    nc.gpsimd.indirect_dma_start(
                        out=out, out_offset=bass.IndirectOffsetOnAxis(ap=home[:, s:s + 1], axis=0),
                        in_=y[:, s, :], in_offset=None, bounds_check=TOKENS - 1, oob_is_err=False)\
                        .then_inc(sent[s].sem, 16)

                for s in range(RING):
                    one = slice(s, s + 1)
                    pool.wait_ge(stats_ready.sem, stats_ready.at(i, s + 1))
                    hold(pool, held_pool)
                    nc.gpsimd.tensor_scalar(var_eps[:, one], mv[:, s, 1:2], EPS, None, ALU.add)\
                        .then_inc(norm_step.sem, 1)
                    pool.wait_ge(norm_step.sem, norm_step.at(i, 3 * s + 1))
                    nc.gpsimd.tensor_tensor(rstd[:, one], var_eps[:, one], half_neg[:, :], ALU.pow)\
                        .then_inc(norm_step.sem, 1)
                    pool.wait_ge(norm_step.sem, norm_step.at(i, 3 * s + 2))
                    hold(pool, held_pool)
                    nc.gpsimd.tensor_scalar(shift[:, one], mv[:, s, 0:1], rstd[:, one], -1.0, ALU.mult, ALU.mult)\
                        .then_inc(norm_step.sem, 1)
                    send(s)
            for s in range(RING):
                pool.wait_ge(sent[s].sem, sent[s].at(STEPS // RING, 0))

        @block.scalar
        def _(act):
            def high(slot):
                nc.scalar.activation(xt[:, slot, HI, :], xt_ps[slot][:, :], ACT.Copy).then_inc(xt_high.sem, 1)

            for e in range(EXPERTS):
                if e == EXPERTS - 2:
                    act.wait_ge(turned.sem, turned.early(1))
                    high(0)
                act.wait_ge(raw_in[e % RAWS], 16 * (e // RAWS + 1))
                nc.scalar.activation(weight[:, HI, e * KT * D:(e + 1) * KT * D], w_raw[:, e % RAWS, :], ACT.Copy)\
                    .then_inc(high_done, 1)
                if e in (1, 2):
                    act.wait_ge(bias_in, 16 * e)
                    act.wait_ge(consts, 1)
                    nc.scalar.activation(bias[0:2, (e - 1) * RING * D:e * RING * D], bias_raw, ACT.Copy)\
                        .then_inc(bias_high, 1)

            act.wait_ge(turned.sem, turned.at(0, 1))
            high(1)
            with act.Fori(0, STEPS // RING) as i:
                def norm(s):
                    act.wait_ge(norm_step.sem, norm_step.at(i, 3 * s + 3))
                    nc.scalar.activation(y[:, s, :], y[:, s, :], ACT.Identity, bias=shift[:, s:s + 1],
                                         scale=rstd[:, s:s + 1]).then_inc(normed.sem, 1)

                for s in range(RING):
                    act.wait_ge(turned.sem, turned.at(i, s + 2))
                    act.wait_ge(y_full.sem, y_full.at(i, s + 1))
                    high(s % 2)
                    norm(s)

        @block.vector
        def _(dve):
            step = 0

            def link(ins):
                nonlocal step
                step += 1
                ins.then_inc(plan_step, 1)
                dve.wait_ge(plan_step, step)

            dve.wait_ge(plan_consts, 1)
            link(nc.vector.tensor_tensor(tail[:, :], region_end[:, :], lane[:, :], ALU.add))
            nc.vector.tensor_copy(tail_row[:, :], tail[:, :]).then_inc(tail_ready, 1)
            link(nc.vector.tensor_tensor(count[:, :], region_end[:, :], first[:, :], ALU.subtract))
            wide = [P, EXPERTS, TOKENS // P]
            link(nc.vector.tensor_tensor(more[:, :, :], count[:, :].unsqueeze(2).to_broadcast(wide),
                                         tile_rows[:, :].unsqueeze(1).to_broadcast(wide), ALU.is_gt))
            link(nc.vector.tensor_reduce(tiles[:, :], more[:, :, :], AX.X, ALU.add))
            link(nc.vector.tensor_copy(end[:, 0:1], tiles[:, 0:1]))
            for e in range(1, EXPERTS):
                link(nc.vector.tensor_tensor(end[:, e:e + 1], end[:, e - 1:e], tiles[:, e:e + 1], ALU.add))
            wide = [P, TABLE, EXPERTS]
            per_expert = lambda a: a.unsqueeze(1).to_broadcast(wide)
            link(nc.vector.tensor_tensor(passed[:, :, :], tile_no[:, :].unsqueeze(2).to_broadcast(wide),
                                         per_expert(end[:, :]), ALU.is_ge))
            link(nc.vector.tensor_reduce(expert_f[:, :], passed[:, :, :], AX.X, ALU.add))
            link(nc.vector.tensor_tensor(scaled[:, :, :], passed[:, :, :], per_expert(tiles[:, :]), ALU.mult))
            link(nc.vector.tensor_reduce(work[:, 0, :], scaled[:, :, :], AX.X, ALU.add))
            link(nc.vector.tensor_tensor(work[:, 1, :], tile_no[:, :], work[:, 0, :], ALU.subtract))
            link(nc.vector.tensor_scalar(work[:, 1, :], work[:, 1, :], float(P), None, ALU.mult))
            link(nc.vector.scalar_tensor_tensor(out=start_f[:, :], in0=expert_f[:, :], scalar=float(REGION),
                                                in1=work[:, 1, :], op0=ALU.mult, op1=ALU.add))
            link(nc.vector.tensor_scalar(start_f[:, :], start_f[:, :], float(SPARE), None, ALU.min))
            link(nc.vector.tensor_scalar(expert_f[:, :], expert_f[:, :], float(EXPERTS - 1), None, ALU.min))
            nc.vector.tensor_copy(start[:, :], start_f[:, :]).then_inc(table_ready, 1)
            nc.vector.tensor_copy(expert[:, :], expert_f[:, :]).then_inc(table_ready, 1)
            def low(slot):
                nc.vector.tensor_tensor(xt[:, slot, LO, :], xt_ps[slot][:, :], xt[:, slot, HI, :].bitcast(F32),
                                        ALU.subtract).then_inc(xt_low.sem, 1)

            for e in range(EXPERTS):
                if e == EXPERTS - 2:
                    dve.wait_ge(xt_high.sem, xt_high.early(1))
                    low(0)
                dve.wait_ge(high_done, e + 1)
                nc.vector.tensor_tensor(weight[:, LO, e * KT * D:(e + 1) * KT * D], w_raw[:, e % RAWS, :],
                                        weight[:, HI, e * KT * D:(e + 1) * KT * D].bitcast(F32), ALU.subtract)\
                    .then_inc(low_done, 1)
                if e in (1, 2):
                    half = bias[0:2, (e - 1) * RING * D:e * RING * D]
                    dve.wait_ge(bias_high, e)
                    nc.vector.scalar_tensor_tensor(out=half, in0=half.bitcast(F32), scalar=minus_row[:, :],
                                                   in1=bias_raw, op0=ALU.mult, op1=ALU.add).then_inc(bias_low, 1)

            with dve.Fori(0, STEPS // RING) as i:
                for s in range(RING):
                    dve.wait_ge(xt_high.sem, xt_high.at(i, s + 1))
                    low((s + 1) % 2)
                    dve.wait_ge(sent[s].sem, sent[s].at(i, 0))
                    dve.wait_ge(got_in[s].sem, got_in[s].at(i, 16 * (s == AHEAD)))
                    nc.vector.tensor_copy(home[:, s:s + 1], got[:, s, ID_COL:ROW]).then_inc(row_step.sem, 1)
                    dve.wait_ge(y_full.sem, y_full.at(i, s + 1))
                    nc.vector.scalar_tensor_tensor(out=y[:, s, :], in0=y_ps[s][:, :], scalar=got[:, s, W_COL:W_COL + 1],
                                                   in1=got[:, s, 0:D], op0=ALU.mult, op1=ALU.add).then_inc(summed.sem, 1)
                    dve.wait_ge(summed.sem, summed.at(i, s + 1))
                    nc.vector.bn_stats(stats[:, s, :], y[:, s, :]).then_inc(row_step.sem, 1)
                    dve.wait_ge(row_step.sem, row_step.at(i, 2 * s + 2))
                    hold(dve, held_dve)
                    nc.vector.bn_aggr(mv[:, s, :], stats[:, s, :]).then_inc(stats_ready.sem, 1)

        @block.tensor
        def _(pe):
            def turn(slot, bank):
                for k in range(KT):
                    mm = nc.tensor.transpose(xt_ps[bank][:, k * P:(k + 1) * P], got[:, slot, k * P:(k + 1) * P],
                                             ident[:, :])
                mm.then_inc(turned.sem, 1)

            pe.wait_ge(consts, 1)
            pe.wait_ge(table_ready, 2)
            pe.wait_ge(got_in[0].sem, got_in[0].early(16))
            turn(0, 0)
            pe.wait_ge(bias_low, 2)
            with pe.Fori(0, STEPS // RING) as i:
                for s in range(RING):
                    nxt = (s + 1) % RING
                    pe.wait_ge(got_in[nxt].sem, got_in[nxt].at(i, 16 * (nxt in (0, AHEAD))))
                    pe.wait_ge(xt_low.sem, xt_low.at(i, s - 1))
                    turn(nxt, (s + 1) % 2)
                    e = pe.value_load(expert[0:1, bass.ds(i * RING + s, 1)], min_val=0, max_val=EXPERTS - 1)
                    pe.wait_ge(low_done, e + 1)
                    pe.wait_ge(xt_low.sem, xt_low.at(i, s))
                    pe.wait_ge(summed.sem, summed.at(i, s - AHEAD))
                    nc.tensor.matmul(y_ps[s][:, :], pick_bias[:, :], bias[:, bass.ds(e * D, D)], start=True, stop=False)
                    for c in range(3 * KT):
                        k, (xs, ws) = c // 3, MM3[c % 3]
                        mm = nc.tensor.matmul(y_ps[s][:, :], xt[:, s % 2, xs, k * P:(k + 1) * P],
                                              weight[:, ws, bass.ds(e * (KT * D) + k * D, D)],
                                              start=False, stop=c == 3 * KT - 1)
                    mm.then_inc(y_full.sem, 1)
            pe.wait_ge(got_in[1].sem, got_in[1].at(STEPS // RING, 0))
            pe.wait_ge(xt_low.sem, xt_low.at(STEPS // RING, -1))
            turn(1, 1)


def run(nc, x_t, x_rows, wq_t, wk_t, wv_t, wo_t, router_w_t, router_b, expert_w_t, expert_b, out=None):
    w_qk_parts = nc.dram_tensor("w_qk_parts", [UNITS, 2, P, 2 * KT * P], F32).ap()
    w_vo_parts = nc.dram_tensor("w_vo_parts", [2, P, 2 * KT * D], F32).ap()
    dispatched = nc.dram_tensor("dispatched", [SPARE + P, ROW], F32).ap()
    unread = nc.dram_tensor("unread", [4 * P, ROW], F32).ap()
    with ExitStack() as ctx:
        region_end = ctx.enter_context(nc.sbuf_tensor("region_end", [P, EXPERTS], F32))
        with ExitStack() as attention:
            xt = attention.enter_context(nc.sbuf_tensor("xt", [P, 2, KT, SEQ], F32R))
            xt_raw = attention.enter_context(nc.sbuf_tensor("xt_raw", [P, 2, SEQ], F32))
            split_weights(nc, xt, xt_raw, x_t, w_qk_parts, w_vo_parts, wq_t, wk_t, wv_t, wo_t)
            attend(nc, region_end, xt, xt_raw, x_t, x_rows, router_w_t, router_b, w_qk_parts, w_vo_parts, dispatched)
        if out is not None:
            run_experts(nc, region_end, expert_w_t, expert_b, dispatched, unread, out)


def kernel(**inputs):
    import numpy as np
    import concourse.bacc as bacc
    from concourse.bass_utils import run_bass_kernel_spmd

    x = np.asarray(inputs["L0_attn_x"])
    rows = x.reshape(TOKENS, D)
    laid_out = {
        "x_t": rows.T,
        "x_rows": rows,
        "wq_t": np.asarray(inputs["L0_attn_W_Q"]).T,
        "wk_t": np.asarray(inputs["L0_attn_W_K"]).T,
        "wv_t": np.asarray(inputs["L0_attn_W_V"]).T,
        "wo_t": np.asarray(inputs["L0_attn_W_O"]).T,
        "router_w_t": np.asarray(inputs["L0_ffn_router_w"]).T,
        "router_b": np.asarray(inputs["L0_ffn_router_b"]),
        "expert_w_t": np.asarray(inputs["L0_ffn_expert_w"]).transpose(0, 2, 1),
        "expert_b": np.asarray(inputs["L0_ffn_expert_b"]),
    }
    laid_out = {name: np.ascontiguousarray(a) for name, a in laid_out.items()}
    nc = bacc.Bacc("TRN2", target_bir_lowering=False, num_devices=1)
    aps = {name: nc.dram_tensor(name, a.shape, mybir.dt.from_np(a.dtype), kind="ExternalInput").ap()
           for name, a in laid_out.items()}
    out = nc.dram_tensor("out", [TOKENS, D], F32, kind="ExternalOutput").ap()
    run(nc, out=out, **aps)
    result = run_bass_kernel_spmd(nc, [laid_out], core_ids=[0])
    return result.results[0]["out"].reshape(BATCHES, SEQ, D)
```
